# Optimizing a Trainium2 kernel written in Bass

```python
import numpy as np
import jax
import jax.numpy as jnp

def _softmax(x, axis=-1):
    return jax.nn.softmax(x, axis=axis)

def _gelu(x):
    return jax.nn.gelu(x, approximate=True)

def _silu(x):
    return jax.nn.silu(x)

def _sigmoid(x):
    return jax.nn.sigmoid(x)

def _layernorm(x, axis=-1, eps=1e-05):
    m = jnp.mean(x, axis=axis, keepdims=True)
    v = jnp.var(x, axis=axis, keepdims=True)
    return (x - m) / jnp.sqrt(v + eps)

def _scatter_add(tgt, idx, src, axis=0):
    return tgt.at[idx].add(src)

def _segment_sum(src, seg, n):
    return jax.ops.segment_sum(src, seg, n)
kernel_name = 'mk_lm_tower_d2_tok_ids1024_r4_2edc29'

def setup_inputs(seed: int=0):
    np.random.seed(seed)
    _w = jnp.asarray

    def _rec_inputs():
        import jax
        import jax.numpy as jnp
        _rk = jax.random.key(seed)
        x = jax.random.randint(jax.random.fold_in(_rk, 1), (4, 1024), 0, 12564, jnp.int32)
        return x
    x = _rec_inputs()

    def _L0_tok_setup():
        import jax, jax.numpy as jnp
        import numpy as np
        VOCAB, D, R, ALPHA = (50257, 256, 16, 32)
        SCALING = ALPHA / R
        key = jax.random.key(seed)
        k1, k2, k3, k4 = jax.random.split(key, 4)
        x = jax.random.randint(k1, (4, 1024), 0, VOCAB)
        weight = jax.random.normal(k2, (VOCAB, D), dtype=jnp.float32)
        lora_a = jax.random.normal(k3, (VOCAB, R), dtype=jnp.float32)
        lora_b = jax.random.normal(k4, (R, D), dtype=jnp.float32)
        return {'x': x, 'weight': weight, 'lora_a': lora_a, 'lora_b': lora_b}
    _L0_tok_all = _L0_tok_setup()
    _L0_tok_in = {k: v for k, v in _L0_tok_all.items() if k in ('weight', 'lora_a', 'lora_b')}
    del _L0_tok_all

    def _L0_attn_setup():
        import jax, jax.numpy as jnp
        import numpy as np
        D_MODEL = 256
        NUM_HEADS = 16
        HEAD_DIM = D_MODEL // NUM_HEADS
        THETA = 10000.0
        B, S = (2, 512)

        def _apply_rope(t, cos, sin):
            te = t[..., 0::2]
            to = t[..., 1::2]
            re = te * cos - to * sin
            ro = te * sin + to * cos
            out = jnp.stack([re, ro], axis=-1)
            return out.reshape(t.shape)
        key = jax.random.key(seed)
        kx, kq, kk, kv, ko = jax.random.split(key, 5)
        std = 2.0 / (2 * D_MODEL) ** 0.5

        def w(k):
            return jnp.clip(std * jax.random.normal(k, (D_MODEL, D_MODEL), jnp.float32), -3.0 * std, 3.0 * std)
        return {'x': jax.random.normal(kx, (B, S, D_MODEL), jnp.float32), 'Wq': w(kq), 'Wk': w(kk), 'Wv': w(kv), 'Wo': w(ko)}
    _L0_attn_all = _L0_attn_setup()
    _L0_attn_in = {k: v for k, v in _L0_attn_all.items() if k in ('Wq', 'Wk', 'Wv', 'Wo')}
    del _L0_attn_all

    def _L0_ffn_setup():
        import jax, jax.numpy as jnp
        import numpy as np
        N_EMBED = 256
        FFN_HIDDEN = 1024
        NUM_EXPERTS = 8
        TOP_K = 2
        key = jax.random.key(seed)
        ks = jax.random.split(key, 8)
        d, f, E = (N_EMBED, FFN_HIDDEN, NUM_EXPERTS)
        s_d = 1.0 / np.sqrt(d)
        s_f = 1.0 / np.sqrt(f)
        return {'x': jax.random.normal(ks[0], (2, 512, d), dtype=jnp.float32), 'Wg': jax.random.uniform(ks[1], (d, E), jnp.float32, -s_d, s_d), 'bg': jax.random.uniform(ks[2], (E,), jnp.float32, -s_d, s_d), 'W1': jax.random.uniform(ks[3], (E, d, f), jnp.float32, -s_d, s_d), 'b1': jax.random.uniform(ks[4], (E, f), jnp.float32, -s_d, s_d), 'W2': jax.random.uniform(ks[5], (E, f, d), jnp.float32, -s_f, s_f), 'b2': jax.random.uniform(ks[6], (E, d), jnp.float32, -s_f, s_f)}
    _L0_ffn_all = _L0_ffn_setup()
    _L0_ffn_in = {k: v for k, v in _L0_ffn_all.items() if k in ('Wg', 'bg', 'W1', 'b1', 'W2', 'b2')}
    del _L0_ffn_all

    def _L1_attn_setup():
        import jax, jax.numpy as jnp
        import numpy as np
        MODEL_DIM = 256
        HEADS = 16
        HEAD_DIM = MODEL_DIM // HEADS
        B, T = (2, 512)
        TB_LEN = 125
        key = jax.random.key(seed)
        ks = jax.random.split(key, 12)
        s = 0.02
        d = MODEL_DIM
        return {'x': jax.random.normal(ks[0], (B, T, d), dtype=jnp.float32), 'Wq': jax.random.normal(ks[1], (d, d), dtype=jnp.float32) * s, 'bq': jnp.zeros((d,), jnp.float32), 'Wk': jax.random.normal(ks[2], (d, d), dtype=jnp.float32) * s, 'bk': jnp.zeros((d,), jnp.float32), 'Wv': jax.random.normal(ks[3], (d, d), dtype=jnp.float32) * s, 'bv': jnp.zeros((d,), jnp.float32), 'Wo': jax.random.normal(ks[4], (d, d), dtype=jnp.float32) * s, 'bo': jnp.zeros((d,), jnp.float32), 'et_gate': jax.random.normal(ks[5], (1, 1, 1), dtype=jnp.float32), 'is_gate': jax.random.normal(ks[6], (1, 1, 1), dtype=jnp.float32), 'time_bias': jnp.linspace(-1.0, 1.0, TB_LEN, dtype=jnp.float32).reshape(1, 1, TB_LEN)}
    _L1_attn_all = _L1_attn_setup()
    _L1_attn_in = {k: v for k, v in _L1_attn_all.items() if k in ('Wq', 'bq', 'Wk', 'bk', 'Wv', 'bv', 'Wo', 'bo', 'et_gate', 'is_gate', 'time_bias')}
    del _L1_attn_all

    def _L1_ffn_setup():
        import jax, jax.numpy as jnp
        import numpy as np
        B, K, D = (128, 32, 256)
        E = 32
        H = int(D * 0.25)

        def _rsqrt_uniform(key, shape, d):
            bound = d ** (-0.5)
            return jax.random.uniform(key, shape, jnp.float32, -bound, bound)
        key = jax.random.key(seed)
        ks = jax.random.split(key, 7)
        return {'x': jax.random.normal(ks[0], (B, K, D), jnp.float32), 'router_w': _rsqrt_uniform(ks[1], (E, D), D), 'router_b': _rsqrt_uniform(ks[2], (E,), D), 'weights1': _rsqrt_uniform(ks[3], (E, D, H), H), 'bias1': _rsqrt_uniform(ks[4], (E, H), H), 'weights2': _rsqrt_uniform(ks[5], (E, H, D), D), 'bias2': _rsqrt_uniform(ks[6], (E, D), D)}
    _L1_ffn_all = _L1_ffn_setup()
    _L1_ffn_in = {k: v for k, v in _L1_ffn_all.items() if k in ('router_w', 'router_b', 'weights1', 'bias1', 'weights2', 'bias2')}
    del _L1_ffn_all
    return {'x': x, 'L0_tok_weight': _L0_tok_in['weight'], 'L0_tok_lora_a': _L0_tok_in['lora_a'], 'L0_tok_lora_b': _L0_tok_in['lora_b'], 'L0_attn_Wq': _L0_attn_in['Wq'], 'L0_attn_Wk': _L0_attn_in['Wk'], 'L0_attn_Wv': _L0_attn_in['Wv'], 'L0_attn_Wo': _L0_attn_in['Wo'], 'L0_ffn_Wg': _L0_ffn_in['Wg'], 'L0_ffn_bg': _L0_ffn_in['bg'], 'L0_ffn_W1': _L0_ffn_in['W1'], 'L0_ffn_b1': _L0_ffn_in['b1'], 'L0_ffn_W2': _L0_ffn_in['W2'], 'L0_ffn_b2': _L0_ffn_in['b2'], 'L1_attn_Wq': _L1_attn_in['Wq'], 'L1_attn_bq': _L1_attn_in['bq'], 'L1_attn_Wk': _L1_attn_in['Wk'], 'L1_attn_bk': _L1_attn_in['bk'], 'L1_attn_Wv': _L1_attn_in['Wv'], 'L1_attn_bv': _L1_attn_in['bv'], 'L1_attn_Wo': _L1_attn_in['Wo'], 'L1_attn_bo': _L1_attn_in['bo'], 'L1_attn_et_gate': _L1_attn_in['et_gate'], 'L1_attn_is_gate': _L1_attn_in['is_gate'], 'L1_attn_time_bias': _L1_attn_in['time_bias'], 'L1_ffn_router_w': _L1_ffn_in['router_w'], 'L1_ffn_router_b': _L1_ffn_in['router_b'], 'L1_ffn_weights1': _L1_ffn_in['weights1'], 'L1_ffn_bias1': _L1_ffn_in['bias1'], 'L1_ffn_weights2': _L1_ffn_in['weights2'], 'L1_ffn_bias2': _L1_ffn_in['bias2']}

def reference(x, L0_tok_weight, L0_tok_lora_a, L0_tok_lora_b, L0_attn_Wq, L0_attn_Wk, L0_attn_Wv, L0_attn_Wo, L0_ffn_Wg, L0_ffn_bg, L0_ffn_W1, L0_ffn_b1, L0_ffn_W2, L0_ffn_b2, L1_attn_Wq, L1_attn_bq, L1_attn_Wk, L1_attn_bk, L1_attn_Wv, L1_attn_bv, L1_attn_Wo, L1_attn_bo, L1_attn_et_gate, L1_attn_is_gate, L1_attn_time_bias, L1_ffn_router_w, L1_ffn_router_b, L1_ffn_weights1, L1_ffn_bias1, L1_ffn_weights2, L1_ffn_bias2):
    import jax
    import jax.numpy as jnp

    def _L0_tok_ref(x, weight, lora_a, lora_b):
        import jax, jax.numpy as jnp
        import numpy as np
        VOCAB, D, R, ALPHA = (50257, 256, 16, 32)
        SCALING = ALPHA / R
        base = weight[x]
        delta = jnp.einsum('bsr,rd->bsd', lora_a[x], lora_b) * SCALING
        return base + delta

    def _L0_attn_ref(x, Wq, Wk, Wv, Wo):
        import jax, jax.numpy as jnp
        import numpy as np
        D_MODEL = 256
        NUM_HEADS = 16
        HEAD_DIM = D_MODEL // NUM_HEADS
        THETA = 10000.0
        B, S = (2, 512)

        def _apply_rope(t, cos, sin):
            te = t[..., 0::2]
            to = t[..., 1::2]
            re = te * cos - to * sin
            ro = te * sin + to * cos
            out = jnp.stack([re, ro], axis=-1)
            return out.reshape(t.shape)
        Bv, Sv, _ = x.shape

        def proj(W):
            return jnp.einsum('bsd,ed->bse', x, W).reshape(Bv, Sv, NUM_HEADS, HEAD_DIM).transpose(0, 2, 1, 3)
        q, k, v = (proj(Wq), proj(Wk), proj(Wv))
        pos = jnp.arange(Sv, dtype=jnp.float32)
        inv_freq = THETA ** (-jnp.arange(0, HEAD_DIM, 2, dtype=jnp.float32) / HEAD_DIM)
        ang = pos[:, None] * inv_freq[None, :]
        cos, sin = (jnp.cos(ang), jnp.sin(ang))
        q = _apply_rope(q, cos, sin)
        k = _apply_rope(k, cos, sin)
        scale = 1.0 / jnp.sqrt(jnp.float32(HEAD_DIM))
        scores = jnp.einsum('bhqd,bhkd->bhqk', q.astype(jnp.float32), k.astype(jnp.float32)) * scale
        causal = jnp.tril(jnp.ones((Sv, Sv), dtype=bool))
        scores = jnp.where(causal[None, None], scores, -jnp.inf)
        attn = jax.nn.softmax(scores, axis=-1)
        out = jnp.einsum('bhqk,bhkd->bhqd', attn, v.astype(jnp.float32))
        out = out.transpose(0, 2, 1, 3).reshape(Bv, Sv, D_MODEL)
        return jnp.einsum('bsd,ed->bse', out, Wo)

    def _L0_ffn_ref(x, Wg, bg, W1, b1, W2, b2):
        import jax, jax.numpy as jnp
        import numpy as np
        N_EMBED = 256
        FFN_HIDDEN = 1024
        NUM_EXPERTS = 8
        TOP_K = 2
        gate_scores = jax.nn.softmax(x @ Wg + bg, axis=-1)
        topk_scores, topk_idx = jax.lax.top_k(gate_scores, TOP_K)
        topk_scores = topk_scores / (jnp.sum(topk_scores, axis=-1, keepdims=True) + 1e-08)
        onehot = jax.nn.one_hot(topk_idx, NUM_EXPERTS, dtype=x.dtype)
        combine_w = jnp.einsum('bsk,bske->bse', topk_scores, onehot)
        output = jnp.zeros_like(x)
        for e in range(NUM_EXPERTS):
            h = jax.nn.gelu(x @ W1[e] + b1[e])
            y = h @ W2[e] + b2[e]
            output = output + y * combine_w[..., e:e + 1]
        return output

    def _L1_attn_ref(x, Wq, bq, Wk, bk, Wv, bv, Wo, bo, et_gate, is_gate, time_bias):
        import jax, jax.numpy as jnp
        import numpy as np
        MODEL_DIM = 256
        HEADS = 16
        HEAD_DIM = MODEL_DIM // HEADS
        B, T = (2, 512)
        TB_LEN = 125
        Bb, Tt, D = x.shape
        H, hd = (HEADS, HEAD_DIM)
        Q = (x @ Wq.T + bq).reshape(Bb, Tt, H, hd).transpose(0, 2, 1, 3)
        K = (x @ Wk.T + bk).reshape(Bb, Tt, H, hd).transpose(0, 2, 1, 3)
        V = (x @ Wv.T + bv).reshape(Bb, Tt, H, hd).transpose(0, 2, 1, 3)
        scores = jnp.einsum('bhqd,bhkd->bhqk', Q, K) / jnp.sqrt(jnp.float32(hd))
        pos = jnp.arange(Tt)[None, :] - jnp.arange(Tt)[:, None]
        idx = jnp.clip(pos + TB_LEN // 2, 0, TB_LEN - 1)
        tp = time_bias[:, :, idx]
        tp = jnp.squeeze(tp, axis=1)[None, None]
        scores = scores + jax.nn.sigmoid(et_gate) * tp + is_gate
        attn = jax.nn.softmax(scores, axis=-1)
        context = jnp.matmul(attn, V)
        context = context.transpose(0, 2, 1, 3, 4).reshape(Bb, Tt, D)
        return context @ Wo.T + bo

    def _L1_ffn_ref(x, router_w, router_b, weights1, bias1, weights2, bias2):
        import jax, jax.numpy as jnp
        import numpy as np
        B, K, D = (128, 32, 256)
        E = 32
        H = int(D * 0.25)

        def _rsqrt_uniform(key, shape, d):
            bound = d ** (-0.5)
            return jax.random.uniform(key, shape, jnp.float32, -bound, bound)
        b, k, d = x.shape
        x_flat = x.reshape(-1, d)
        n = x_flat.shape[0]
        logits = x_flat @ router_w.T + router_b
        routed_idx = jnp.argmax(logits, axis=-1)

        def expert_mlp(w1, b1, w2, b2):
            h = jax.nn.relu(x_flat @ w1 + b1)
            return jax.nn.relu(h @ w2 + b2)
        y_all = jax.vmap(expert_mlp)(weights1, bias1, weights2, bias2)
        out_flat = y_all[routed_idx, jnp.arange(n)]
        return out_flat.reshape(b, k, d)
    h = _L0_tok_ref(x, L0_tok_weight, L0_tok_lora_a, L0_tok_lora_b)
    h = h + _L0_attn_ref(_layernorm(h, axis=-1), L0_attn_Wq, L0_attn_Wk, L0_attn_Wv, L0_attn_Wo)
    h = h + _L0_ffn_ref(_layernorm(h, axis=-1), L0_ffn_Wg, L0_ffn_bg, L0_ffn_W1, L0_ffn_b1, L0_ffn_W2, L0_ffn_b2)
    h = h + _L1_attn_ref(_layernorm(h, axis=-1), L1_attn_Wq, L1_attn_bq, L1_attn_Wk, L1_attn_bk, L1_attn_Wv, L1_attn_bv, L1_attn_Wo, L1_attn_bo, L1_attn_et_gate, L1_attn_is_gate, L1_attn_time_bias)
    h = h + _L1_ffn_ref(_layernorm(h, axis=-1), L1_ffn_router_w, L1_ffn_router_b, L1_ffn_weights1, L1_ffn_bias1, L1_ffn_weights2, L1_ffn_bias2)
    return h

_drawn_inputs = setup_inputs


def setup_inputs(seed=0):
    import zlib

    import numpy as np

    out = dict(_drawn_inputs(seed))
    spreads = {'L1_attn_bq': (0.0, 0.8),
     'L1_attn_bk': (0.0, 2.0),
     'L1_attn_bv': (0.0, 0.8),
     'L1_attn_bo': (0.0, 0.647)}
    factors = {'L0_ffn_Wg': 3.641,
     'L0_ffn_bg': 8.0,
     'L0_ffn_W1': 3.315,
     'L0_ffn_b1': 8.0,
     'L0_ffn_W2': 3.104,
     'L0_ffn_b2': 8.0,
     'L1_attn_Wq': 8.0,
     'L1_attn_Wk': 8.0,
     'L1_attn_Wv': 8.0,
     'L1_attn_Wo': 8.0,
     'L1_attn_time_bias': 8.0,
     'L1_ffn_router_w': 3.322,
     'L1_ffn_router_b': 8.0,
     'L1_ffn_weights1': 3.851,
     'L1_ffn_bias1': 8.0,
     'L1_ffn_weights2': 3.319,
     'L1_ffn_bias2': 25.52}
    for name, (base, spread) in spreads.items():
        noise = np.random.default_rng([zlib.crc32(name.encode()), seed]).standard_normal(out[name].shape)
        drawn = base * np.exp(spread * noise) if base else spread * noise
        out[name] = jnp.asarray(drawn.astype(out[name].dtype))
    for name, factor in factors.items():
        out[name] = (out[name] * factor).astype(out[name].dtype)
    return out
```

```python
from contextlib import ExitStack, contextmanager

import numpy as np

import concourse.bass as bass
from concourse import mybir

F32 = mybir.dt.float32
F32R = mybir.dt.float32r
BF16 = mybir.dt.bfloat16
I32 = mybir.dt.int32
ALU = mybir.AluOpType
ACT = mybir.ActivationFunctionType
AX = mybir.AxisListType.X

P = 128
B, S, D = 4, 1024, 256
TILES = B * S // P
DT = D // P
HEADS, HD = 16, 16
FREQ = HD // 2
GH = 4
UNITS = B * 2
UH = HEADS // 2
KT = S // P
LT = 4
EPS = 1e-5
NEG = -1e30
PARTS_Q = (0, 0, 1, 0, 1, 2)
PARTS_K = (0, 1, 0, 2, 1, 0)
PROD = len(PARTS_Q) * HD
ROW_MAX = 2
TB = 125
REACH = TB // 2
BAND = P + 2 * 64
BIAS_ROWS = 3 * KT
STRIP = 2 * S - P


@contextmanager
def phase(nc, *names):
    with ExitStack() as held:
        sems = [held.enter_context(nc.semaphore(n)) for n in names]
        with nc.Block() as block:
            yield (block, *sems)
        numbers = sorted(s.num for s in sems)
        first = 0
        for i in range(len(numbers)):
            if i + 1 == len(numbers) or numbers[i + 1] != numbers[i] + 1:
                used = range(numbers[first], numbers[i] + 1)
                nc.gpsimd.dma_reset(used)
                nc.gpsimd.sem_clear(used)
                first = i + 1
        nc.all_engine_barrier()


def buffers(nc, held, tag):
    return (lambda n, s, d=F32: held.enter_context(nc.sbuf_tensor(f"{tag}_{n}", s, d)),
            lambda n, s: held.enter_context(nc.psum_tensor(f"{tag}_ps_{n}", s, F32)))


class Tensors:
    pass


class Chain:

    def __init__(self, eng, sem):
        self.eng, self.sem, self.n = eng, sem, 0

    def __call__(self, ins):
        ins.then_inc(self.sem, 1)
        self.n += 1
        self.eng.wait_ge(self.sem, self.n)


class Expert:

    def __init__(self, experts, top, hidden):
        self.E, self.top, self.F = experts, top, hidden
        self.FT = max(1, hidden // P)
        self.FP = min(P, hidden)
        self.cap = B * S + P
        self.tiles = B * S * top // P + experts - 1
        self.per = 8
        self.passes = -(-self.tiles // self.per)
        self.NT = self.passes * self.per
        self.zero_row = experts * self.cap
        self.rows = self.zero_row + P


MOE0, MOE1 = Expert(8, 2, 1024), Expert(32, 1, 64)


def setup(nc, ctx, t, a):
    sb, ps = buffers(nc, ctx, "all")
    t.h = sb("h", [P, TILES, D])
    t.ident = sb("ident", [P, P])
    t.ident_bf = sb("ident_bf", [P, P], BF16)
    t.ident_r = sb("ident_r", [P, P], F32R)
    t.ones_bf = sb("ones_bf", [P, P], BF16)
    t.before = sb("before", [P, P], BF16)
    t.den_row = sb("den_row", [P, P])
    t.wqT = [sb(f"wqT{l}", [P, DT, D]) for l in range(2)]
    t.wkT = [sb(f"wkT{l}", [P, DT, D]) for l in range(2)]
    t.wvT = [sb(f"wvT{l}", [P, DT, D]) for l in range(2)]
    t.woP = [sb(f"woP{l}", [P, HEADS // GH, D]) for l in range(2)]
    t.bqk = sb("bqk", [P, 2, 2])
    t.bv = sb("bv", [P, D])
    t.bo = sb("bo", [P, D])
    w = {0: "L0_attn_", 1: "L1_attn_"}
    with ExitStack() as own:
        tmp_sb, tmp_ps = buffers(nc, own, "setup")
        nat = tmp_sb("w_nat", [P, 8, 2, D])
        woT = tmp_sb("woT", [P, 2, DT, D])
        ps = tmp_ps("w", [P, 8, 512])
        with phase(nc, "consts_in", "w_in", "made", "turned", "moved", "placed", "zeroed", "small_in") as (
                block, consts_in, w_in, made, turned, moved, placed, zeroed, small_in):

            @block.sync
            def _(sp):
                sp.dma_start(t.ident[:], a["c_ident"]).then_inc(consts_in, 16)
                sp.dma_start(t.den_row[:], a["c_den_row"]).then_inc(consts_in, 16)
                for l in range(2):
                    for m, n in enumerate(("Wq", "Wk")):
                        src = a[w[l] + n].rearrange("(hi par) d -> hi par d", par=2)
                        sp.dma_start(nat[:, 4 * l + m, :, :], src).then_inc(w_in, 16)
                    for m, n in enumerate(("Wv", "Wo")):
                        src = a[w[l] + n].rearrange("(et e) d -> e et d", e=P)
                        sp.dma_start(nat[:, 4 * l + 2 + m, :, :], src).then_inc(w_in, 16)
                with nc.allow_non_contiguous_dma(reason="biases of one value per partition"):
                    for m, n in enumerate(("bq", "bk")):
                        src = a["L1_attn_" + n].rearrange("(hi par) -> hi par", par=2)
                        sp.dma_start(t.bqk[:, m, :], src).then_inc(small_in, 16)
                for dst, n in ((t.bv, "bv"), (t.bo, "bo")):
                    src = a["L1_attn_" + n].rearrange("(o d) -> o d", o=1).to_broadcast([P, D])
                    sp.dma_start(dst[:], src).then_inc(small_in, 16)
                sp.wait_ge(zeroed, 2)
                sp.wait_ge(moved, 8)
                for l in range(2):
                    for g in range(HEADS // GH):
                        for j in range(GH):
                            d0 = (GH * g + j) * HD
                            row, slot = (j, g) if l == 0 else (g, j)
                            sp.dma_start(t.woP[l][32 * row:32 * row + HD, slot, :],
                                         woT[d0 % P:d0 % P + HD, l, d0 // P, :]).then_inc(placed, 16)
                sp.wait_ge(placed, 16 * 2 * HEADS)
                sp.wait_ge(small_in, 64)

            @block.gpsimd
            def _(pool):
                for l in range(2):
                    pool.memset(t.woP[l][:], 0.0).then_inc(zeroed, 1)
                pool.memset(t.ones_bf[:], 1.0)
                pool.memset(t.before[:], 1.0).then_inc(made, 1)
                pool.wait_ge(made, 1)
                pool.affine_select(out=t.before[:], in_=t.before[:], compare_op=ALU.is_gt, fill=0.0,
                                   base=0, pattern=[[1, P]], channel_multiplier=-1)

            @block.tensor
            def _(pe):
                pe.wait_ge(consts_in, 32)
                pe.wait_ge(w_in, 128)
                for m in range(8):
                    for dt in range(DT):
                        for et in range(2):
                            at = dt * D + et * P
                            mm = pe.transpose(ps[:, m, at:at + P], nat[:, m, et, dt * P:(dt + 1) * P], t.ident[:])
                    mm.then_inc(turned, 1)

            @block.vector
            def _(dve):
                dve.wait_ge(consts_in, 32)
                dve.tensor_copy(t.ident_bf[:], t.ident[:])
                dve.tensor_copy(t.ident_r[:], t.ident[:])
                for m in range(8):
                    l = m // 4
                    dst = (t.wqT[l], t.wkT[l], t.wvT[l], None)[m % 4]
                    dst = woT[:, l] if dst is None else dst[:]
                    dve.wait_ge(turned, m + 1)
                    dve.tensor_copy(dst.rearrange("p a b -> p (a b)"), ps[:, m, :]).then_inc(moved, 1)


def embed(nc, t, a):
    R = 16
    with ExitStack() as own:
        sb, ps = buffers(nc, own, "embed")
        ids = sb("ids", [P, KT], I32)
        base = sb("emb_rows", [P, KT, D])
        la = sb("lora_rows", [P, KT, R])
        laT = sb("lora_rowsT", [R, KT, P])
        lb = sb("lora_b", [R, D])
        psT = ps("loraT", [R, KT, P])
        psD = ps("delta", [P, KT, D])
        x = a["x"].rearrange("b (t p) -> b p t", p=P)
        with nc.Fori(0, B) as b:
            with phase(nc, "ids_in", "lb_in", "rows_in", "lora_in", "turned", "copied", "delta") as (
                    block, ids_in, lb_in, rows_in, lora_in, turned, copied, delta):

                @block.sync
                def _(sp):
                    with nc.allow_non_contiguous_dma(reason="token ids go one to a partition"):
                        sp.dma_start(ids[:], x[bass.ds(b, 1)].rearrange("o p t -> (o p) t")).then_inc(ids_in, 16)
                    sp.dma_start(lb[:], a["L0_tok_lora_b"]).then_inc(lb_in, 16)

                @block.gpsimd
                def _(pool):
                    pool.wait_ge(ids_in, 16)
                    for i in range(KT):
                        off = bass.IndirectOffsetOnAxis(ap=ids[:, i:i + 1], axis=0)
                        pool.indirect_dma_start(la[:, i, :], None, a["L0_tok_lora_a"], off).then_inc(lora_in, 16)
                    for i in range(KT):
                        off = bass.IndirectOffsetOnAxis(ap=ids[:, i:i + 1], axis=0)
                        pool.indirect_dma_start(base[:, i, :], None, a["L0_tok_weight"], off).then_inc(rows_in, 16)
                    pool.wait_ge(lora_in, 16 * KT)
                    pool.wait_ge(rows_in, 16 * KT)

                @block.tensor
                def _(pe):
                    pe.wait_ge(lora_in, 16 * KT)
                    for i in range(KT):
                        mm = pe.transpose(psT[:, i, :], la[:, i, :], t.ident[:])
                    mm.then_inc(turned, 1)
                    pe.wait_ge(copied, 1)
                    pe.wait_ge(lb_in, 16)
                    for i in range(KT):
                        mm = pe.matmul(psD[:, i, :], laT[:, i, :], lb[:], start=True, stop=True)
                    mm.then_inc(delta, 1)

                @block.vector
                def _(dve):
                    dve.wait_ge(turned, 1)
                    dve.tensor_copy(laT[:], psT[:]).then_inc(copied, 1)
                    dve.wait_ge(delta, 1)
                    dve.wait_ge(rows_in, 16 * KT)
                    dve.scalar_tensor_tensor(out=t.h[:, bass.ds(b * KT, KT), :], in0=psD[:], scalar=2.0, in1=base[:],
                                             op0=ALU.mult, op1=ALU.add)


def norm_vector(dve, chain, t, n, tile0, var_ready, root_ready, normed):
    for j in range(LT):
        dve.bn_stats(n.stats[:, j, :], t.h[:, bass.ds(tile0 + j, 1), :].rearrange("p o d -> p (o d)")
                     ).then_inc(chain.sem, 1)
        chain.n += 1
    dve.wait_ge(chain.sem, chain.n)
    for j in range(LT):
        dve.bn_aggr(n.mv[:, j, :], n.stats[:, j, :]).then_inc(chain.sem, 1)
        chain.n += 1
    dve.wait_ge(chain.sem, chain.n)
    dve.tensor_scalar(n.var[:], n.mv[:, :, 1], EPS, None, ALU.add).then_inc(var_ready, 1)
    dve.wait_ge(root_ready, 1)
    chain(dve.reciprocal(n.inv[:], n.root[:]))
    chain(dve.tensor_tensor(n.inv[:], n.var[:], n.inv[:], ALU.mult))
    chain(dve.tensor_tensor(n.inv[:], n.inv[:], n.root[:], ALU.add))
    chain(dve.tensor_scalar(n.inv[:], n.inv[:], 0.5, None, ALU.mult))
    chain(dve.reciprocal(n.inv[:], n.inv[:]))
    for j in range(LT):
        dve.tensor_scalar(n.xn[:, j, :], t.h[:, bass.ds(tile0 + j, 1), :].rearrange("p o d -> p (o d)"),
                          n.mv[:, j, 0:1], n.inv[:, j:j + 1], ALU.subtract, ALU.mult).then_inc(normed, 1)


def norm_root(act, n, var_ready, root_ready):
    act.wait_ge(var_ready, 1)
    act.activation(n.root[:], n.var[:], ACT.Sqrt).then_inc(root_ready, 1)


def norm_turn(pe, t, n, psT, normed, turned):
    for j in range(LT):
        pe.wait_ge(normed, j + 1)
        for dt in range(DT):
            mm = pe.transpose(psT[:, dt, j * P:(j + 1) * P], n.xn[:, j, dt * P:(dt + 1) * P], t.ident[:])
    mm.then_inc(turned, 1)


def norm_buffers(sb):
    n = Tensors()
    n.stats, n.mv, n.var = sb("stats", [P, LT, 6]), sb("mv", [P, LT, 2]), sb("var", [P, LT])
    n.root, n.inv = sb("root", [P, LT]), sb("inv", [P, LT])
    n.xn, n.xT = sb("xn", [P, LT, D]), sb("xT", [P, DT, LT * P])
    return n


def project(nc, t, a, layer):
    W = LT * P
    rope = layer == 0
    with ExitStack() as own:
        sb, ps = buffers(nc, own, f"proj{layer}")
        n = norm_buffers(sb)
        raw = sb("qk_raw", [P, 2, 2, W])
        rot = sb("qk_rot", [P, 2, 2, W]) if rope else raw
        m1, m2 = (sb(f"rope_m{i}", [P, 2, W]) for i in range(2))
        m3, m4 = (sb(f"rope_m{i}", [P, 2, W]) for i in range(2, 4))
        part = [sb(f"part{i}", [P, 2, 2, W], BF16) for i in range(3)]
        rest = sb("rest", [P, 2, 2, W])
        vst = sb("v_stage", [P, LT, HEADS, 32])
        if rope:
            cos, sin = sb("cos", [P, S]), sb("sin", [P, S])
        psT = ps("xT", [P, DT, W])
        psQ = ps("qk", [P, 2, 2, W])
        psV = ps("v", [P, LT, D])
        with phase(nc, "tables_in", "v_set") as (block, tables_in, v_set):

            @block.sync
            def _(sp):
                if rope:
                    sp.dma_start(cos[:], a["c_cos"]).then_inc(tables_in, 16)
                    sp.dma_start(sin[:], a["c_sin"]).then_inc(tables_in, 16)
                    sp.wait_ge(tables_in, 32)

            @block.gpsimd
            def _(pool):
                pool.memset(vst[:, :, :, HD:32], 0.0).then_inc(v_set, 1)
                pool.wait_ge(v_set, 1)
                pool.memset(vst[:, :, :, HD:HD + 1], 1.0)

            if not rope:
                @block.vector
                def _(dve):
                    dve.tensor_scalar(t.bqk[:, 0, :], t.bqk[:, 0, :], 0.25, None, ALU.mult)

        with nc.Fori(0, B) as b, nc.Fori(0, 2) as th:
            with phase(nc, "chain", "var_ready", "root_ready", "normed", "turned", "x_ready", "qk_ready", "v_ready",
                       "raw_ready", "v_staged", "pool_m", "rotated", "split1", "split2", "rest1", "split3",
                       "v_out", "qk_out") as (
                    block, chain_sem, var_ready, root_ready, normed, turned, x_ready, qk_ready, v_ready,
                    raw_ready, v_staged, pool_m, rotated, split1, split2, rest1, split3, v_out, qk_out):

                @block.tensor
                def _(pe):
                    norm_turn(pe, t, n, psT, normed, turned)
                    pe.wait_ge(x_ready, 1)
                    for m, wT in enumerate((t.wqT[layer], t.wkT[layer])):
                        for par in range(2):
                            for dt in range(DT):
                                mm = pe.matmul(psQ[:, m, par, :], wT[:, dt, par * P:(par + 1) * P], n.xT[:, dt, :],
                                               start=(dt == 0), stop=(dt == DT - 1))
                            mm.then_inc(qk_ready, 1)
                    for j in range(LT):
                        for dt in range(DT):
                            mm = pe.matmul(psV[:, j, :], n.xT[:, dt, j * P:(j + 1) * P], t.wvT[layer][:, dt, :],
                                           start=(dt == 0), stop=(dt == DT - 1))
                    mm.then_inc(v_ready, 1)

                @block.scalar
                def _(act):
                    norm_root(act, n, var_ready, root_ready)
                    for i in range(4):
                        m, par = i // 2, i % 2
                        act.wait_ge(qk_ready, i + 1)
                        bias = 0.0 if rope else t.bqk[:, m, par:par + 1]
                        act.activation(raw[:, m, par, :], psQ[:, m, par, :], ACT.Identity, bias=bias,
                                       scale=(0.25 if m == 0 else 1.0)).then_inc(raw_ready, 1)
                    act.wait_ge(v_ready, 1)
                    for j in range(LT):
                        act.activation(vst[:, j, :, 0:HD], psV[:, j, :].rearrange("p (h c) -> p h c", h=HEADS),
                                       ACT.Copy).then_inc(v_staged, 1)
                    if rope:
                        act.wait_ge(rotated, 2)
                    else:
                        act.wait_ge(raw_ready, 4)
                    act.activation(part[0][:], rot[:], ACT.Copy).then_inc(split1, 1)
                    act.wait_ge(rest1, 1)
                    act.activation(part[1][:], rest[:], ACT.Copy).then_inc(split2, 1)

                @block.vector
                def _(dve):
                    chain = Chain(dve, chain_sem)
                    norm_vector(dve, chain, t, n, b * KT + th * LT, var_ready, root_ready, normed)
                    dve.wait_ge(turned, 1)
                    dve.tensor_copy(n.xT[:], psT[:]).then_inc(x_ready, 1)
                    if rope:
                        at = bass.ds(th * W, W)
                        c = cos[:, at].rearrange("p (o w) -> p o w", o=1).to_broadcast([P, 2, W])
                        s = sin[:, at].rearrange("p (o w) -> p o w", o=1).to_broadcast([P, 2, W])
                        dve.wait_ge(raw_ready, 4)
                        dve.tensor_tensor(m1[:], raw[:, :, 0, :], c, ALU.mult).then_inc(chain.sem, 1)
                        dve.tensor_tensor(m2[:], raw[:, :, 1, :], s, ALU.mult).then_inc(chain.sem, 1)
                        chain.n += 2
                        dve.wait_ge(chain.sem, chain.n)
                        dve.tensor_tensor(rot[:, :, 0, :], m1[:], m2[:], ALU.subtract).then_inc(rotated, 1)
                    elif layer == 1:
                        dve.wait_ge(v_staged, LT)
                        for j in range(LT):
                            v = vst[:, j, :, 0:HD]
                            dve.tensor_tensor(v, v, t.bv[:].rearrange("p (h c) -> p h c", h=HEADS),
                                              ALU.add).then_inc(v_staged, 1)
                    dve.wait_ge(split1, 1)
                    if rope:
                        dve.wait_ge(rotated, 2)
                    dve.tensor_tensor(rest[:], rot[:], part[0][:], ALU.subtract).then_inc(rest1, 1)
                    dve.wait_ge(split2, 1)
                    dve.wait_ge(rest1, 1)
                    dve.tensor_tensor(part[2][:], rest[:], part[1][:], ALU.subtract).then_inc(split3, 1)

                @block.gpsimd
                def _(pool):
                    if rope:
                        at = bass.ds(th * W, W)
                        c = cos[:, at].rearrange("p (o w) -> p o w", o=1).to_broadcast([P, 2, W])
                        s = sin[:, at].rearrange("p (o w) -> p o w", o=1).to_broadcast([P, 2, W])
                        pool.wait_ge(raw_ready, 4)
                        pool.tensor_tensor(m3[:], raw[:, :, 0, :], s, ALU.mult).then_inc(pool_m, 1)
                        pool.tensor_tensor(m4[:], raw[:, :, 1, :], c, ALU.mult).then_inc(pool_m, 1)
                        pool.wait_ge(pool_m, 2)
                        pool.tensor_tensor(rot[:, :, 1, :], m3[:], m4[:], ALU.add).then_inc(rotated, 1)

                @block.sync
                def _(sp):
                    sp.wait_ge(v_staged, LT if rope else 2 * LT)
                    dst = t.v_dram[bass.ds(b * KT + th * LT, LT)].rearrange("j p c -> p j c")
                    sp.dma_start(dst, vst[:].rearrange("p j h c -> p j (h c)")).then_inc(v_out, 16)
                    for s, ready in enumerate((split1, split2, split3)):
                        sp.wait_ge(ready, 1)
                        for m in range(2):
                            for par in range(2):
                                dst = t.qk_dram[bass.ds(b, 1), m, s, :, par * FREQ:(par + 1) * FREQ,
                                                bass.ds(th * W, W)]
                                sp.dma_start(dst.rearrange("o h i w -> (o h) i w"),
                                             part[s][:, m, par, :]).then_inc(qk_out, 16)
                    sp.wait_ge(qk_out, 16 * 12)
                    sp.wait_ge(v_out, 16)


def bias_tables(nc, own, t, a):
    sb, ps = buffers(nc, own, "bias")
    t.strip = sb("bias_strip", [P, STRIP])
    t.band = [sb(f"band{i}", [P, BAND], F32R) for i in range(2)]
    LS = STRIP + P - 1
    strip_dram = nc.dram_tensor("strip_rows", [P, LS], F32).ap()
    row_dram = nc.dram_tensor("strip_row", [1, LS], F32).ap()
    t.far_dram = nc.dram_tensor("bias_far", [BIAS_ROWS, S], BF16).ap()
    with ExitStack() as tmp:
        tb_, tp_ = buffers(nc, tmp, "bias_tmp")
        g = tb_("gates", [1, 4])
        tbf = tb_("time_bias", [1, TB])
        srow = tb_("strip_row_sb", [1, LS])
        vcol = tb_("bias_vals_col", [KT, 2])
        above, below = tb_("above", [KT, S]), tb_("below", [KT, S])
        far, rest = tb_("far", [KT, S]), tb_("far_rest", [KT, S])
        fp = [tb_(f"far_part{i}", [KT, S], BF16) for i in range(3)]
        bandf = tp_("band", [P, BAND])
        with phase(nc, "inputs", "sig", "chain", "row_ready", "row_out", "sheared", "strip_in", "col_in",
                   "parts_ready", "parts_out", "masks_in", "band_ready") as (
                block, inputs, sig, chain_sem, row_ready, row_out, sheared, strip_in, col_in,
                parts_ready, parts_out, masks_in, band_ready):

            @block.sync
            def _(sp):
                tbd = a["L1_attn_time_bias"].rearrange("a b n -> (a b) n")
                sp.dma_start(g[:, 0:1], a["L1_attn_et_gate"].rearrange("a b n -> (a b) n")).then_inc(inputs, 16)
                sp.dma_start(g[:, 1:2], a["L1_attn_is_gate"].rearrange("a b n -> (a b) n")).then_inc(inputs, 16)
                sp.dma_start(tbf[:], tbd).then_inc(inputs, 16)
                sp.dma_start(above[:], a["c_above"]).then_inc(masks_in, 16)
                sp.dma_start(below[:], a["c_below"]).then_inc(masks_in, 16)
                sp.wait_ge(row_ready, 1)
                sp.dma_start(row_dram, srow[:]).then_inc(row_out, 16)
                sp.wait_ge(row_out, 16)
                sp.dma_start(strip_dram, row_dram.to_broadcast([P, LS])).then_inc(sheared, 16)
                for i, x in enumerate((LS - 1, 0)):
                    sp.dma_start(vcol[:, i:i + 1], row_dram[:, x:x + 1].to_broadcast([KT, 1])).then_inc(col_in, 16)
                sp.wait_ge(sheared, 16)
                sp.dma_start(t.strip[:], bass.AP(tensor=strip_dram.tensor, offset=P - 1, ap=[[LS - 1, P], [1, STRIP]])
                             ).then_inc(strip_in, 16)
                sp.wait_ge(parts_ready, 3)
                for s in range(3):
                    sp.dma_start(t.far_dram[s * KT:(s + 1) * KT, :], fp[s][:]).then_inc(parts_out, 16)
                sp.wait_ge(parts_out, 48)

            @block.tensor
            def _(pe):
                pe.wait_ge(strip_in, 16)
                for c in range(2):
                    x = S - P + 64 - c * P
                    mm = pe.transpose(bandf[:, c * P:(c + 1) * P], t.strip[:, x:x + P], t.ident[:])
                mm.then_inc(band_ready, 1)

            @block.scalar
            def _(act):
                act.wait_ge(inputs, 48)
                act.activation(g[:, 2:3], g[:, 0:1], ACT.Exp, scale=-1.0).then_inc(sig, 1)

            @block.vector
            def _(dve):
                chain = Chain(dve, chain_sem)
                dve.wait_ge(sig, 1)
                chain(dve.tensor_scalar(g[:, 2:3], g[:, 2:3], 1.0, None, ALU.add))
                chain(dve.reciprocal(g[:, 3:4], g[:, 2:3]))
                chain(dve.tensor_scalar(tbf[:], tbf[:], g[:, 3:4], None, ALU.mult))
                first = S - 1 - REACH
                chain(dve.memset(srow[:], 0.0))
                chain(dve.tensor_scalar(srow[:, 0:first], srow[:, 0:first], tbf[:, 0:1], g[:, 1:2], ALU.add, ALU.add))
                chain(dve.tensor_scalar(srow[:, first:first + TB], tbf[:], g[:, 1:2], None, ALU.add))
                dve.tensor_scalar(srow[:, first + TB:], srow[:, first + TB:], tbf[:, TB - 1:TB], g[:, 1:2],
                                  ALU.add, ALU.add).then_inc(row_ready, 1)
                dve.wait_ge(band_ready, 1)
                chain(dve.tensor_copy(t.band[0][:], bandf[:]))
                chain(dve.tensor_tensor(t.band[1][:], bandf[:], t.band[0][:].bitcast(F32), ALU.subtract))
                dve.wait_ge(col_in, 32)
                dve.wait_ge(masks_in, 32)
                chain(dve.tensor_scalar(far[:], above[:], vcol[:, 0:1], None, ALU.mult))
                chain(dve.tensor_scalar(rest[:], below[:], vcol[:, 1:2], None, ALU.mult))
                chain(dve.tensor_tensor(far[:], far[:], rest[:], ALU.add))
                chain(dve.tensor_copy(fp[0][:], far[:]))
                chain(dve.tensor_tensor(rest[:], far[:], fp[0][:], ALU.subtract))
                chain(dve.tensor_copy(fp[1][:], rest[:]))
                dve.tensor_tensor(fp[2][:], rest[:], fp[1][:], ALU.subtract).then_inc(parts_ready, 3)


def attention(nc, t, a, layer):
    causal = layer == 0
    KS = PROD + ROW_MAX + (0 if causal else BIAS_ROWS)
    with ExitStack() as own:
        sb, ps = buffers(nc, own, f"attn{layer}")
        if causal:
            t.strip = sb("mask_strip", [P, STRIP])
            maskT = sb("maskT", [P, P], BF16)
        else:
            bias_tables(nc, own, t, a)
        qst = [sb(f"q_rows{g}", [P, GH, S], BF16) for g in range(2)]
        kst = [sb(f"k_rows{g}", [P, GH, S], BF16) for g in range(2)]
        v = sb("v", [P, KT, UH * 32])
        prob = sb("prob", [P, 2 * GH, S])
        junk = sb("junk", [P, 512], BF16)
        mx = sb("mx", [P, 2, 2, GH * KT])
        negm = sb("negm", [P, 2, 2, GH * KT], BF16)
        negmT = sb("negmT", [2 * GH * KT, 2, P], BF16)
        oT = sb("oT", [P, 2, S])
        rden = sb("rden", [P, S])
        on = sb("on", [P, 2, S])
        stage = None if causal else sb("out_stage", [P, 2, 2, D])
        psS = ps("scores", [P, 2, S])
        acc = ps("out", [P, S])
        aux = ps("aux", [P, 2, 512])
        with phase(nc, "filled", "far_in", "chain") as (block, filled, far_in, chain_sem):

            @block.gpsimd
            def _(pool):
                chain = Chain(pool, chain_sem)
                if causal:
                    chain(pool.memset(t.strip[:], 0.0))
                    chain(pool.affine_select(out=t.strip[:], in_=t.strip[:], compare_op=ALU.is_ge, fill=NEG,
                                             base=S - P, pattern=[[-1, STRIP]], channel_multiplier=1))
                    chain(pool.memset(maskT[:], 0.0))
                    chain(pool.affine_select(out=maskT[:], in_=maskT[:], compare_op=ALU.is_ge, fill=NEG,
                                             base=0, pattern=[[1, P]], channel_multiplier=-1))
                chain(pool.memset(mx[:], NEG))
                for g in range(2):
                    for j in range(GH):
                        pool.dma_start(kst[g][PROD:KS, j, :], a["c_key_rows"][0:KS - PROD, :]).then_inc(filled, 16)
                pool.wait_ge(filled, 16 * 2 * GH)

            if not causal:
                @block.sync
                def _(sp):
                    for g in range(2):
                        for j in range(GH):
                            sp.dma_start(qst[g][PROD + ROW_MAX:KS, j, :], t.far_dram).then_inc(far_in, 16)
                    sp.wait_ge(far_in, 16 * 2 * GH)

        jobs = []
        for j in range(GH):
            for qt in range(KT):
                end = (qt + 1) * P if causal else S
                for kh in range(2):
                    n = min(end - 512 * kh, 512)
                    if n > 0:
                        jobs.append((j, qt, kh, n))
        NJ = len(jobs)
        plan = [("max", 0, i) for i in range(NJ)] + [("turn", 0, 0)]
        steps = []
        spv = [[("spv", g, kt) for kt in range(KT)] for g in range(2)]
        order = [*plan]
        per = -(-NJ // KT)
        for kt in range(KT):
            order.append(("spv", 0, kt))
            order += [("max", 1, i) for i in range(kt * per, min((kt + 1) * per, NJ))]
        order += [("turn", 1, 0)]
        order += [("den", 0, 0), ("den", 0, 1)]
        order += spv[1]
        order += [("den", 1, 0), ("den", 1, 1)]
        order += [("out", i // 2, i % 2) for i in range(4)]
        aux_jobs = [x for x in order if x[0] != "spv"]
        aux_no = {x: i for i, x in enumerate(aux_jobs)}
        live = lambda kt: (kt * P if causal else 0)
        last_kt = lambda qh: (3 if causal and qh == 0 else KT - 1)

        with nc.Fori(0, B) as b, nc.Fori(0, 2) as hg:
            with phase(nc, "q0_in", "q1_in", "k0_in", "k1_in", "v_in", "m0_in", "m1_in", "aux_full", "aux_free",
                       "negm_ready", "scores_full", "probs_ready", "pv_done", "acc_full",
                       "acc_moved", "rden_ready", "on_ready", "rows_out", "chain") as (
                    block, q0_in, q1_in, k0_in, k1_in, v_in, m0_in, m1_in, aux_full, aux_free,
                    negm_ready, scores_full, probs_ready, pv_done, acc_full,
                    acc_moved, rden_ready, on_ready, rows_out, chain_sem):
                q_in, k_in, m_in = (q0_in, q1_in), (k0_in, k1_in), (m0_in, m1_in)

                @block.sync
                def _(sp):
                    for g in range(2):
                        for m, (dst, parts, sem) in enumerate(((qst[g], PARTS_Q, q_in[g]), (kst[g], PARTS_K, k_in[g]))):
                            for c, s in enumerate(parts):
                                src = t.qk_dram[bass.ds(b, 1), m, s, bass.ds(hg * UH + g * GH, GH)]
                                sp.dma_start(dst[c * HD:(c + 1) * HD, :, :],
                                             src.rearrange("o h i w -> i (o h) w")).then_inc(sem, 16)
                    src = t.v_dram[bass.ds(b * KT, KT), :, bass.ds(hg * UH * 32, UH * 32)]
                    sp.dma_start(v[:], src.rearrange("k p c -> p k c")).then_inc(v_in, 16)
                    for g in range(2):
                        sp.wait_ge(aux_free, aux_no[("turn", g, 0)] + 1)
                        for s in range(ROW_MAX):
                            n = GH * KT
                            sp.dma_start(qst[g][PROD + s:PROD + s + 1, :, :].rearrange("p j (q w) -> p (j q) w", w=P),
                                         negmT[s * n:(s + 1) * n, g, :]).then_inc(m_in[g], 16)
                    if not causal:
                        for g in range(2):
                            for i in range(2):
                                sp.wait_ge(aux_free, aux_no[("out", g, i)] + 1)
                                for k in range(2):
                                    row = bass.ds(((hg * 2 + g) * GH + 2 * i + k) * B + b, 1)
                                    sp.dma_start(t.attn_dram[row].rearrange("o p d -> (o p) d"),
                                                 stage[64 * k:64 * k + 64, g, i, :]).then_inc(rows_out, 16)
                        sp.wait_ge(rows_out, 16 * 8)

                def scores(pe, g, kt):
                    for j in range(GH):
                        n = (g * KT + kt) * GH + j
                        if n >= 2:
                            pe.wait_ge(probs_ready, n - 1)
                        if kt == 0 and j == 0:
                            pe.wait_ge(m_in[g], 32)
                        lhs = kst[g][0:KS, j, kt * P:(kt + 1) * P]
                        for qh in range(2):
                            c0, c1 = max(live(kt), 512 * qh), 512 * (qh + 1)
                            if c0 >= c1:
                                continue
                            extra = []
                            if causal and live(kt) // 512 == qh:
                                extra = [(live(kt), P, t.ident_bf, maskT[:])]
                            if not causal:
                                q0, q1 = max(c0, kt * P - 64), min(c1, kt * P - 64 + BAND)
                                if q0 < q1:
                                    o = q0 - (kt * P - 64)
                                    extra = [(q0, q1 - q0, t.ident_r, t.band[i][:, o:o + q1 - q0]) for i in range(2)]
                            mm = pe.matmul(psS[:, n % 2, c0:c1], lhs, qst[g][0:KS, j, c0:c1],
                                           start=True, stop=True)
                            for i, (q0, w, eye, add) in enumerate(extra):
                                mm = pe.matmul(psS[:, n % 2, q0:q0 + w], eye[:], add, start=False,
                                               stop=True, skip_group_check=True)
                        mm.then_inc(scores_full, 1)

                def times_v(pe, g, kt):
                    n = (g * KT + kt) * GH
                    pe.wait_ge(probs_ready, n + GH)
                    if g == 0 and kt == 0:
                        pe.wait_ge(v_in, 16)
                    if g == 1 and kt == 0:
                        pe.wait_ge(acc_moved, 1)
                    for qh in range(2):
                        c0, c1 = max(live(kt), 512 * qh), 512 * (qh + 1)
                        if c0 >= c1:
                            continue
                        for j in range(GH):
                            c = (g * GH + j) * 32
                            if causal:
                                mm = pe.matmul(acc[32 * j:32 * j + 32, c0:c1], v[:, kt, c:c + 32],
                                               prob[:, (n + j) % (2 * GH), c0:c1],
                                               start=(kt == 0), stop=(kt == last_kt(qh)))
                                continue
                            for w in range(2 * qh, 2 * qh + 2):
                                mm = pe.matmul(acc[32 * w:32 * w + 32, j * 256:(j + 1) * 256], v[:, kt, c:c + 32],
                                               prob[:, (n + j) % (2 * GH), :].rearrange("p (u w r) -> p w u r", w=4, r=4)[:, w],
                                               start=(kt == 0 and j % 2 == 0), stop=(kt == KT - 1),
                                               skip_group_check=True)
                    mm.then_inc(pv_done, 1)

                @block.tensor
                def _(pe):
                    late = None
                    for kind, g, i in order:
                        if kind == "spv":
                            scores(pe, g, i)
                            if late:
                                times_v(pe, *late)
                            late = (g, i)
                            if i == KT - 1:
                                times_v(pe, *late)
                                late = None
                            continue
                        n = aux_no[(kind, g, i)]
                        if n >= 2:
                            pe.wait_ge(aux_free, n - 1)
                        bank = aux[:, n % 2, :]
                        if kind == "max":
                            j, qt, kh, w = jobs[i]
                            if i == 0:
                                pe.wait_ge(q_in[g], 16 * 6)
                                pe.wait_ge(k_in[g], 16 * 6)
                            mm = pe.matmul(bank[:, 0:w], qst[g][0:PROD, j, qt * P:(qt + 1) * P],
                                           kst[g][0:PROD, j, kh * 512:kh * 512 + w], start=True, stop=True)
                        elif kind == "turn":
                            pe.wait_ge(negm_ready, g + 1)
                            mm = pe.transpose(bank[0:2 * GH * KT, 0:P // 2].bitcast(BF16),
                                              negm[:, g, :, :].rearrange("p s n -> p (s n)"), t.ident_bf[:])
                        elif kind == "den":
                            pe.wait_ge(acc_moved, g + 1)
                            mm = pe.matmul(bank, t.den_row[:], oT[:, g, i * 512:(i + 1) * 512], start=True, stop=True)
                        elif not causal:
                            pe.wait_ge(on_ready, 2 * g + 2)
                            for k in range(2):
                                j = 2 * i + k
                                for r in range(4):
                                    lhs = on[:, g, j * 256:(j + 1) * 256].rearrange("p (u r) -> p r u", r=4)[:, r]
                                    mm = pe.matmul(bank[64 * k:64 * k + 64, 0:D], lhs, t.woP[layer][:, r, :],
                                                   start=(r == 0), stop=(r == 3))
                        else:
                            pe.wait_ge(on_ready, 4)
                            for k in range(2):
                                q = (2 * (2 * g + i) + k) * P
                                for gg in range(2):
                                    mm = pe.matmul(bank[:, k * D:(k + 1) * D], on[:, gg, q:q + P],
                                                   t.woP[layer][:, bass.ds(hg * 2 + gg, 1), :].rearrange("p o d -> p (o d)"),
                                                   start=(gg == 0), stop=(gg == 1))
                        mm.then_inc(aux_full, 1)

                @block.scalar
                def _(act):
                    for g in range(2):
                        for kt in range(KT):
                            for j in range(GH):
                                n = (g * KT + kt) * GH + j
                                act.wait_ge(scores_full, n + 1)
                                if n >= 2 * GH:
                                    act.wait_ge(pv_done, n // GH - 1)
                                q0 = live(kt)
                                act.activation(prob[:, n % (2 * GH), q0:S], psS[:, n % 2, q0:S], ACT.Exp
                                               ).then_inc(probs_ready, 1)
                        act.wait_ge(pv_done, (g + 1) * KT)
                        act.activation(oT[:, g, :], acc[:], ACT.Copy).then_inc(acc_moved, 1)

                @block.vector
                def _(dve):
                    chain = Chain(dve, chain_sem)
                    for n, (kind, g, i) in enumerate(aux_jobs):
                        bank = aux[:, n % 2, :]
                        dve.wait_ge(aux_full, n + 1)
                        if kind == "max":
                            j, qt, kh, w = jobs[i]
                            at = S - P - P * qt + 512 * kh
                            c = j * KT + qt
                            if i or g:
                                dve.wait_ge(aux_free, n)
                            dve.tensor_tensor_reduce(junk[:, 0:w], bank[:, 0:w], t.strip[:, at:at + w], 1.0, NEG,
                                                     ALU.add, ALU.max, mx[:, g, kh, c:c + 1]).then_inc(aux_free, 1)
                            if i == NJ - 1:
                                dve.wait_ge(aux_free, n + 1)
                                chain(dve.tensor_tensor(mx[:, g, 0, :], mx[:, g, 0, :], mx[:, g, 1, :], ALU.max))
                                chain(dve.tensor_scalar(negm[:, g, 0, :], mx[:, g, 0, :], -1.0, None, ALU.mult))
                                dve.scalar_tensor_tensor(out=negm[:, g, 1, :], in0=mx[:, g, 0, :], scalar=-1.0,
                                                         in1=negm[:, g, 0, :], op0=ALU.mult, op1=ALU.subtract
                                                         ).then_inc(negm_ready, 1)
                        elif kind == "turn":
                            dve.tensor_copy(negmT[:, g, :], bank[0:2 * GH * KT, 0:P // 2].bitcast(BF16)
                                            ).then_inc(aux_free, 1)
                        elif kind == "den":
                            if g == 1:
                                dve.wait_ge(on_ready, 2)
                            dve.reciprocal(rden[:, i * 512:(i + 1) * 512], bank).then_inc(aux_free, 1)
                            dve.wait_ge(aux_free, n + 1)
                            dve.tensor_tensor(on[:, g, i * 512:(i + 1) * 512], oT[:, g, i * 512:(i + 1) * 512],
                                              rden[:, i * 512:(i + 1) * 512], ALU.mult).then_inc(on_ready, 1)
                        elif not causal:
                            dve.tensor_copy(stage[:, g, i, :], bank[:, 0:D]).then_inc(aux_free, 1)
                        else:
                            i = 2 * g + i
                            hh = t.h[:, bass.ds(b * KT + 2 * i, 2), :].rearrange("p k d -> p (k d)")
                            dve.tensor_tensor(hh, hh, bank, ALU.add).then_inc(aux_free, 1)


def add_attention(nc, t):
    with ExitStack() as own:
        sb, _ = buffers(nc, own, "add")
        rows = sb("attn_rows", [P, KT, D])
        src = t.attn_dram.rearrange("(n k) p d -> n (k p) d", k=2)
        with nc.Fori(0, B) as b:
            with phase(nc, "rows_in", "biased") as (block, rows_in, biased):
                tiles = bass.ds(b * KT, KT)

                @block.sync
                def _(sp):
                    sp.dma_start(rows[:], src[tiles].rearrange("n p d -> p n d")).then_inc(rows_in, 16)

                @block.vector
                def _(dve):
                    bo = t.bo[:].rearrange("p (o d) -> p o d", o=1).to_broadcast([P, KT, D])
                    dve.tensor_tensor(t.h[:, tiles, :], t.h[:, tiles, :], bo, ALU.add).then_inc(biased, 1)
                    dve.wait_ge(rows_in, 16)
                    dve.wait_ge(biased, 1)
                    dve.tensor_tensor(t.h[:, tiles, :], t.h[:, tiles, :], rows[:], ALU.add)


def route(nc, t, a, layer, m):
    W, E, K = LT * P, m.E, m.top
    with ExitStack() as own:
        sb, ps = buffers(nc, own, f"route{layer}")
        n = norm_buffers(sb)
        wg = sb("router_w", [P, DT, E])
        bg = sb("router_b", [P, E])
        iota_e, cap_e = t.iota_e[:, 0:E], sb("cap_e", [P, E])
        carry = sb("carry", [P, E])
        base = sb("base", [P, LT, E])
        lg, pr, pos = sb("logits", [P, LT, E]), sb("gate_probs", [P, LT, E]), sb("pos", [P, LT, E])
        tmp = sb("tmp", [P, LT, E])
        red = sb("red", [P, LT])
        top = sb("top8", [P, LT, 8])
        topi = sb("top8_index", [P, LT, 8], mybir.dt.uint32)
        topf = sb("top_index", [P, LT, K])
        hot = sb("one_hot", [P, K, LT, E])
        hot_bf = sb("one_hot_bf", [P, LT, E], BF16)
        posf = sb("pos_f", [P, K, LT])
        posi = sb("pos_i", [P, K, LT], I32)
        wsum = sb("weight_sum", [P, LT])
        zero = sb("zero_rows", [P, D])
        zpos, zposi = sb("zero_pos", [P, E]), sb("zero_pos_i", [P, E], I32)
        pcol = sb("partition_no", [P, 1])
        psT = ps("xT", [P, DT, W])
        psL = ps("logits", [P, LT, E])
        psR = ps("rank", [P, LT, E])
        psN = ps("count", [P, LT, E])
        if layer == 1:
            wnat = sb("router_nat", [E, D])
        wide = lambda ap: ap.rearrange("p (o e) -> p o e", o=1).to_broadcast([P, LT, E])
        tall = lambda ap: ap.rearrange("p (k o) -> p k o", o=1).to_broadcast([P, LT, E])
        with phase(nc, "loaded", "made", "turned", "copied") as (block, loaded, made, turned, copied):

            @block.sync
            def _(sp):
                if layer == 0:
                    sp.dma_start(wg[:], a["L0_ffn_Wg"].rearrange("(dt d) e -> d dt e", d=P)).then_inc(loaded, 16)
                    bias = a["L0_ffn_bg"]
                else:
                    sp.dma_start(wnat[:], a["L1_ffn_router_w"]).then_inc(loaded, 16)
                    bias = a["L1_ffn_router_b"]
                sp.dma_start(bg[:], bias.rearrange("(o e) -> o e", o=1).to_broadcast([P, E])).then_inc(loaded, 16)
                sp.wait_ge(loaded, 32)

            @block.gpsimd
            def _(pool):
                pool.iota(iota_e, pattern=[[1, E]], base=0, channel_multiplier=0,
                          allow_small_or_imprecise_dtypes=True)
                pool.iota(cap_e[:], pattern=[[m.cap, E]], base=0, channel_multiplier=0,
                          allow_small_or_imprecise_dtypes=True)
                pool.iota(carry[:], pattern=[[m.cap, E]], base=0, channel_multiplier=0,
                          allow_small_or_imprecise_dtypes=True)
                pool.iota(pcol[:], pattern=[[1, 1]], base=0, channel_multiplier=1,
                          allow_small_or_imprecise_dtypes=True)
                pool.memset(zero[:], 0.0)

            if layer == 1:
                @block.tensor
                def _(pe):
                    pe.wait_ge(loaded, 32)
                    for dt in range(DT):
                        mm = pe.transpose(psT[:, dt, 0:E], wnat[:, dt * P:(dt + 1) * P], t.ident[0:E, 0:E])
                    mm.then_inc(turned, 1)

                @block.vector
                def _(dve):
                    dve.wait_ge(turned, 1)
                    dve.tensor_copy(wg[:], psT[:, :, 0:E])

        with nc.Fori(0, B) as b, nc.Fori(0, 2) as th:
            with phase(nc, "chain", "var_ready", "root_ready", "normed", "turned", "x_ready", "logits_ready",
                       "shifted", "exped", "hot_ready", "ranked", "pos_ready", "scattered") as (
                    block, chain_sem, var_ready, root_ready, normed, turned, x_ready, logits_ready,
                    shifted, exped, hot_ready, ranked, pos_ready, scattered):

                @block.tensor
                def _(pe):
                    norm_turn(pe, t, n, psT, normed, turned)
                    pe.wait_ge(x_ready, 1)
                    for j in range(LT):
                        for dt in range(DT):
                            mm = pe.matmul(psL[:, j, :], n.xT[:, dt, j * P:(j + 1) * P], wg[:, dt, :],
                                           start=(dt == 0), stop=(dt == DT - 1))
                    mm.then_inc(logits_ready, 1)
                    pe.wait_ge(hot_ready, 1)
                    flat = hot_bf[:].rearrange("p j e -> p (j e)")
                    pe.matmul(psR[:].rearrange("p j e -> p (j e)"), t.before[:], flat, start=True, stop=True)
                    pe.matmul(psN[:].rearrange("p j e -> p (j e)"), t.ones_bf[:], flat, start=True, stop=True
                              ).then_inc(ranked, 1)

                @block.scalar
                def _(act):
                    norm_root(act, n, var_ready, root_ready)
                    if K == 2:
                        act.wait_ge(shifted, 1)
                        act.activation(pr[:], lg[:], ACT.Exp).then_inc(exped, 1)

                @block.vector
                def _(dve):
                    chain = Chain(dve, chain_sem)
                    norm_vector(dve, chain, t, n, b * KT + th * LT, var_ready, root_ready, normed)
                    dve.wait_ge(turned, 1)
                    dve.tensor_copy(n.xT[:], psT[:]).then_inc(x_ready, 1)
                    dve.wait_ge(logits_ready, 1)
                    chain(dve.tensor_tensor(lg[:], psL[:], wide(bg[:]), ALU.add))
                    score = lg
                    if K == 2:
                        chain(dve.tensor_reduce(red[:], lg[:], AX, ALU.max))
                        dve.tensor_tensor(lg[:], lg[:], tall(red[:]), ALU.subtract).then_inc(shifted, 1)
                        dve.wait_ge(exped, 1)
                        chain(dve.tensor_reduce(red[:], pr[:], AX, ALU.add))
                        chain(dve.reciprocal(red[:], red[:]))
                        chain(dve.tensor_tensor(pr[:], pr[:], tall(red[:]), ALU.mult))
                        score = pr
                    for j in range(LT):
                        chain(dve.max(top[:, j, :], score[:, j, :]))
                        chain(dve.max_index(topi[:, j, :], top[:, j, :], score[:, j, :]))
                    chain(dve.tensor_copy(topf[:], topi[:, :, 0:K]))
                    for k in range(K):
                        chain(dve.tensor_tensor(hot[:, k], wide(iota_e),
                                                topf[:, :, k:k + 1].to_broadcast([P, LT, E]), ALU.is_equal))
                    if K == 2:
                        dve.tensor_tensor(hot_bf[:], hot[:, 0], hot[:, 1], ALU.add).then_inc(hot_ready, 1)
                        chain(dve.tensor_tensor(wsum[:], top[:, :, 0], top[:, :, 1], ALU.add))
                        chain(dve.tensor_scalar(wsum[:], wsum[:], 1e-8, None, ALU.add))
                        chain(dve.reciprocal(wsum[:], wsum[:]))
                        for k in range(K):
                            dve.tensor_tensor(t.weight[:, k, bass.ds(b * KT + th * LT, LT)], top[:, :, k], wsum[:],
                                              ALU.mult)
                    else:
                        dve.tensor_copy(hot_bf[:], hot[:, 0]).then_inc(hot_ready, 1)
                    dve.wait_ge(ranked, 1)
                    chain(dve.tensor_copy(base[:, 0, :], carry[:]))
                    for j in range(1, LT):
                        chain(dve.tensor_tensor(base[:, j, :], base[:, j - 1, :], psN[:, j - 1, :], ALU.add))
                    chain(dve.tensor_tensor(carry[:], base[:, LT - 1, :], psN[:, LT - 1, :], ALU.add))
                    chain(dve.tensor_tensor(pos[:], base[:], psR[:], ALU.add))
                    for k in range(K):
                        chain(dve.tensor_tensor(tmp[:], pos[:], hot[:, k], ALU.mult))
                        chain(dve.tensor_reduce(posf[:, k, :], tmp[:], AX, ALU.add))
                    dve.tensor_copy(posi[:], posf[:]).then_inc(pos_ready, 1)
                    dve.tensor_copy(t.row_of[:, 0:K, bass.ds(b * KT + th * LT, LT)], posf[:])
                    dve.tensor_copy(t.expert_of[:, 0:K, bass.ds(b * KT + th * LT, LT)],
                                    topf[:].rearrange("p j k -> p k j"))

                @block.gpsimd
                def _(pool):
                    pool.wait_ge(pos_ready, 1)
                    for k in range(K):
                        for j in range(LT):
                            off = bass.IndirectOffsetOnAxis(ap=posi[:, k, j:j + 1], axis=0)
                            pool.indirect_dma_start(t.x_rows[layer], off, n.xn[:, j, :], None).then_inc(scattered, 16)
                    pool.wait_ge(scattered, 16 * K * LT)

        expert_table(nc, own, t, m, layer, carry, cap_e, iota_e, pcol, zpos, zposi, zero)


def expert_table(nc, own, t, m, layer, carry, cap_e, iota_e, pcol, zpos, zposi, zero):
    E, NT = m.E, m.NT
    sb, ps = buffers(nc, own, f"table{layer}")
    cnt, cnti = sb("cnt", [P, E]), sb("cnt_i", [P, E], I32)
    end, one = sb("end", [P, E]), sb("one_row", [P, E])
    f = t.shift[:, 0:E]
    tno = sb("tile_no", [1, NT])
    ge, sel = sb("past", [1, NT, E]), sb("owner", [1, NT, E])
    te, row, tail = sb("tile_expert", [1, NT]), sb("tile_row", [1, NT]), sb("tail", [1, NT])
    x1 = sb("x1", [1, NT])
    with phase(nc, "zpos_ready", "zeroed", "tno_ready", "chain") as (block, zpos_ready, zeroed, tno_ready, chain_sem):

        @block.gpsimd
        def _(pool):
            pool.iota(tno[:], pattern=[[1, NT]], base=0, channel_multiplier=0,
                      allow_small_or_imprecise_dtypes=True).then_inc(tno_ready, 1)
            pool.wait_ge(zpos_ready, 1)
            for e in range(E):
                off = bass.IndirectOffsetOnAxis(ap=zposi[:, e:e + 1], axis=0)
                pool.indirect_dma_start(t.x_rows[layer], off, zero[:], None).then_inc(zeroed, 16)
            pool.dma_start(t.x_rows[layer][m.zero_row:m.zero_row + P, :], zero[:]).then_inc(zeroed, 16)
            pool.wait_ge(zeroed, 16 * (E + 1))

        @block.vector
        def _(dve):
            chain = Chain(dve, chain_sem)
            chain(dve.tensor_scalar(zpos[:], carry[:], pcol[:, 0:1], None, ALU.add))
            dve.tensor_copy(zposi[:], zpos[:]).then_inc(zpos_ready, 1)
            chain(dve.tensor_tensor(cnt[:], carry[:], cap_e[:], ALU.subtract))
            chain(dve.tensor_scalar(cnt[:], cnt[:], float(P - 1), None, ALU.add))
            chain(dve.tensor_copy(cnti[:], cnt[:]))
            chain(dve.tensor_scalar(cnti[:], cnti[:], 7, None, ALU.arith_shift_right))
            chain(dve.tensor_copy(cnt[:], cnti[:]))
            chain(dve.memset(one[:], 1.0))
            chain(dve.tensor_tensor_scan(end[:], one[:], cnt[:], 0.0, ALU.mult, ALU.add))
            chain(dve.tensor_tensor(f, end[:], cnt[:], ALU.subtract))
            chain(dve.tensor_scalar(f, f, -float(P), None, ALU.mult))
            chain(dve.tensor_tensor(f, f, cap_e[:], ALU.add))
            dve.wait_ge(tno_ready, 1)
            by_tile = lambda ap: ap.rearrange("p (n o) -> p n o", o=1).to_broadcast([1, NT, E])
            by_e = lambda ap: ap.rearrange("p (o e) -> p o e", o=1).to_broadcast([1, NT, E])
            chain(dve.tensor_tensor(ge[:], by_e(end[0:1, :]), by_tile(tno[:]), ALU.is_le))
            chain(dve.tensor_reduce(te[:], ge[:], AX, ALU.add))
            chain(dve.tensor_scalar(te[:], te[:], float(E - 1), None, ALU.min))
            chain(dve.tensor_tensor(sel[:], by_e(iota_e[0:1, :]), by_tile(te[:]), ALU.is_equal))
            chain(dve.tensor_tensor(sel[:], sel[:], by_e(t.shift[0:1, 0:E]), ALU.mult))
            chain(dve.tensor_reduce(row[:], sel[:], AX, ALU.add))
            chain(dve.tensor_scalar(x1[:], tno[:], float(P), None, ALU.mult))
            chain(dve.tensor_tensor(row[:], row[:], x1[:], ALU.add))
            chain(dve.tensor_copy(tail[:], ge[:, :, E - 1]))
            chain(dve.tensor_copy(t.table[:, 0, 0:NT], te[:]))
            chain(dve.tensor_scalar(x1[:], row[:], -1.0, float(m.zero_row), ALU.mult, ALU.add))
            chain(dve.tensor_tensor(x1[:], x1[:], tail[:], ALU.mult))
            chain(dve.tensor_tensor(x1[:], x1[:], row[:], ALU.add))
            chain(dve.tensor_copy(t.table[:, 1, 0:NT], x1[:]))
            chain(dve.memset(x1[:], 1.0))
            chain(dve.tensor_tensor(x1[:, 2:NT], te[:, 2:NT], te[:, 0:NT - 2], ALU.not_equal))
            chain(dve.tensor_copy(t.table[:, 2, 0:NT], x1[:]))


def experts(nc, t, a, layer, m):
    E, FT, FP, F, NT = m.E, m.FT, m.FP, m.F, m.NT
    with ExitStack() as own:
        sb, ps = buffers(nc, own, f"experts{layer}")
        w1 = sb("w1", [P, 2, DT, F])
        w2 = sb("w2", [FP, 2, FT, D])
        b1 = sb("b1", [FP, E * FT])
        b2 = sb("b2", [P, E, D])
        NX = 4
        HB = 512 // P
        HBANKS = -(-FT // HB)
        xr = sb("x_tile", [P, NX, D])
        xT = sb("xT_tile", [P, 2, DT, P])
        hT = sb("hidden", [FP, 2, FT, P])
        y = sb("y_tile", [P, NX, D])
        psX = ps("x", [P, 2, 512])
        psH = ps("hidden", [FP, 2, 1024])
        psY = ps("y", [P, 2, 512])
        n0 = ("L0_ffn_W1", "L0_ffn_b1", "L0_ffn_W2", "L0_ffn_b2")
        n1 = ("L1_ffn_weights1", "L1_ffn_bias1", "L1_ffn_weights2", "L1_ffn_bias2")
        W1, B1, W2, B2 = (a[x] for x in (n1 if layer else n0))
        with phase(nc, "loaded") as (block, loaded):

            @block.sync
            def _(sp):
                with nc.allow_non_contiguous_dma(reason="hidden biases go one to a partition"):
                    sp.dma_start(b1[:], B1.rearrange("e (ft f) -> f (e ft)", f=FP)).then_inc(loaded, 16)
                src = B2.rearrange("(o e) d -> o e d", o=1).to_broadcast([P, E, D])
                sp.dma_start(b2[:], src).then_inc(loaded, 16)
                sp.wait_ge(loaded, 32)

        with nc.Fori(0, m.passes) as it:
            names = ([f"w_in{i}" for i in range(2)] + [f"x_in{i}" for i in range(NX)] +
                     [f"y_out{i}" for i in range(NX)] +
                     ["turned", "xT_ready", "hidden_full", "hidden_ready", "y_full", "y_ready", "y_rect"])
            with phase(nc, *names) as (block, *sems):
                w_in, x_in, y_out = sems[0:2], sems[2:2 + NX], sems[2 + NX:2 + 2 * NX]
                turned, xT_ready, hidden_full, hidden_ready, y_full, y_ready, y_rect = sems[2 + 2 * NX:]

                @block.sync
                def _(sp):
                    def load_x(i):
                        row = sp.value_load(t.table[0:1, 1, bass.ds(it * m.per + i, 1)], min_val=0, max_val=m.rows - P)
                        if i >= NX:
                            sp.wait_ge(turned, i - NX + 1)
                        sp.dma_start(xr[:, i % NX, :], t.x_rows[layer][bass.ds(row, P), :]).then_inc(x_in[i % NX], 16)

                    def load_w(i):
                        e = sp.value_load(t.table[0:1, 0, bass.ds(it * m.per + i, 1)], min_val=0, max_val=E - 1)
                        need = sp.value_load(t.table[0:1, 2, bass.ds(it * m.per + i, 1)], min_val=0, max_val=1)
                        if i >= 2:
                            sp.wait_ge(y_full, i - 1)
                        src1 = W1[bass.ds(e, 1)].rearrange("o (dt d) f -> d (o dt) f", d=P)
                        sp.dma_start(w1[:, i % 2], src1, cond=need).then_inc(w_in[i % 2], 16)
                        src2 = W2[bass.ds(e, 1)].rearrange("o (ft f) d -> f (o ft) d", f=FP)
                        sp.dma_start(w2[:, i % 2], src2, cond=need).then_inc(w_in[i % 2], 16)

                    load_x(0)
                    load_w(0)
                    load_x(1)
                    load_w(1)
                    for i in range(2, m.per):
                        load_x(i)
                        load_w(i)

                @block.tensor
                def _(pe):
                    def turn(i):
                        pe.wait_ge(x_in[i % NX], 16 * (i // NX + 1))
                        if i >= 2:
                            pe.wait_ge(xT_ready, i - 1)
                        for dt in range(DT):
                            mm = pe.transpose(psX[:, i % 2, dt * P:(dt + 1) * P], xr[:, i % NX, dt * P:(dt + 1) * P],
                                              t.ident[:])
                        mm.then_inc(turned, 1)

                    def up(i):
                        pe.wait_ge(w_in[i % 2], 32 * (i // 2 + 1))
                        pe.wait_ge(xT_ready, i + 1)
                        for ft in range(FT):
                            if i >= 2 and ft % HB == 0:
                                pe.wait_ge(hidden_ready, FT * (i - 2) + min(ft + HB, FT))
                            for dt in range(DT):
                                mm = pe.matmul(psH[:, i % 2, ft * P:ft * P + P], w1[:, i % 2, dt, ft * P:ft * P + FP],
                                               xT[:, i % 2, dt, :], start=(dt == 0), stop=(dt == DT - 1))
                            if ft % HB == HB - 1 or ft == FT - 1:
                                mm.then_inc(hidden_full, 1)

                    def down(i):
                        if i >= 2:
                            pe.wait_ge(y_ready, i - 1)
                        for ft in range(FT):
                            pe.wait_ge(hidden_ready, FT * i + ft + 1)
                            mm = pe.matmul(psY[:, i % 2, 0:D], hT[:, i % 2, ft, :], w2[:, i % 2, ft, :],
                                           start=(ft == 0), stop=(ft == FT - 1))
                        mm.then_inc(y_full, 1)

                    turn(0)
                    for i in range(m.per):
                        up(i)
                        if i + 1 < m.per:
                            turn(i + 1)
                        down(i)

                @block.scalar
                def _(act):
                    for i in range(m.per):
                        e = act.value_load(t.table[0:1, 0, bass.ds(it * m.per + i, 1)], min_val=0, max_val=E - 1)
                        for ft in range(FT):
                            if ft % HB == 0:
                                act.wait_ge(hidden_full, HBANKS * i + ft // HB + 1)
                            if i >= 2:
                                act.wait_ge(y_full, i - 1)
                            act.activation(hT[:, i % 2, ft, :], psH[:, i % 2, ft * P:(ft + 1) * P],
                                           ACT.Relu if layer else ACT.Gelu_apprx_tanh,
                                           bias=b1[:, bass.ds(e * FT + ft, 1)]).then_inc(hidden_ready, 1)

                @block.vector
                def _(dve):
                    def move(i):
                        dve.wait_ge(turned, i + 1)
                        if i >= 2:
                            dve.wait_ge(hidden_full, HBANKS * (i - 1))
                        dve.tensor_copy(xT[:, i % 2], psX[:, i % 2, 0:DT * P].rearrange("p (a b) -> p a b", a=DT)
                                        ).then_inc(xT_ready, 1)

                    move(0)
                    for i in range(m.per):
                        e = dve.value_load(t.table[0:1, 0, bass.ds(it * m.per + i, 1)], min_val=0, max_val=E - 1)
                        if i + 1 < m.per:
                            move(i + 1)
                        dve.wait_ge(y_full, i + 1)
                        if i >= NX:
                            dve.wait_ge(y_out[i % NX], 16 * (i // NX))
                        bias = b2[:, bass.ds(e, 1), :].rearrange("p o d -> p (o d)")
                        dve.tensor_tensor(y[:, i % NX, :], psY[:, i % 2, 0:D], bias, ALU.add).then_inc(y_ready, 1)
                        if layer:
                            dve.wait_ge(y_ready, i + 1)
                            dve.tensor_scalar(y[:, i % NX, :], y[:, i % NX, :], 0.0, None, ALU.max).then_inc(y_rect, 1)

                @block.gpsimd
                def _(pool):
                    for i in range(m.per):
                        pool.wait_ge(y_rect if layer else y_ready, i + 1)
                        pool.dma_start(t.y_rows[layer][bass.ds((it * m.per + i) * P, P), :], y[:, i % NX, :]).then_inc(y_out[i % NX], 16)
                    for s in range(NX):
                        pool.wait_ge(y_out[s], 16 * (m.per // NX))


def combine(nc, t, a, layer, m, out):
    K = m.top
    with ExitStack() as own:
        sb, ps = buffers(nc, own, f"combine{layer}")
        rows = sb("y_rows", [P, K, LT, D])
        idx = sb("row_idx", [P, K, LT], I32)
        rowf, shift = sb("row_f", [P, K, LT]), sb("shift", [P, K, LT])
        hot = sb("one_hot", [P, K * LT, m.E])
        wts = sb("weights_of_tile", [P, K, LT])
        res = sb("result", [P, LT, D])
        with nc.Fori(0, B) as b, nc.Fori(0, 2) as th:
            with phase(nc, "idx_ready", "wts_ready", "rows_in", "chain", "stored") as (
                    block, idx_ready, wts_ready, rows_in, chain_sem, stored):
                tiles = bass.ds(b * KT + th * LT, LT)

                @block.vector
                def _(dve):
                    chain = Chain(dve, chain_sem)
                    by_e = lambda ap: ap.rearrange("p (o e) -> p o e", o=1).to_broadcast([P, LT, m.E])
                    for k in range(K):
                        mine = t.expert_of[:, k, tiles].rearrange("p (j o) -> p j o", o=1).to_broadcast([P, LT, m.E])
                        chain(dve.tensor_tensor(hot[:, k * LT:(k + 1) * LT, :], by_e(t.iota_e[:, 0:m.E]), mine,
                                                ALU.is_equal))
                        chain(dve.tensor_tensor(hot[:, k * LT:(k + 1) * LT, :], hot[:, k * LT:(k + 1) * LT, :],
                                                by_e(t.shift[:, 0:m.E]), ALU.mult))
                        chain(dve.tensor_reduce(shift[:, k, :], hot[:, k * LT:(k + 1) * LT, :], AX, ALU.add))
                    chain(dve.tensor_tensor(rowf[:], t.row_of[:, 0:K, tiles], shift[:], ALU.subtract))
                    dve.tensor_copy(idx[:], rowf[:]).then_inc(idx_ready, 1)
                    if K == 2:
                        chain(dve.tensor_copy(wts[:], t.weight[:, :, tiles]))
                    dve.wait_ge(rows_in, 16 * K * LT)
                    if K == 2:
                        for k in range(K):
                            for j in range(LT):
                                hh = t.h[:, bass.ds(b * KT + th * LT + j, 1), :].rearrange("p o d -> p (o d)")
                                src = hh if k == 0 else res[:, j, :]
                                dst = res[:, j, :] if k == 0 else hh
                                dve.scalar_tensor_tensor(out=dst, in0=rows[:, k, j, :], scalar=wts[:, k, j:j + 1],
                                                         in1=src, op0=ALU.mult, op1=ALU.add).then_inc(chain.sem, 1)
                                chain.n += 1
                            dve.wait_ge(chain.sem, chain.n)
                    else:
                        chain(dve.tensor_tensor(res[:], rows[:, 0], t.h[:, tiles, :], ALU.add))

                @block.gpsimd
                def _(pool):
                    pool.wait_ge(idx_ready, 1)
                    for k in range(K):
                        for j in range(LT):
                            off = bass.IndirectOffsetOnAxis(ap=idx[:, k, j:j + 1], axis=0)
                            pool.indirect_dma_start(rows[:, k, j, :], None, t.y_rows[layer], off).then_inc(rows_in, 16)
                    pool.wait_ge(rows_in, 16 * K * LT)

                if layer:
                    @block.sync
                    def _(sp):
                        sp.wait_ge(chain_sem, 3 * K + 2)
                        dst = out.rearrange("b (k p) d -> (b k) p d", p=P)[tiles].rearrange("k p d -> p k d")
                        sp.dma_start(dst, res[:]).then_inc(stored, 16)
                        sp.wait_ge(stored, 16)


def build(nc, a, out, upto=99):
    with ExitStack() as ctx:
        t = Tensors()
        dram = lambda n, s, d=F32: nc.dram_tensor(n, s, d).ap()
        t.qk_dram = dram("qk_parts", [B, 2, 3, HEADS, HD, S], BF16)
        t.v_dram = dram("v_rows", [B * KT, P, HEADS * 32])
        t.attn_dram = dram("attn_rows", [B * HEADS, S * HD // D, D])
        t.x_rows = [dram(f"x_rows{l}", [m.rows, D]) for l, m in enumerate((MOE0, MOE1))]
        t.y_rows = [dram(f"y_rows{l}", [m.NT * P, D]) for l, m in enumerate((MOE0, MOE1))]
        sb = lambda n, s, d=F32: ctx.enter_context(nc.sbuf_tensor(n, s, d))
        t.table = sb("tile_table", [1, 3, max(MOE0.NT, MOE1.NT)], I32)
        t.row_of = sb("row_of", [P, 2, TILES])
        t.weight = sb("weight", [P, 2, TILES])
        t.expert_of = sb("expert_of", [P, 2, TILES])
        t.shift = sb("region_shift", [P, MOE1.E])
        t.iota_e = sb("iota_e", [P, MOE1.E])
        setup(nc, ctx, t, a)
        steps = [lambda: embed(nc, t, a),
                 lambda: project(nc, t, a, 0), lambda: attention(nc, t, a, 0),
                 lambda: route(nc, t, a, 0, MOE0), lambda: experts(nc, t, a, 0, MOE0),
                 lambda: combine(nc, t, a, 0, MOE0, out),
                 lambda: project(nc, t, a, 1), lambda: (attention(nc, t, a, 1), add_attention(nc, t)),
                 lambda: route(nc, t, a, 1, MOE1), lambda: experts(nc, t, a, 1, MOE1),
                 lambda: combine(nc, t, a, 1, MOE1, out)]
        for s in steps[:upto]:
            s()
        if upto < len(steps):
            with phase(nc, "stored") as (block, stored):
                @block.sync
                def _(sp):
                    sp.dma_start(out.rearrange("b (k p) d -> p (b k) d", p=P), t.h[:]).then_inc(stored, 16)
                    sp.wait_ge(stored, 16)


def constants():
    f = np.float32
    p, k, q = np.arange(P), np.arange(KT), np.arange(S)
    freq = (10000.0 ** (-np.arange(0, HD, 2) / HD)).astype(f)
    angle = q.astype(f)[None, :] * freq[p % FREQ][:, None]
    ident = np.eye(P, dtype=f)
    den_row = (p[:, None] == 32 * (p[None, :] // 32) + HD).astype(f)
    key_rows = np.concatenate([np.ones((ROW_MAX, S), f)] + [(q[None, :] // P == k[:, None]).astype(f)] * 3)
    above = (q[None, :] < P * k[:, None] - 64).astype(f)
    below = (q[None, :] >= P * k[:, None] - 64 + BAND).astype(f)
    return {"c_ident": ident, "c_den_row": den_row, "c_cos": np.cos(angle), "c_sin": np.sin(angle),
            "c_key_rows": key_rows, "c_above": above, "c_below": below}


def kernel(**inputs):
    from concourse import bacc
    from concourse.bass_utils import run_bass_kernel_spmd

    nc = bacc.Bacc("TRN2", target_bir_lowering=False, num_devices=1)
    arrays, a = {}, {}
    for name, value in [*inputs.items(), *constants().items()]:
        value = np.ascontiguousarray(value)
        arrays[name] = value
        a[name] = nc.dram_tensor(name, value.shape, mybir.dt.from_np(value.dtype), kind="ExternalInput").ap()
    out = nc.dram_tensor("out", [B, S, D], F32, kind="ExternalOutput").ap()
    build(nc, a, out)
    r = run_bass_kernel_spmd(nc, [arrays], core_ids=[0])
    return r.results[0]["out"]
```

```python
from contextlib import ExitStack, contextmanager

import numpy as np

import concourse.bass as bass
from concourse import mybir

F32 = mybir.dt.float32
F32R = mybir.dt.float32r
BF16 = mybir.dt.bfloat16
I32 = mybir.dt.int32
ALU = mybir.AluOpType
ACT = mybir.ActivationFunctionType
AX = mybir.AxisListType.X

P = 128
B, S, D = 4, 1024, 256
TILES = B * S // P
DT = D // P
HEADS, HD = 16, 16
FREQ = HD // 2
GH = 4
UNITS = B * 2
UH = HEADS // 2
KT = S // P
LT = 4
EPS = 1e-5
NEG = -1e30
PARTS_Q = (0, 0, 1, 0, 1, 2)
PARTS_K = (0, 1, 0, 2, 1, 0)
PROD = len(PARTS_Q) * HD
LATEST = (0.75, 0.9)
ROW_MAX = 2
TB = 125
REACH = TB // 2
BAND = P + 2 * 64
BIAS_ROWS = 3 * KT
STRIP = 2 * S - P


@contextmanager
def phase(nc, *names):
    with ExitStack() as held:
        sems = [held.enter_context(nc.semaphore(n)) for n in names]
        with nc.Block() as block:
            yield (block, *sems)
        numbers = sorted(s.num for s in sems)
        first = 0
        for i in range(len(numbers)):
            if i + 1 == len(numbers) or numbers[i + 1] != numbers[i] + 1:
                used = range(numbers[first], numbers[i] + 1)
                nc.gpsimd.dma_reset(used)
                nc.gpsimd.sem_clear(used)
                first = i + 1
        nc.all_engine_barrier()


def buffers(nc, held, tag):
    return (lambda n, s, d=F32: held.enter_context(nc.sbuf_tensor(f"{tag}_{n}", s, d)),
            lambda n, s: held.enter_context(nc.psum_tensor(f"{tag}_ps_{n}", s, F32)))


class Tensors:
    pass


class Chain:

    def __init__(self, eng, sem):
        self.eng, self.sem, self.n = eng, sem, 0

    def __call__(self, ins):
        ins.then_inc(self.sem, 1)
        self.n += 1
        self.eng.wait_ge(self.sem, self.n)


class Expert:

    def __init__(self, experts, top, hidden):
        self.E, self.top, self.F = experts, top, hidden
        self.FT = max(1, hidden // P)
        self.FP = min(P, hidden)
        self.cap = B * S + P
        self.tiles = B * S * top // P + experts - 1
        self.per = 8
        self.passes = -(-self.tiles // self.per)
        self.NT = self.passes * self.per
        self.zero_row = experts * self.cap
        self.rows = self.zero_row + P


MOE0, MOE1 = Expert(8, 2, 1024), Expert(32, 1, 64)


def setup(nc, ctx, t, a):
    sb, ps = buffers(nc, ctx, "all")
    t.h = sb("h", [P, TILES, D])
    t.ident = sb("ident", [P, P])
    t.ident_bf = sb("ident_bf", [P, P], BF16)
    t.ident_r = sb("ident_r", [P, P], F32R)
    t.ones_bf = sb("ones_bf", [P, P], BF16)
    t.before = sb("before", [P, P], BF16)
    t.den_row = sb("den_row", [P, P])
    t.wqT = [sb(f"wqT{l}", [P, DT, D]) for l in range(2)]
    t.wkT = [sb(f"wkT{l}", [P, DT, D]) for l in range(2)]
    t.wvT = [sb(f"wvT{l}", [P, DT, D]) for l in range(2)]
    t.woP = [sb(f"woP{l}", [P, HEADS // GH, D]) for l in range(2)]
    t.bqk = sb("bqk", [P, 2, 2])
    t.bv = sb("bv", [P, D])
    t.bo = sb("bo", [P, D])
    w = {0: "L0_attn_", 1: "L1_attn_"}
    with ExitStack() as own:
        tmp_sb, tmp_ps = buffers(nc, own, "setup")
        nat = tmp_sb("w_nat", [P, 8, 2, D])
        woT = tmp_sb("woT", [P, 2, DT, D])
        ps = tmp_ps("w", [P, 8, 512])
        with phase(nc, "consts_in", "w_in", "made", "turned", "moved", "placed", "zeroed", "small_in") as (
                block, consts_in, w_in, made, turned, moved, placed, zeroed, small_in):

            @block.sync
            def _(sp):
                sp.dma_start(t.ident[:], a["c_ident"]).then_inc(consts_in, 16)
                sp.dma_start(t.den_row[:], a["c_den_row"]).then_inc(consts_in, 16)
                for l in range(2):
                    for m, n in enumerate(("Wq", "Wk")):
                        src = a[w[l] + n].rearrange("(hi par) d -> hi par d", par=2)
                        sp.dma_start(nat[:, 4 * l + m, :, :], src).then_inc(w_in, 16)
                    for m, n in enumerate(("Wv", "Wo")):
                        src = a[w[l] + n].rearrange("(et e) d -> e et d", e=P)
                        sp.dma_start(nat[:, 4 * l + 2 + m, :, :], src).then_inc(w_in, 16)
                with nc.allow_non_contiguous_dma(reason="biases of one value per partition"):
                    for m, n in enumerate(("bq", "bk")):
                        src = a["L1_attn_" + n].rearrange("(hi par) -> hi par", par=2)
                        sp.dma_start(t.bqk[:, m, :], src).then_inc(small_in, 16)
                for dst, n in ((t.bv, "bv"), (t.bo, "bo")):
                    src = a["L1_attn_" + n].rearrange("(o d) -> o d", o=1).to_broadcast([P, D])
                    sp.dma_start(dst[:], src).then_inc(small_in, 16)
                sp.wait_ge(zeroed, 2)
                sp.wait_ge(moved, 8)
                for l in range(2):
                    for g in range(HEADS // GH):
                        for j in range(GH):
                            d0 = (GH * g + j) * HD
                            row, slot = (j, g) if l == 0 else (g, j)
                            sp.dma_start(t.woP[l][32 * row:32 * row + HD, slot, :],
                                         woT[d0 % P:d0 % P + HD, l, d0 // P, :]).then_inc(placed, 16)
                sp.wait_ge(placed, 16 * 2 * HEADS)
                sp.wait_ge(small_in, 64)

            @block.gpsimd
            def _(pool):
                for l in range(2):
                    pool.memset(t.woP[l][:], 0.0).then_inc(zeroed, 1)
                pool.memset(t.ones_bf[:], 1.0)
                pool.memset(t.before[:], 1.0).then_inc(made, 1)
                pool.wait_ge(made, 1)
                pool.affine_select(out=t.before[:], in_=t.before[:], compare_op=ALU.is_gt, fill=0.0,
                                   base=0, pattern=[[1, P]], channel_multiplier=-1)

            @block.tensor
            def _(pe):
                pe.wait_ge(consts_in, 32)
                pe.wait_ge(w_in, 128)
                for m in range(8):
                    for dt in range(DT):
                        for et in range(2):
                            at = dt * D + et * P
                            mm = pe.transpose(ps[:, m, at:at + P], nat[:, m, et, dt * P:(dt + 1) * P], t.ident[:])
                    mm.then_inc(turned, 1)

            @block.vector
            def _(dve):
                dve.wait_ge(consts_in, 32)
                dve.tensor_copy(t.ident_bf[:], t.ident[:])
                dve.tensor_copy(t.ident_r[:], t.ident[:])
                for m in range(8):
                    l = m // 4
                    dst = (t.wqT[l], t.wkT[l], t.wvT[l], None)[m % 4]
                    dst = woT[:, l] if dst is None else dst[:]
                    dve.wait_ge(turned, m + 1)
                    dve.tensor_copy(dst.rearrange("p a b -> p (a b)"), ps[:, m, :]).then_inc(moved, 1)


def embed(nc, t, a):
    R = 16
    with ExitStack() as own:
        sb, ps = buffers(nc, own, "embed")
        ids = sb("ids", [P, KT], I32)
        base = sb("emb_rows", [P, KT, D])
        la = sb("lora_rows", [P, KT, R])
        laT = sb("lora_rowsT", [R, KT, P])
        lb = sb("lora_b", [R, D])
        psT = ps("loraT", [R, KT, P])
        psD = ps("delta", [P, KT, D])
        x = a["x"].rearrange("b (t p) -> b p t", p=P)
        with nc.Fori(0, B) as b:
            with phase(nc, "ids_in", "lb_in", "rows_in", "lora_in", "turned", "copied", "delta") as (
                    block, ids_in, lb_in, rows_in, lora_in, turned, copied, delta):

                @block.sync
                def _(sp):
                    with nc.allow_non_contiguous_dma(reason="token ids go one to a partition"):
                        sp.dma_start(ids[:], x[bass.ds(b, 1)].rearrange("o p t -> (o p) t")).then_inc(ids_in, 16)
                    sp.dma_start(lb[:], a["L0_tok_lora_b"]).then_inc(lb_in, 16)

                @block.gpsimd
                def _(pool):
                    pool.wait_ge(ids_in, 16)
                    for i in range(KT):
                        off = bass.IndirectOffsetOnAxis(ap=ids[:, i:i + 1], axis=0)
                        pool.indirect_dma_start(la[:, i, :], None, a["L0_tok_lora_a"], off).then_inc(lora_in, 16)
                    for i in range(KT):
                        off = bass.IndirectOffsetOnAxis(ap=ids[:, i:i + 1], axis=0)
                        pool.indirect_dma_start(base[:, i, :], None, a["L0_tok_weight"], off).then_inc(rows_in, 16)
                    pool.wait_ge(lora_in, 16 * KT)
                    pool.wait_ge(rows_in, 16 * KT)

                @block.tensor
                def _(pe):
                    pe.wait_ge(lora_in, 16 * KT)
                    for i in range(KT):
                        mm = pe.transpose(psT[:, i, :], la[:, i, :], t.ident[:])
                    mm.then_inc(turned, 1)
                    pe.wait_ge(copied, 1)
                    pe.wait_ge(lb_in, 16)
                    for i in range(KT):
                        mm = pe.matmul(psD[:, i, :], laT[:, i, :], lb[:], start=True, stop=True)
                    mm.then_inc(delta, 1)

                @block.vector
                def _(dve):
                    dve.wait_ge(turned, 1)
                    dve.tensor_copy(laT[:], psT[:]).then_inc(copied, 1)
                    dve.wait_ge(delta, 1)
                    dve.wait_ge(rows_in, 16 * KT)
                    dve.scalar_tensor_tensor(out=t.h[:, bass.ds(b * KT, KT), :], in0=psD[:], scalar=2.0, in1=base[:],
                                             op0=ALU.mult, op1=ALU.add)


def norm_vector(dve, chain, t, n, tile0, var_ready, root_ready, normed):
    for j in range(LT):
        dve.bn_stats(n.stats[:, j, :], t.h[:, bass.ds(tile0 + j, 1), :].rearrange("p o d -> p (o d)")
                     ).then_inc(chain.sem, 1)
        chain.n += 1
    dve.wait_ge(chain.sem, chain.n)
    for j in range(LT):
        dve.bn_aggr(n.mv[:, j, :], n.stats[:, j, :]).then_inc(chain.sem, 1)
        chain.n += 1
    dve.wait_ge(chain.sem, chain.n)
    dve.tensor_scalar(n.var[:], n.mv[:, :, 1], EPS, None, ALU.add).then_inc(var_ready, 1)
    dve.wait_ge(root_ready, 1)
    chain(dve.reciprocal(n.inv[:], n.root[:]))
    chain(dve.tensor_tensor(n.inv[:], n.var[:], n.inv[:], ALU.mult))
    chain(dve.tensor_tensor(n.inv[:], n.inv[:], n.root[:], ALU.add))
    chain(dve.tensor_scalar(n.inv[:], n.inv[:], 0.5, None, ALU.mult))
    chain(dve.reciprocal(n.inv[:], n.inv[:]))
    for j in range(LT):
        dve.tensor_scalar(n.xn[:, j, :], t.h[:, bass.ds(tile0 + j, 1), :].rearrange("p o d -> p (o d)"),
                          n.mv[:, j, 0:1], n.inv[:, j:j + 1], ALU.subtract, ALU.mult).then_inc(normed, 1)


def norm_root(act, n, var_ready, root_ready):
    act.wait_ge(var_ready, 1)
    act.activation(n.root[:], n.var[:], ACT.Sqrt).then_inc(root_ready, 1)


def norm_turn(pe, t, n, psT, normed, turned):
    for j in range(LT):
        pe.wait_ge(normed, j + 1)
        for dt in range(DT):
            mm = pe.transpose(psT[:, dt, j * P:(j + 1) * P], n.xn[:, j, dt * P:(dt + 1) * P], t.ident[:])
    mm.then_inc(turned, 1)


def norm_buffers(sb):
    n = Tensors()
    n.stats, n.mv, n.var = sb("stats", [P, LT, 6]), sb("mv", [P, LT, 2]), sb("var", [P, LT])
    n.root, n.inv = sb("root", [P, LT]), sb("inv", [P, LT])
    n.xn, n.xT = sb("xn", [P, LT, D]), sb("xT", [P, DT, LT * P])
    return n


def project(nc, t, a, layer):
    W = LT * P
    rope = layer == 0
    with ExitStack() as own:
        sb, ps = buffers(nc, own, f"proj{layer}")
        n = norm_buffers(sb)
        raw = sb("qk_raw", [P, 2, 2, W])
        rot = sb("qk_rot", [P, 2, 2, W]) if rope else raw
        m1, m2 = (sb(f"rope_m{i}", [P, 2, W]) for i in range(2))
        m3, m4 = (sb(f"rope_m{i}", [P, 2, W]) for i in range(2, 4))
        part = [sb(f"part{i}", [P, 2, 2, W], BF16) for i in range(3)]
        rest = sb("rest", [P, 2, 2, W])
        vst = sb("v_stage", [P, LT, HEADS, 32])
        if rope:
            cos, sin = sb("cos", [P, S]), sb("sin", [P, S])
        psT = ps("xT", [P, DT, W])
        psQ = ps("qk", [P, 2, 2, W])
        psV = ps("v", [P, LT, D])
        with phase(nc, "tables_in", "v_set") as (block, tables_in, v_set):

            @block.sync
            def _(sp):
                if rope:
                    sp.dma_start(cos[:], a["c_cos"]).then_inc(tables_in, 16)
                    sp.dma_start(sin[:], a["c_sin"]).then_inc(tables_in, 16)
                    sp.wait_ge(tables_in, 32)

            @block.gpsimd
            def _(pool):
                pool.memset(vst[:, :, :, HD:32], 0.0).then_inc(v_set, 1)
                pool.wait_ge(v_set, 1)
                pool.memset(vst[:, :, :, HD:HD + 1], 1.0)

            if not rope:
                @block.vector
                def _(dve):
                    dve.tensor_scalar(t.bqk[:, 0, :], t.bqk[:, 0, :], 0.25, None, ALU.mult)

        with nc.Fori(0, B) as b, nc.Fori(0, 2) as th:
            with phase(nc, "chain", "var_ready", "root_ready", "normed", "turned", "x_ready", "qk_ready", "v_ready",
                       "raw_ready", "v_staged", "pool_m", "rotated", "split1", "split2", "rest1", "split3",
                       "v_out", "qk_out") as (
                    block, chain_sem, var_ready, root_ready, normed, turned, x_ready, qk_ready, v_ready,
                    raw_ready, v_staged, pool_m, rotated, split1, split2, rest1, split3, v_out, qk_out):

                @block.tensor
                def _(pe):
                    norm_turn(pe, t, n, psT, normed, turned)
                    pe.wait_ge(x_ready, 1)
                    for m, wT in enumerate((t.wqT[layer], t.wkT[layer])):
                        for par in range(2):
                            for dt in range(DT):
                                mm = pe.matmul(psQ[:, m, par, :], wT[:, dt, par * P:(par + 1) * P], n.xT[:, dt, :],
                                               start=(dt == 0), stop=(dt == DT - 1))
                            mm.then_inc(qk_ready, 1)
                    for j in range(LT):
                        for dt in range(DT):
                            mm = pe.matmul(psV[:, j, :], n.xT[:, dt, j * P:(j + 1) * P], t.wvT[layer][:, dt, :],
                                           start=(dt == 0), stop=(dt == DT - 1))
                    mm.then_inc(v_ready, 1)

                @block.scalar
                def _(act):
                    norm_root(act, n, var_ready, root_ready)
                    for i in range(4):
                        m, par = i // 2, i % 2
                        act.wait_ge(qk_ready, i + 1)
                        bias = 0.0 if rope else t.bqk[:, m, par:par + 1]
                        act.activation(raw[:, m, par, :], psQ[:, m, par, :], ACT.Identity, bias=bias,
                                       scale=(0.25 if m == 0 else 1.0)).then_inc(raw_ready, 1)
                    act.wait_ge(v_ready, 1)
                    for j in range(LT):
                        act.activation(vst[:, j, :, 0:HD], psV[:, j, :].rearrange("p (h c) -> p h c", h=HEADS),
                                       ACT.Copy).then_inc(v_staged, 1)
                    if rope:
                        act.wait_ge(rotated, 2)
                    else:
                        act.wait_ge(raw_ready, 4)
                    act.activation(part[0][:], rot[:], ACT.Copy).then_inc(split1, 1)
                    act.wait_ge(rest1, 1)
                    act.activation(part[1][:], rest[:], ACT.Copy).then_inc(split2, 1)

                @block.vector
                def _(dve):
                    chain = Chain(dve, chain_sem)
                    norm_vector(dve, chain, t, n, b * KT + th * LT, var_ready, root_ready, normed)
                    dve.wait_ge(turned, 1)
                    dve.tensor_copy(n.xT[:], psT[:]).then_inc(x_ready, 1)
                    if rope:
                        at = bass.ds(th * W, W)
                        c = cos[:, at].rearrange("p (o w) -> p o w", o=1).to_broadcast([P, 2, W])
                        s = sin[:, at].rearrange("p (o w) -> p o w", o=1).to_broadcast([P, 2, W])
                        dve.wait_ge(raw_ready, 4)
                        dve.tensor_tensor(m1[:], raw[:, :, 0, :], c, ALU.mult).then_inc(chain.sem, 1)
                        dve.tensor_tensor(m2[:], raw[:, :, 1, :], s, ALU.mult).then_inc(chain.sem, 1)
                        chain.n += 2
                        dve.wait_ge(chain.sem, chain.n)
                        dve.tensor_tensor(rot[:, :, 0, :], m1[:], m2[:], ALU.subtract).then_inc(rotated, 1)
                    elif layer == 1:
                        dve.wait_ge(v_staged, LT)
                        for j in range(LT):
                            v = vst[:, j, :, 0:HD]
                            dve.tensor_tensor(v, v, t.bv[:].rearrange("p (h c) -> p h c", h=HEADS),
                                              ALU.add).then_inc(v_staged, 1)
                    dve.wait_ge(split1, 1)
                    if rope:
                        dve.wait_ge(rotated, 2)
                    dve.tensor_tensor(rest[:], rot[:], part[0][:], ALU.subtract).then_inc(rest1, 1)
                    dve.wait_ge(split2, 1)
                    dve.wait_ge(rest1, 1)
                    dve.tensor_tensor(part[2][:], rest[:], part[1][:], ALU.subtract).then_inc(split3, 1)

                @block.gpsimd
                def _(pool):
                    if rope:
                        at = bass.ds(th * W, W)
                        c = cos[:, at].rearrange("p (o w) -> p o w", o=1).to_broadcast([P, 2, W])
                        s = sin[:, at].rearrange("p (o w) -> p o w", o=1).to_broadcast([P, 2, W])
                        pool.wait_ge(raw_ready, 4)
                        pool.tensor_tensor(m3[:], raw[:, :, 0, :], s, ALU.mult).then_inc(pool_m, 1)
                        pool.tensor_tensor(m4[:], raw[:, :, 1, :], c, ALU.mult).then_inc(pool_m, 1)
                        pool.wait_ge(pool_m, 2)
                        pool.tensor_tensor(rot[:, :, 1, :], m3[:], m4[:], ALU.add).then_inc(rotated, 1)

                @block.sync
                def _(sp):
                    sp.wait_ge(v_staged, LT if rope else 2 * LT)
                    dst = t.v_dram[bass.ds(b * KT + th * LT, LT)].rearrange("j p c -> p j c")
                    sp.dma_start(dst, vst[:].rearrange("p j h c -> p j (h c)")).then_inc(v_out, 16)
                    for s, ready in enumerate((split1, split2, split3)):
                        sp.wait_ge(ready, 1)
                        for m in range(2):
                            for par in range(2):
                                dst = t.qk_dram[bass.ds(b, 1), m, s, :, par * FREQ:(par + 1) * FREQ,
                                                bass.ds(th * W, W)]
                                sp.dma_start(dst.rearrange("o h i w -> (o h) i w"),
                                             part[s][:, m, par, :]).then_inc(qk_out, 16)
                    sp.wait_ge(qk_out, 16 * 12)
                    sp.wait_ge(v_out, 16)


def bias_tables(nc, own, t, a):
    sb, ps = buffers(nc, own, "bias")
    t.strip = sb("bias_strip", [P, STRIP])
    t.band = [sb(f"band{i}", [P, BAND], F32R) for i in range(2)]
    LS = STRIP + P - 1
    strip_dram = nc.dram_tensor("strip_rows", [P, LS], F32).ap()
    row_dram = nc.dram_tensor("strip_row", [1, LS], F32).ap()
    t.far_dram = nc.dram_tensor("bias_far", [BIAS_ROWS, S], BF16).ap()
    with ExitStack() as tmp:
        tb_, tp_ = buffers(nc, tmp, "bias_tmp")
        g = tb_("gates", [1, 4])
        tbf = tb_("time_bias", [1, TB])
        srow = tb_("strip_row_sb", [1, LS])
        vcol = tb_("bias_vals_col", [KT, 2])
        above, below = tb_("above", [KT, S]), tb_("below", [KT, S])
        far, rest = tb_("far", [KT, S]), tb_("far_rest", [KT, S])
        fp = [tb_(f"far_part{i}", [KT, S], BF16) for i in range(3)]
        bandf = tp_("band", [P, BAND])
        with phase(nc, "inputs", "sig", "chain", "row_ready", "row_out", "sheared", "strip_in", "col_in",
                   "parts_ready", "parts_out", "masks_in", "band_ready") as (
                block, inputs, sig, chain_sem, row_ready, row_out, sheared, strip_in, col_in,
                parts_ready, parts_out, masks_in, band_ready):

            @block.sync
            def _(sp):
                tbd = a["L1_attn_time_bias"].rearrange("a b n -> (a b) n")
                sp.dma_start(g[:, 0:1], a["L1_attn_et_gate"].rearrange("a b n -> (a b) n")).then_inc(inputs, 16)
                sp.dma_start(g[:, 1:2], a["L1_attn_is_gate"].rearrange("a b n -> (a b) n")).then_inc(inputs, 16)
                sp.dma_start(tbf[:], tbd).then_inc(inputs, 16)
                sp.dma_start(above[:], a["c_above"]).then_inc(masks_in, 16)
                sp.dma_start(below[:], a["c_below"]).then_inc(masks_in, 16)
                sp.wait_ge(row_ready, 1)
                sp.dma_start(row_dram, srow[:]).then_inc(row_out, 16)
                sp.wait_ge(row_out, 16)
                sp.dma_start(strip_dram, row_dram.to_broadcast([P, LS])).then_inc(sheared, 16)
                for i, x in enumerate((LS - 1, 0)):
                    sp.dma_start(vcol[:, i:i + 1], row_dram[:, x:x + 1].to_broadcast([KT, 1])).then_inc(col_in, 16)
                sp.wait_ge(sheared, 16)
                sp.dma_start(t.strip[:], bass.AP(tensor=strip_dram.tensor, offset=P - 1, ap=[[LS - 1, P], [1, STRIP]])
                             ).then_inc(strip_in, 16)
                sp.wait_ge(parts_ready, 3)
                for s in range(3):
                    sp.dma_start(t.far_dram[s * KT:(s + 1) * KT, :], fp[s][:]).then_inc(parts_out, 16)
                sp.wait_ge(parts_out, 48)

            @block.tensor
            def _(pe):
                pe.wait_ge(strip_in, 16)
                for c in range(2):
                    x = S - P + 64 - c * P
                    mm = pe.transpose(bandf[:, c * P:(c + 1) * P], t.strip[:, x:x + P], t.ident[:])
                mm.then_inc(band_ready, 1)

            @block.scalar
            def _(act):
                act.wait_ge(inputs, 48)
                act.activation(g[:, 2:3], g[:, 0:1], ACT.Exp, scale=-1.0).then_inc(sig, 1)

            @block.vector
            def _(dve):
                chain = Chain(dve, chain_sem)
                dve.wait_ge(sig, 1)
                chain(dve.tensor_scalar(g[:, 2:3], g[:, 2:3], 1.0, None, ALU.add))
                chain(dve.reciprocal(g[:, 3:4], g[:, 2:3]))
                chain(dve.tensor_scalar(tbf[:], tbf[:], g[:, 3:4], None, ALU.mult))
                first = S - 1 - REACH
                chain(dve.memset(srow[:], 0.0))
                chain(dve.tensor_scalar(srow[:, 0:first], srow[:, 0:first], tbf[:, 0:1], g[:, 1:2], ALU.add, ALU.add))
                chain(dve.tensor_scalar(srow[:, first:first + TB], tbf[:], g[:, 1:2], None, ALU.add))
                dve.tensor_scalar(srow[:, first + TB:], srow[:, first + TB:], tbf[:, TB - 1:TB], g[:, 1:2],
                                  ALU.add, ALU.add).then_inc(row_ready, 1)
                dve.wait_ge(band_ready, 1)
                chain(dve.tensor_copy(t.band[0][:], bandf[:]))
                chain(dve.tensor_tensor(t.band[1][:], bandf[:], t.band[0][:].bitcast(F32), ALU.subtract))
                dve.wait_ge(col_in, 32)
                dve.wait_ge(masks_in, 32)
                chain(dve.tensor_scalar(far[:], above[:], vcol[:, 0:1], None, ALU.mult))
                chain(dve.tensor_scalar(rest[:], below[:], vcol[:, 1:2], None, ALU.mult))
                chain(dve.tensor_tensor(far[:], far[:], rest[:], ALU.add))
                chain(dve.tensor_copy(fp[0][:], far[:]))
                chain(dve.tensor_tensor(rest[:], far[:], fp[0][:], ALU.subtract))
                chain(dve.tensor_copy(fp[1][:], rest[:]))
                dve.tensor_tensor(fp[2][:], rest[:], fp[1][:], ALU.subtract).then_inc(parts_ready, 3)


def attention(nc, t, a, layer):
    causal = layer == 0
    KS = PROD + ROW_MAX + (0 if causal else BIAS_ROWS)
    G = HEADS // GH
    with ExitStack() as own:
        sb, ps = buffers(nc, own, f"attn{layer}")
        if causal:
            t.strip = sb("mask_strip", [P, STRIP])
            maskT = sb("maskT", [P, P], BF16)
        else:
            bias_tables(nc, own, t, a)
        qst = [sb(f"q_rows{g}", [P, GH, S], BF16) for g in range(G)]
        kst = [sb(f"k_rows{g}", [P, GH, S], BF16) for g in range(G)]
        v = sb("v", [P, 2, KT, GH * 32])
        prob = sb("prob", [P, 2 * GH, S])
        junk = sb("junk", [P, 4, 512], BF16)
        mx = sb("mx", [P, 2, 2, GH * KT])
        negm = sb("negm", [P, 2, 2, GH * KT], BF16)
        negmT = sb("negmT", [2 * GH * KT, 2, P], BF16)
        oT = sb("oT", [P, 2, S])
        rsum = sb("one_over_sums", [P, S])
        fold = sb("sums_folded", [P, S // 32])
        on = sb("on", [P, 2, S])
        dens = sb("den_partitions", [P, 1])
        stage = None if causal else sb("out_stage", [P, 4, D])
        psS = ps("scores", [P, 2, S])
        acc = ps("out", [P, S])
        aux = ps("aux", [P, 2, 512])
        with phase(nc, "filled", "far_in", "dens_ready", "chain") as (block, filled, far_in, dens_ready, chain_sem):

            @block.gpsimd
            def _(pool):
                chain = Chain(pool, chain_sem)
                if causal:
                    chain(pool.memset(t.strip[:], 0.0))
                    chain(pool.affine_select(out=t.strip[:], in_=t.strip[:], compare_op=ALU.is_ge, fill=NEG,
                                             base=S - P, pattern=[[-1, STRIP]], channel_multiplier=1))
                    chain(pool.memset(maskT[:], 0.0))
                    chain(pool.affine_select(out=maskT[:], in_=maskT[:], compare_op=ALU.is_ge, fill=NEG,
                                             base=0, pattern=[[1, P]], channel_multiplier=-1))
                chain(pool.memset(mx[:], NEG))
                for g in range(G):
                    for j in range(GH):
                        pool.dma_start(kst[g][PROD:KS, j, :], a["c_key_rows"][0:KS - PROD, :]).then_inc(filled, 16)
                pool.wait_ge(filled, 16 * G * GH)

            @block.vector
            def _(dve):
                chain = Chain(dve, dens_ready)
                chain(dve.memset(on[:], 0.0))
                chain(dve.memset(rsum[:], 0.0))
                chain(dve.memset(oT[:], 1.0))
                chain(dve.tensor_reduce(dens[:], t.den_row[:].rearrange("p (j c) -> p c j", j=GH)[:, 0, :], AX, ALU.add))
                dve.tensor_scalar(oT[:, 1, :], oT[:, 1, :], dens[:], None, ALU.mult)

            if not causal:
                @block.sync
                def _(sp):
                    for g in range(G):
                        for j in range(GH):
                            sp.dma_start(qst[g][PROD + ROW_MAX:KS, j, :], t.far_dram).then_inc(far_in, 16)
                    sp.wait_ge(far_in, 16 * G * GH)

        jobs = []
        for j in range(GH):
            for qt in range(KT):
                end = (qt + 1) * P if causal else S
                for kh in range(2):
                    n = min(end - 512 * kh, 512)
                    if n > 0:
                        jobs.append((j, qt, kh, n))
        NJ = len(jobs)
        live = lambda kt: (kt * P if causal else 0)
        last_kt = lambda qh: (3 if causal and qh == 0 else KT - 1)
        halves = lambda kt: [qh for qh in range(2) if live(kt) < 512 * (qh + 1)]

        def load_qk(sp, b, g, sem):
            for m, (dst, parts) in enumerate(((qst[g], PARTS_Q), (kst[g], PARTS_K))):
                for c, s in enumerate(parts):
                    src = t.qk_dram[bass.ds(b, 1), m, s, g * GH:(g + 1) * GH]
                    sp.dma_start(dst[c * HD:(c + 1) * HD, :, :],
                                 src.rearrange("o h i w -> i (o h) w")).then_inc(sem, 16)
        QK_IN = 16 * 2 * len(PARTS_Q)

        def load_v(sp, b, g, sem):
            src = t.v_dram[bass.ds(b * KT, KT), :, g * GH * 32:(g + 1) * GH * 32]
            sp.dma_start(v[:, g % 2], src.rearrange("k p c -> p k c")).then_inc(sem, 16)

        def store_max(sp, g, sem):
            n = GH * KT
            for s in range(ROW_MAX):
                sp.dma_start(qst[g][PROD + s:PROD + s + 1, :, :].rearrange("p j (q w) -> p (j q) w", w=P),
                             negmT[s * n:(s + 1) * n, g % 2, :]).then_inc(sem, 16)
        MAX_IN = 16 * ROW_MAX

        def pe_max(pe, g, i, bank):
            j, qt, kh, w = jobs[i]
            return pe.matmul(bank[:, 0:w], qst[g][0:PROD, j, qt * P:(qt + 1) * P],
                             kst[g][0:PROD, j, kh * 512:kh * 512 + w], start=True, stop=True)

        def pe_turn(pe, g, bank):
            return pe.transpose(bank[0:2 * GH * KT, 0:P // 2].bitcast(BF16),
                                negm[:, g % 2, :, :].rearrange("p s n -> p (s n)"), t.ident_bf[:])

        def dve_max(dve, chain, g, i, bank, n, aux_free, negm_ready):
            j, qt, kh, w = jobs[i]
            at = S - P - P * qt + 512 * kh
            c = j * KT + qt
            if n >= 4:
                dve.wait_ge(aux_free, n - 3)
            dve.tensor_tensor_reduce(junk[:, n % 4, 0:w], bank[:, 0:w], t.strip[:, at:at + w], 1.0, NEG,
                                     ALU.add, ALU.max, mx[:, g % 2, kh, c:c + 1]).then_inc(aux_free, 1)
            if i == NJ - 1:
                dve.wait_ge(aux_free, n + 1)
                top = mx[:, g % 2, 0, :]
                chain(dve.tensor_tensor(top, top, mx[:, g % 2, 1, :], ALU.max))
                chain(dve.tensor_scalar(negm[:, g % 2, 0, :], top, -1.0, None, ALU.mult))
                dve.scalar_tensor_tensor(out=negm[:, g % 2, 1, :], in0=top, scalar=-1.0, in1=negm[:, g % 2, 0, :],
                                         op0=ALU.mult, op1=ALU.subtract).then_inc(negm_ready, 1)

        def dve_turn(dve, g, bank, aux_free):
            dve.tensor_copy(negmT[:, g % 2, :], bank[0:2 * GH * KT, 0:P // 2].bitcast(BF16)).then_inc(aux_free, 1)

        def fold_sums(pool, g, sem):
            pool.dma_start(fold[:], oT[HD:P:32, g % 2, :].rearrange("j (k q) -> j k q", k=32)).then_inc(sem, 16)

        def unfold_sums(pool, sem):
            pool.dma_start(rsum[HD:P:32, :].rearrange("j (k q) -> j k q", k=32), fold[:]).then_inc(sem, 16)

        def pe_sums(pe, i, bank):
            return pe.matmul(bank, t.den_row[:], rsum[:, i * 512:(i + 1) * 512], start=True, stop=True)

        def dve_sums(dve, g, i, bank, aux_free):
            cols = slice(i * 512, (i + 1) * 512)
            dve.tensor_tensor(on[:, g % 2, cols], oT[:, g % 2, cols], bank, ALU.mult).then_inc(aux_free, 1)

        def pe_out(pe, hg, i, bank):
            if causal:
                for k in range(2):
                    q = (2 * i + k) * P
                    for g in range(2):
                        mm = pe.matmul(bank[:, k * D:(k + 1) * D], on[:, g, q:q + P], t.woP[layer][:, 2 * hg + g, :],
                                       start=(g == 0), stop=(g == 1))
                return mm
            for k in range(2):
                j = 2 * (i % 2) + k
                for r in range(4):
                    lhs = on[:, i // 2, j * 256:(j + 1) * 256].rearrange("p (u r) -> p r u", r=4)[:, r]
                    mm = pe.matmul(bank[64 * k:64 * k + 64, 0:D], lhs, t.woP[layer][:, r, :],
                                   start=(r == 0), stop=(r == 3))
            return mm

        def dve_out(dve, b, i, bank, aux_free):
            if causal:
                hh = t.h[:, bass.ds(b * KT + 2 * i, 2), :].rearrange("p k d -> p (k d)")
                dve.tensor_tensor(hh, hh, bank, ALU.add).then_inc(aux_free, 1)
            else:
                dve.tensor_copy(stage[:, i, :], bank[:, 0:D]).then_inc(aux_free, 1)

        def store_rows(sp, b, hg, i, rows_out):
            for k in range(2):
                head = hg * UH + 2 * i + k
                sp.dma_start(t.attn_dram[bass.ds(head * B + b, 1)].rearrange("o p d -> (o p) d"),
                             stage[64 * k:64 * k + 64, i, :]).then_inc(rows_out, 16)

        early = int(NJ * (1 - LATEST[layer]))
        first_jobs = ([("max", 0, i) for i in range(NJ)] + [("turn", 0, 0)] + [("max", 1, i) for i in range(early)])
        with phase(nc, "qk0_in", "qk1_in", "v_in", "m_in", "aux_full", "aux_free", "negm_ready", "chain") as (
                block, qk0_in, qk1_in, v_in, m_in, aux_full, aux_free, negm_ready, chain_sem):

            @block.sync
            def _(sp):
                load_qk(sp, 0, 0, qk0_in)
                load_v(sp, 0, 0, v_in)
                load_qk(sp, 0, 1, qk1_in)
                sp.wait_ge(aux_free, NJ + 1)
                store_max(sp, 0, m_in)
                sp.wait_ge(m_in, MAX_IN)
                sp.wait_ge(v_in, 16)
                sp.wait_ge(qk1_in, QK_IN)

            @block.tensor
            def _(pe):
                pe.wait_ge(qk0_in, QK_IN)
                for n, (kind, g, i) in enumerate(first_jobs):
                    if n >= 2:
                        pe.wait_ge(aux_free, n - 1)
                    if kind == "turn":
                        pe.wait_ge(negm_ready, 1)
                        pe_turn(pe, 0, aux[:, n % 2, :]).then_inc(aux_full, 1)
                        continue
                    if g == 1 and i == 0:
                        pe.wait_ge(qk1_in, QK_IN)
                    pe_max(pe, g, i, aux[:, n % 2, :]).then_inc(aux_full, 1)

            @block.vector
            def _(dve):
                chain = Chain(dve, chain_sem)
                for n, (kind, g, i) in enumerate(first_jobs):
                    dve.wait_ge(aux_full, n + 1)
                    if kind == "max":
                        dve_max(dve, chain, g, i, aux[:, n % 2, :], n, aux_free, negm_ready)
                    else:
                        dve_turn(dve, 0, aux[:, n % 2, :], aux_free)

        pieces = []
        for g in range(G):
            for kt in range(KT):
                for j in range(GH):
                    pieces.append(("score", g, kt, j))
                    if j % 2 == 1:
                        pg, pk = (g, kt - 1) if kt else (g - 1, KT - 1)
                        if pg >= 0 and j // 2 in halves(pk):
                            pieces.append(("pv", pg, pk, j // 2))
        pieces += [("pv", G - 1, KT - 1, qh) for qh in halves(KT - 1)]

        def cost(x):
            kind, g, kt, j = x
            if kind == "score":
                return S - live(kt) + (0 if causal else 650)
            return GH * (512 * (j + 1) - max(live(kt), 512 * j)) * 1.15

        after = {}
        add = lambda g, kt, j, x: after.setdefault(("score", g, kt, j), []).append(x)
        for g in range(G):
            add(g, 2, 0, ("invert", (g - 1) % G, 0))
            for i in range(2):
                add(g, 2, 3, ("sums", (g - 1) % G, i))
            if g % 2 == 0:
                for i in range(4):
                    add(g, 3, i, ("out", (g // 2 - 1) % 2, i))
        order = []
        for g in range(G):
            mine = [x for x in pieces if (x[1] if x[0] == "score" else x[1] + (x[2] == KT - 1)) == g]
            total, done = sum(cost(x) for x in mine), 0
            todo = [("max", (g + 1) % G, i) for i in range(early, NJ)] + [("turn", (g + 1) % G, 0)]
            todo += [("max", (g + 2) % G, i) for i in range(early)]
            given = 0
            for x in mine:
                order.append(x)
                order += after.get(x, [])
                done += cost(x)
                while given < len(todo) * done / total:
                    order.append(todo[given])
                    given += 1
            order += todo[given:]
        order += [x for x in pieces if x[1] == G - 1 and x[0] == "pv" and x[2] == KT - 1]
        aux_jobs = [x for x in order if x[0] not in ("score", "pv", "invert")]
        aux_no = {x: i for i, x in enumerate(aux_jobs)}
        sums_done = lambda g: aux_no[("sums", g % G, 1)] + 1

        with nc.Fori(0, B) as b:
            b_next, b_prev = (b + 1) & (B - 1), (b + B - 1) & (B - 1)
            in_names = [f"qk{g}_in" for g in range(G)] + [f"v{g}_in" for g in range(G)] + [f"m{g}_in" for g in range(G)]
            with phase(nc, *in_names, "aux_full", "aux_free", "negm_ready", "scores_full", "probs_ready",
                       "pv_done", "acc_moved", "folded", "inverted", "unfolded", "rows_out", "chain") as (block, *sems):
                qk_in, v_in, m_in = sems[0:G], sems[G:2 * G], sems[2 * G:3 * G]
                (aux_full, aux_free, negm_ready, scores_full, probs_ready,
                 pv_done, acc_moved, folded, inverted, unfolded, rows_out, chain_sem) = sems[3 * G:]

                @block.sync
                def _(sp):
                    for g in range(G):
                        far, near = (g + 2) % G, (g + 1) % G
                        if g >= 2:
                            sp.wait_ge(scores_full, (g - 1) * KT * GH)
                        load_qk(sp, b if g < 2 else b_next, far, qk_in[far])
                        if g >= 1:
                            sp.wait_ge(pv_done, g * KT)
                        load_v(sp, b if g < 3 else b_next, near, v_in[near])
                        if not causal and g % 2 == 0:
                            hg = (g // 2 - 1) % 2
                            for i in range(4):
                                sp.wait_ge(aux_free, aux_no[("out", hg, i)] + 1)
                                store_rows(sp, b_prev if g == 0 else b, hg, i, rows_out)
                        sp.wait_ge(aux_free, aux_no[("turn", near, 0)] + 1)
                        store_max(sp, near, m_in[near])
                    sp.wait_ge(m_in[0], MAX_IN)
                    sp.wait_ge(v_in[0], 16)
                    for g in range(2):
                        sp.wait_ge(qk_in[g], QK_IN)
                    if not causal:
                        sp.wait_ge(rows_out, 16 * 16)

                def scores(pe, g, kt, j):
                    n = (g * KT + kt) * GH + j
                    if n >= 2:
                        pe.wait_ge(probs_ready, n - 1)
                    if g and kt == 0 and j == 0:
                        pe.wait_ge(m_in[g], MAX_IN)
                    lhs = kst[g][0:KS, j, kt * P:(kt + 1) * P]
                    for qh in halves(kt):
                        c0, c1 = max(live(kt), 512 * qh), 512 * (qh + 1)
                        extra = []
                        if causal and live(kt) // 512 == qh:
                            extra = [(live(kt), P, t.ident_bf, maskT[:])]
                        if not causal:
                            q0, q1 = max(c0, kt * P - 64), min(c1, kt * P - 64 + BAND)
                            if q0 < q1:
                                o = q0 - (kt * P - 64)
                                extra = [(q0, q1 - q0, t.ident_r, t.band[i][:, o:o + q1 - q0]) for i in range(2)]
                        mm = pe.matmul(psS[:, n % 2, c0:c1], lhs, qst[g][0:KS, j, c0:c1],
                                       start=True, stop=True)
                        for q0, w, eye, add in extra:
                            mm = pe.matmul(psS[:, n % 2, q0:q0 + w], eye[:], add, start=False,
                                           stop=True, skip_group_check=True)
                    mm.then_inc(scores_full, 1)

                def times_v(pe, g, kt, qh):
                    n = (g * KT + kt) * GH
                    pe.wait_ge(probs_ready, n + GH)
                    if g and kt == 0:
                        pe.wait_ge(acc_moved, g)
                        pe.wait_ge(v_in[g], 16)
                    c0, c1 = max(live(kt), 512 * qh), 512 * (qh + 1)
                    for j in range(GH):
                        vj = v[:, g % 2, kt, 32 * j:32 * j + 32]
                        if causal:
                            mm = pe.matmul(acc[32 * j:32 * j + 32, c0:c1], vj, prob[:, (n + j) % (2 * GH), c0:c1],
                                           start=(kt == 0), stop=(kt == last_kt(qh)))
                            continue
                        by_w = prob[:, (n + j) % (2 * GH), :].rearrange("p (u w r) -> p w u r", w=4, r=4)
                        for w in range(2 * qh, 2 * qh + 2):
                            mm = pe.matmul(acc[32 * w:32 * w + 32, j * 256:(j + 1) * 256], vj, by_w[:, w],
                                           start=(kt == 0 and j % 2 == 0), stop=(kt == KT - 1),
                                           skip_group_check=True)
                    if qh == 1:
                        mm.then_inc(pv_done, 1)

                @block.tensor
                def _(pe):
                    for x in order:
                        kind, g, i = x[0:3]
                        if kind == "score":
                            scores(pe, g, i, x[3])
                            continue
                        if kind == "pv":
                            times_v(pe, g, i, x[3])
                            continue
                        if kind == "invert":
                            continue
                        n = aux_no[x]
                        if n >= 2:
                            pe.wait_ge(aux_free, n - 1)
                        bank = aux[:, n % 2, :]
                        if kind == "max":
                            if i == 0:
                                pe.wait_ge(qk_in[g], QK_IN)
                            mm = pe_max(pe, g, i, bank)
                        elif kind == "turn":
                            pe.wait_ge(negm_ready, g if g else G)
                            mm = pe_turn(pe, g, bank)
                        elif kind == "sums":
                            pe.wait_ge(unfolded, 16 * ((g + 1) % G + 1))
                            mm = pe_sums(pe, i, bank)
                        else:
                            pe.wait_ge(aux_free, sums_done(2 * g + 1))
                            mm = pe_out(pe, g, i, bank)
                        mm.then_inc(aux_full, 1)

                @block.scalar
                def _(act):
                    def move(g):
                        act.wait_ge(pv_done, (g + 1) * KT)
                        if g:
                            act.wait_ge(aux_free, sums_done(g - 2))
                        act.activation(oT[:, g % 2, :], acc[:], ACT.Copy).then_inc(acc_moved, 1)

                    for g in range(G):
                        for kt in range(KT):
                            for j in range(GH):
                                n = (g * KT + kt) * GH + j
                                act.wait_ge(scores_full, n + 1)
                                if n >= 2 * GH:
                                    act.wait_ge(pv_done, n // GH - 1)
                                q0 = live(kt)
                                act.activation(prob[:, n % (2 * GH), q0:S], psS[:, n % 2, q0:S], ACT.Exp
                                               ).then_inc(probs_ready, 1)
                                if g and kt == 0 and j == 2:
                                    move(g - 1)
                    move(G - 1)

                @block.vector
                def _(dve):
                    chain = Chain(dve, chain_sem)
                    for kind, g, i in [x for x in order if x[0] not in ("score", "pv")]:
                        if kind == "invert":
                            k = (g + 1) % G
                            dve.wait_ge(folded, 16 * (k + 1))
                            dve.reciprocal(fold[:], fold[:]).then_inc(inverted, 1)
                            continue
                        n = aux_no[(kind, g, i)]
                        bank = aux[:, n % 2, :]
                        dve.wait_ge(aux_full, n + 1)
                        if kind == "max":
                            dve_max(dve, chain, g, i, bank, n, aux_free, negm_ready)
                        elif kind == "turn":
                            dve_turn(dve, g, bank, aux_free)
                        elif kind == "sums":
                            dve_sums(dve, g, i, bank, aux_free)
                        else:
                            if g == 0 and not causal:
                                dve.wait_ge(rows_out, 16 * 8)
                            dve_out(dve, b_prev if g else b, i, bank, aux_free)

                @block.gpsimd
                def _(pool):
                    for k in range(G):
                        g = (k - 1) % G
                        if k:
                            pool.wait_ge(acc_moved, k)
                            pool.wait_ge(unfolded, 16 * k)
                        fold_sums(pool, g, folded)
                        pool.wait_ge(inverted, k + 1)
                        if k:
                            pool.wait_ge(aux_full, sums_done(g - 1))
                        unfold_sums(pool, unfolded)
                    pool.wait_ge(unfolded, 16 * G)

        with phase(nc, "aux_full", "aux_free", "folded", "inverted", "unfolded", "rows_out") as (
                block, aux_full, aux_free, folded, inverted, unfolded, rows_out):

            @block.gpsimd
            def _(pool):
                fold_sums(pool, G - 1, folded)
                pool.wait_ge(inverted, 1)
                unfold_sums(pool, unfolded)
                pool.wait_ge(unfolded, 16)

            @block.tensor
            def _(pe):
                pe.wait_ge(unfolded, 16)
                for n in range(6):
                    bank = aux[:, n % 2, :]
                    if n >= 2:
                        pe.wait_ge(aux_free, max(n - 1, 2))
                    (pe_sums(pe, n, bank) if n < 2 else pe_out(pe, 1, n - 2, bank)).then_inc(aux_full, 1)

            @block.vector
            def _(dve):
                dve.wait_ge(folded, 16)
                dve.reciprocal(fold[:], fold[:]).then_inc(inverted, 1)
                for n in range(6):
                    dve.wait_ge(aux_full, n + 1)
                    if n < 2:
                        dve_sums(dve, G - 1, n, aux[:, n % 2, :], aux_free)
                    else:
                        dve_out(dve, B - 1, n - 2, aux[:, n % 2, :], aux_free)

            if not causal:
                @block.sync
                def _(sp):
                    for i in range(4):
                        sp.wait_ge(aux_free, i + 3)
                        store_rows(sp, B - 1, 1, i, rows_out)
                    sp.wait_ge(rows_out, 16 * 8)


def add_attention(nc, t):
    with ExitStack() as own:
        sb, _ = buffers(nc, own, "add")
        rows = sb("attn_rows", [P, KT, D])
        src = t.attn_dram.rearrange("(n k) p d -> n (k p) d", k=2)
        with nc.Fori(0, B) as b:
            with phase(nc, "rows_in", "biased") as (block, rows_in, biased):
                tiles = bass.ds(b * KT, KT)

                @block.sync
                def _(sp):
                    sp.dma_start(rows[:], src[tiles].rearrange("n p d -> p n d")).then_inc(rows_in, 16)

                @block.vector
                def _(dve):
                    bo = t.bo[:].rearrange("p (o d) -> p o d", o=1).to_broadcast([P, KT, D])
                    dve.tensor_tensor(t.h[:, tiles, :], t.h[:, tiles, :], bo, ALU.add).then_inc(biased, 1)
                    dve.wait_ge(rows_in, 16)
                    dve.wait_ge(biased, 1)
                    dve.tensor_tensor(t.h[:, tiles, :], t.h[:, tiles, :], rows[:], ALU.add)


def route(nc, t, a, layer, m):
    W, E, K = LT * P, m.E, m.top
    with ExitStack() as own:
        sb, ps = buffers(nc, own, f"route{layer}")
        n = norm_buffers(sb)
        wg = sb("router_w", [P, DT, E])
        bg = sb("router_b", [P, E])
        iota_e, cap_e = t.iota_e[:, 0:E], sb("cap_e", [P, E])
        carry = sb("carry", [P, E])
        base = sb("base", [P, LT, E])
        lg, pr, pos = sb("logits", [P, LT, E]), sb("gate_probs", [P, LT, E]), sb("pos", [P, LT, E])
        tmp = sb("tmp", [P, LT, E])
        red = sb("red", [P, LT])
        top = sb("top8", [P, LT, 8])
        topi = sb("top8_index", [P, LT, 8], mybir.dt.uint32)
        topf = sb("top_index", [P, LT, K])
        hot = sb("one_hot", [P, K, LT, E])
        hot_bf = sb("one_hot_bf", [P, LT, E], BF16)
        posf = sb("pos_f", [P, K, LT])
        posi = sb("pos_i", [P, K, LT], I32)
        wsum = sb("weight_sum", [P, LT])
        zero = sb("zero_rows", [P, D])
        zpos, zposi = sb("zero_pos", [P, E]), sb("zero_pos_i", [P, E], I32)
        pcol = sb("partition_no", [P, 1])
        psT = ps("xT", [P, DT, W])
        psL = ps("logits", [P, LT, E])
        psR = ps("rank", [P, LT, E])
        psN = ps("count", [P, LT, E])
        if layer == 1:
            wnat = sb("router_nat", [E, D])
        wide = lambda ap: ap.rearrange("p (o e) -> p o e", o=1).to_broadcast([P, LT, E])
        tall = lambda ap: ap.rearrange("p (k o) -> p k o", o=1).to_broadcast([P, LT, E])
        with phase(nc, "loaded", "made", "turned", "copied") as (block, loaded, made, turned, copied):

            @block.sync
            def _(sp):
                if layer == 0:
                    sp.dma_start(wg[:], a["L0_ffn_Wg"].rearrange("(dt d) e -> d dt e", d=P)).then_inc(loaded, 16)
                    bias = a["L0_ffn_bg"]
                else:
                    sp.dma_start(wnat[:], a["L1_ffn_router_w"]).then_inc(loaded, 16)
                    bias = a["L1_ffn_router_b"]
                sp.dma_start(bg[:], bias.rearrange("(o e) -> o e", o=1).to_broadcast([P, E])).then_inc(loaded, 16)
                sp.wait_ge(loaded, 32)

            @block.gpsimd
            def _(pool):
                pool.iota(iota_e, pattern=[[1, E]], base=0, channel_multiplier=0,
                          allow_small_or_imprecise_dtypes=True)
                pool.iota(cap_e[:], pattern=[[m.cap, E]], base=0, channel_multiplier=0,
                          allow_small_or_imprecise_dtypes=True)
                pool.iota(carry[:], pattern=[[m.cap, E]], base=0, channel_multiplier=0,
                          allow_small_or_imprecise_dtypes=True)
                pool.iota(pcol[:], pattern=[[1, 1]], base=0, channel_multiplier=1,
                          allow_small_or_imprecise_dtypes=True)
                pool.memset(zero[:], 0.0)

            if layer == 1:
                @block.tensor
                def _(pe):
                    pe.wait_ge(loaded, 32)
                    for dt in range(DT):
                        mm = pe.transpose(psT[:, dt, 0:E], wnat[:, dt * P:(dt + 1) * P], t.ident[0:E, 0:E])
                    mm.then_inc(turned, 1)

                @block.vector
                def _(dve):
                    dve.wait_ge(turned, 1)
                    dve.tensor_copy(wg[:], psT[:, :, 0:E])

        with nc.Fori(0, B) as b, nc.Fori(0, 2) as th:
            with phase(nc, "chain", "var_ready", "root_ready", "normed", "turned", "x_ready", "logits_ready",
                       "shifted", "exped", "hot_ready", "ranked", "pos_ready", "scattered") as (
                    block, chain_sem, var_ready, root_ready, normed, turned, x_ready, logits_ready,
                    shifted, exped, hot_ready, ranked, pos_ready, scattered):

                @block.tensor
                def _(pe):
                    norm_turn(pe, t, n, psT, normed, turned)
                    pe.wait_ge(x_ready, 1)
                    for j in range(LT):
                        for dt in range(DT):
                            mm = pe.matmul(psL[:, j, :], n.xT[:, dt, j * P:(j + 1) * P], wg[:, dt, :],
                                           start=(dt == 0), stop=(dt == DT - 1))
                    mm.then_inc(logits_ready, 1)
                    pe.wait_ge(hot_ready, 1)
                    flat = hot_bf[:].rearrange("p j e -> p (j e)")
                    pe.matmul(psR[:].rearrange("p j e -> p (j e)"), t.before[:], flat, start=True, stop=True)
                    pe.matmul(psN[:].rearrange("p j e -> p (j e)"), t.ones_bf[:], flat, start=True, stop=True
                              ).then_inc(ranked, 1)

                @block.scalar
                def _(act):
                    norm_root(act, n, var_ready, root_ready)
                    if K == 2:
                        act.wait_ge(shifted, 1)
                        act.activation(pr[:], lg[:], ACT.Exp).then_inc(exped, 1)

                @block.vector
                def _(dve):
                    chain = Chain(dve, chain_sem)
                    norm_vector(dve, chain, t, n, b * KT + th * LT, var_ready, root_ready, normed)
                    dve.wait_ge(turned, 1)
                    dve.tensor_copy(n.xT[:], psT[:]).then_inc(x_ready, 1)
                    dve.wait_ge(logits_ready, 1)
                    chain(dve.tensor_tensor(lg[:], psL[:], wide(bg[:]), ALU.add))
                    score = lg
                    if K == 2:
                        chain(dve.tensor_reduce(red[:], lg[:], AX, ALU.max))
                        dve.tensor_tensor(lg[:], lg[:], tall(red[:]), ALU.subtract).then_inc(shifted, 1)
                        dve.wait_ge(exped, 1)
                        chain(dve.tensor_reduce(red[:], pr[:], AX, ALU.add))
                        chain(dve.reciprocal(red[:], red[:]))
                        chain(dve.tensor_tensor(pr[:], pr[:], tall(red[:]), ALU.mult))
                        score = pr
                    for j in range(LT):
                        chain(dve.max(top[:, j, :], score[:, j, :]))
                        chain(dve.max_index(topi[:, j, :], top[:, j, :], score[:, j, :]))
                    chain(dve.tensor_copy(topf[:], topi[:, :, 0:K]))
                    for k in range(K):
                        chain(dve.tensor_tensor(hot[:, k], wide(iota_e),
                                                topf[:, :, k:k + 1].to_broadcast([P, LT, E]), ALU.is_equal))
                    if K == 2:
                        dve.tensor_tensor(hot_bf[:], hot[:, 0], hot[:, 1], ALU.add).then_inc(hot_ready, 1)
                        chain(dve.tensor_tensor(wsum[:], top[:, :, 0], top[:, :, 1], ALU.add))
                        chain(dve.tensor_scalar(wsum[:], wsum[:], 1e-8, None, ALU.add))
                        chain(dve.reciprocal(wsum[:], wsum[:]))
                        for k in range(K):
                            dve.tensor_tensor(t.weight[:, k, bass.ds(b * KT + th * LT, LT)], top[:, :, k], wsum[:],
                                              ALU.mult)
                    else:
                        dve.tensor_copy(hot_bf[:], hot[:, 0]).then_inc(hot_ready, 1)
                    dve.wait_ge(ranked, 1)
                    chain(dve.tensor_copy(base[:, 0, :], carry[:]))
                    for j in range(1, LT):
                        chain(dve.tensor_tensor(base[:, j, :], base[:, j - 1, :], psN[:, j - 1, :], ALU.add))
                    chain(dve.tensor_tensor(carry[:], base[:, LT - 1, :], psN[:, LT - 1, :], ALU.add))
                    chain(dve.tensor_tensor(pos[:], base[:], psR[:], ALU.add))
                    for k in range(K):
                        chain(dve.tensor_tensor(tmp[:], pos[:], hot[:, k], ALU.mult))
                        chain(dve.tensor_reduce(posf[:, k, :], tmp[:], AX, ALU.add))
                    dve.tensor_copy(posi[:], posf[:]).then_inc(pos_ready, 1)
                    dve.tensor_copy(t.row_of[:, 0:K, bass.ds(b * KT + th * LT, LT)], posf[:])
                    dve.tensor_copy(t.expert_of[:, 0:K, bass.ds(b * KT + th * LT, LT)],
                                    topf[:].rearrange("p j k -> p k j"))

                @block.gpsimd
                def _(pool):
                    pool.wait_ge(pos_ready, 1)
                    for k in range(K):
                        for j in range(LT):
                            off = bass.IndirectOffsetOnAxis(ap=posi[:, k, j:j + 1], axis=0)
                            pool.indirect_dma_start(t.x_rows[layer], off, n.xn[:, j, :], None).then_inc(scattered, 16)
                    pool.wait_ge(scattered, 16 * K * LT)

        expert_table(nc, own, t, m, layer, carry, cap_e, iota_e, pcol, zpos, zposi, zero)


def expert_table(nc, own, t, m, layer, carry, cap_e, iota_e, pcol, zpos, zposi, zero):
    E, NT = m.E, m.NT
    sb, ps = buffers(nc, own, f"table{layer}")
    cnt, cnti = sb("cnt", [P, E]), sb("cnt_i", [P, E], I32)
    end, one = sb("end", [P, E]), sb("one_row", [P, E])
    f = t.shift[:, 0:E]
    tno = sb("tile_no", [1, NT])
    ge, sel = sb("past", [1, NT, E]), sb("owner", [1, NT, E])
    te, row, tail = sb("tile_expert", [1, NT]), sb("tile_row", [1, NT]), sb("tail", [1, NT])
    x1 = sb("x1", [1, NT])
    with phase(nc, "zpos_ready", "zeroed", "tno_ready", "chain") as (block, zpos_ready, zeroed, tno_ready, chain_sem):

        @block.gpsimd
        def _(pool):
            pool.iota(tno[:], pattern=[[1, NT]], base=0, channel_multiplier=0,
                      allow_small_or_imprecise_dtypes=True).then_inc(tno_ready, 1)
            pool.wait_ge(zpos_ready, 1)
            for e in range(E):
                off = bass.IndirectOffsetOnAxis(ap=zposi[:, e:e + 1], axis=0)
                pool.indirect_dma_start(t.x_rows[layer], off, zero[:], None).then_inc(zeroed, 16)
            pool.dma_start(t.x_rows[layer][m.zero_row:m.zero_row + P, :], zero[:]).then_inc(zeroed, 16)
            pool.wait_ge(zeroed, 16 * (E + 1))

        @block.vector
        def _(dve):
            chain = Chain(dve, chain_sem)
            chain(dve.tensor_scalar(zpos[:], carry[:], pcol[:, 0:1], None, ALU.add))
            dve.tensor_copy(zposi[:], zpos[:]).then_inc(zpos_ready, 1)
            chain(dve.tensor_tensor(cnt[:], carry[:], cap_e[:], ALU.subtract))
            chain(dve.tensor_scalar(cnt[:], cnt[:], float(P - 1), None, ALU.add))
            chain(dve.tensor_copy(cnti[:], cnt[:]))
            chain(dve.tensor_scalar(cnti[:], cnti[:], 7, None, ALU.arith_shift_right))
            chain(dve.tensor_copy(cnt[:], cnti[:]))
            chain(dve.memset(one[:], 1.0))
            chain(dve.tensor_tensor_scan(end[:], one[:], cnt[:], 0.0, ALU.mult, ALU.add))
            chain(dve.tensor_tensor(f, end[:], cnt[:], ALU.subtract))
            chain(dve.tensor_scalar(f, f, -float(P), None, ALU.mult))
            chain(dve.tensor_tensor(f, f, cap_e[:], ALU.add))
            dve.wait_ge(tno_ready, 1)
            by_tile = lambda ap: ap.rearrange("p (n o) -> p n o", o=1).to_broadcast([1, NT, E])
            by_e = lambda ap: ap.rearrange("p (o e) -> p o e", o=1).to_broadcast([1, NT, E])
            chain(dve.tensor_tensor(ge[:], by_e(end[0:1, :]), by_tile(tno[:]), ALU.is_le))
            chain(dve.tensor_reduce(te[:], ge[:], AX, ALU.add))
            chain(dve.tensor_scalar(te[:], te[:], float(E - 1), None, ALU.min))
            chain(dve.tensor_tensor(sel[:], by_e(iota_e[0:1, :]), by_tile(te[:]), ALU.is_equal))
            chain(dve.tensor_tensor(sel[:], sel[:], by_e(t.shift[0:1, 0:E]), ALU.mult))
            chain(dve.tensor_reduce(row[:], sel[:], AX, ALU.add))
            chain(dve.tensor_scalar(x1[:], tno[:], float(P), None, ALU.mult))
            chain(dve.tensor_tensor(row[:], row[:], x1[:], ALU.add))
            chain(dve.tensor_copy(tail[:], ge[:, :, E - 1]))
            chain(dve.tensor_copy(t.table[:, 0, 0:NT], te[:]))
            chain(dve.tensor_scalar(x1[:], row[:], -1.0, float(m.zero_row), ALU.mult, ALU.add))
            chain(dve.tensor_tensor(x1[:], x1[:], tail[:], ALU.mult))
            chain(dve.tensor_tensor(x1[:], x1[:], row[:], ALU.add))
            chain(dve.tensor_copy(t.table[:, 1, 0:NT], x1[:]))
            chain(dve.memset(x1[:], 1.0))
            chain(dve.tensor_tensor(x1[:, 2:NT], te[:, 2:NT], te[:, 0:NT - 2], ALU.not_equal))
            chain(dve.tensor_copy(t.table[:, 2, 0:NT], x1[:]))


def experts(nc, t, a, layer, m):
    E, FT, FP, F, NT = m.E, m.FT, m.FP, m.F, m.NT
    with ExitStack() as own:
        sb, ps = buffers(nc, own, f"experts{layer}")
        w1 = sb("w1", [P, 2, DT, F])
        w2 = sb("w2", [FP, 2, FT, D])
        b1 = sb("b1", [FP, E * FT])
        b2 = sb("b2", [P, E, D])
        NX = 4
        HB = 512 // P
        HBANKS = -(-FT // HB)
        xr = sb("x_tile", [P, NX, D])
        xT = sb("xT_tile", [P, 2, DT, P])
        hT = sb("hidden", [FP, 2, FT, P])
        y = sb("y_tile", [P, NX, D])
        psX = ps("x", [P, 2, 512])
        psH = ps("hidden", [FP, 2, 1024])
        psY = ps("y", [P, 2, 512])
        n0 = ("L0_ffn_W1", "L0_ffn_b1", "L0_ffn_W2", "L0_ffn_b2")
        n1 = ("L1_ffn_weights1", "L1_ffn_bias1", "L1_ffn_weights2", "L1_ffn_bias2")
        W1, B1, W2, B2 = (a[x] for x in (n1 if layer else n0))
        with phase(nc, "loaded") as (block, loaded):

            @block.sync
            def _(sp):
                with nc.allow_non_contiguous_dma(reason="hidden biases go one to a partition"):
                    sp.dma_start(b1[:], B1.rearrange("e (ft f) -> f (e ft)", f=FP)).then_inc(loaded, 16)
                src = B2.rearrange("(o e) d -> o e d", o=1).to_broadcast([P, E, D])
                sp.dma_start(b2[:], src).then_inc(loaded, 16)
                sp.wait_ge(loaded, 32)

        with nc.Fori(0, m.passes) as it:
            names = ([f"w_in{i}" for i in range(2)] + [f"x_in{i}" for i in range(NX)] +
                     [f"y_out{i}" for i in range(NX)] +
                     ["turned", "xT_ready", "hidden_full", "hidden_ready", "y_full", "y_ready", "y_rect"])
            with phase(nc, *names) as (block, *sems):
                w_in, x_in, y_out = sems[0:2], sems[2:2 + NX], sems[2 + NX:2 + 2 * NX]
                turned, xT_ready, hidden_full, hidden_ready, y_full, y_ready, y_rect = sems[2 + 2 * NX:]

                @block.sync
                def _(sp):
                    def load_x(i):
                        row = sp.value_load(t.table[0:1, 1, bass.ds(it * m.per + i, 1)], min_val=0, max_val=m.rows - P)
                        if i >= NX:
                            sp.wait_ge(turned, i - NX + 1)
                        sp.dma_start(xr[:, i % NX, :], t.x_rows[layer][bass.ds(row, P), :]).then_inc(x_in[i % NX], 16)

                    def load_w(i):
                        e = sp.value_load(t.table[0:1, 0, bass.ds(it * m.per + i, 1)], min_val=0, max_val=E - 1)
                        need = sp.value_load(t.table[0:1, 2, bass.ds(it * m.per + i, 1)], min_val=0, max_val=1)
                        if i >= 2:
                            sp.wait_ge(y_full, i - 1)
                        src1 = W1[bass.ds(e, 1)].rearrange("o (dt d) f -> d (o dt) f", d=P)
                        sp.dma_start(w1[:, i % 2], src1, cond=need).then_inc(w_in[i % 2], 16)
                        src2 = W2[bass.ds(e, 1)].rearrange("o (ft f) d -> f (o ft) d", f=FP)
                        sp.dma_start(w2[:, i % 2], src2, cond=need).then_inc(w_in[i % 2], 16)

                    load_x(0)
                    load_w(0)
                    load_x(1)
                    load_w(1)
                    for i in range(2, m.per):
                        load_x(i)
                        load_w(i)

                @block.tensor
                def _(pe):
                    def turn(i):
                        pe.wait_ge(x_in[i % NX], 16 * (i // NX + 1))
                        if i >= 2:
                            pe.wait_ge(xT_ready, i - 1)
                        for dt in range(DT):
                            mm = pe.transpose(psX[:, i % 2, dt * P:(dt + 1) * P], xr[:, i % NX, dt * P:(dt + 1) * P],
                                              t.ident[:])
                        mm.then_inc(turned, 1)

                    def up(i):
                        pe.wait_ge(w_in[i % 2], 32 * (i // 2 + 1))
                        pe.wait_ge(xT_ready, i + 1)
                        for ft in range(FT):
                            if i >= 2 and ft % HB == 0:
                                pe.wait_ge(hidden_ready, FT * (i - 2) + min(ft + HB, FT))
                            for dt in range(DT):
                                mm = pe.matmul(psH[:, i % 2, ft * P:ft * P + P], w1[:, i % 2, dt, ft * P:ft * P + FP],
                                               xT[:, i % 2, dt, :], start=(dt == 0), stop=(dt == DT - 1))
                            if ft % HB == HB - 1 or ft == FT - 1:
                                mm.then_inc(hidden_full, 1)

                    def down(i):
                        if i >= 2:
                            pe.wait_ge(y_ready, i - 1)
                        for ft in range(FT):
                            pe.wait_ge(hidden_ready, FT * i + ft + 1)
                            mm = pe.matmul(psY[:, i % 2, 0:D], hT[:, i % 2, ft, :], w2[:, i % 2, ft, :],
                                           start=(ft == 0), stop=(ft == FT - 1))
                        mm.then_inc(y_full, 1)

                    turn(0)
                    for i in range(m.per):
                        up(i)
                        if i + 1 < m.per:
                            turn(i + 1)
                        down(i)

                @block.scalar
                def _(act):
                    for i in range(m.per):
                        e = act.value_load(t.table[0:1, 0, bass.ds(it * m.per + i, 1)], min_val=0, max_val=E - 1)
                        for ft in range(FT):
                            if ft % HB == 0:
                                act.wait_ge(hidden_full, HBANKS * i + ft // HB + 1)
                            if i >= 2:
                                act.wait_ge(y_full, i - 1)
                            act.activation(hT[:, i % 2, ft, :], psH[:, i % 2, ft * P:(ft + 1) * P],
                                           ACT.Relu if layer else ACT.Gelu_apprx_tanh,
                                           bias=b1[:, bass.ds(e * FT + ft, 1)]).then_inc(hidden_ready, 1)

                @block.vector
                def _(dve):
                    def move(i):
                        dve.wait_ge(turned, i + 1)
                        if i >= 2:
                            dve.wait_ge(hidden_full, HBANKS * (i - 1))
                        dve.tensor_copy(xT[:, i % 2], psX[:, i % 2, 0:DT * P].rearrange("p (a b) -> p a b", a=DT)
                                        ).then_inc(xT_ready, 1)

                    move(0)
                    for i in range(m.per):
                        e = dve.value_load(t.table[0:1, 0, bass.ds(it * m.per + i, 1)], min_val=0, max_val=E - 1)
                        if i + 1 < m.per:
                            move(i + 1)
                        dve.wait_ge(y_full, i + 1)
                        if i >= NX:
                            dve.wait_ge(y_out[i % NX], 16 * (i // NX))
                        bias = b2[:, bass.ds(e, 1), :].rearrange("p o d -> p (o d)")
                        dve.tensor_tensor(y[:, i % NX, :], psY[:, i % 2, 0:D], bias, ALU.add).then_inc(y_ready, 1)
                        if layer:
                            dve.wait_ge(y_ready, i + 1)
                            dve.tensor_scalar(y[:, i % NX, :], y[:, i % NX, :], 0.0, None, ALU.max).then_inc(y_rect, 1)

                @block.gpsimd
                def _(pool):
                    for i in range(m.per):
                        pool.wait_ge(y_rect if layer else y_ready, i + 1)
                        pool.dma_start(t.y_rows[layer][bass.ds((it * m.per + i) * P, P), :], y[:, i % NX, :]).then_inc(y_out[i % NX], 16)
                    for s in range(NX):
                        pool.wait_ge(y_out[s], 16 * (m.per // NX))


def combine(nc, t, a, layer, m, out):
    K = m.top
    with ExitStack() as own:
        sb, ps = buffers(nc, own, f"combine{layer}")
        rows = sb("y_rows", [P, K, LT, D])
        idx = sb("row_idx", [P, K, LT], I32)
        rowf, shift = sb("row_f", [P, K, LT]), sb("shift", [P, K, LT])
        hot = sb("one_hot", [P, K * LT, m.E])
        wts = sb("weights_of_tile", [P, K, LT])
        res = sb("result", [P, LT, D])
        with nc.Fori(0, B) as b, nc.Fori(0, 2) as th:
            with phase(nc, "idx_ready", "wts_ready", "rows_in", "chain", "stored") as (
                    block, idx_ready, wts_ready, rows_in, chain_sem, stored):
                tiles = bass.ds(b * KT + th * LT, LT)

                @block.vector
                def _(dve):
                    chain = Chain(dve, chain_sem)
                    by_e = lambda ap: ap.rearrange("p (o e) -> p o e", o=1).to_broadcast([P, LT, m.E])
                    for k in range(K):
                        mine = t.expert_of[:, k, tiles].rearrange("p (j o) -> p j o", o=1).to_broadcast([P, LT, m.E])
                        chain(dve.tensor_tensor(hot[:, k * LT:(k + 1) * LT, :], by_e(t.iota_e[:, 0:m.E]), mine,
                                                ALU.is_equal))
                        chain(dve.tensor_tensor(hot[:, k * LT:(k + 1) * LT, :], hot[:, k * LT:(k + 1) * LT, :],
                                                by_e(t.shift[:, 0:m.E]), ALU.mult))
                        chain(dve.tensor_reduce(shift[:, k, :], hot[:, k * LT:(k + 1) * LT, :], AX, ALU.add))
                    chain(dve.tensor_tensor(rowf[:], t.row_of[:, 0:K, tiles], shift[:], ALU.subtract))
                    dve.tensor_copy(idx[:], rowf[:]).then_inc(idx_ready, 1)
                    if K == 2:
                        chain(dve.tensor_copy(wts[:], t.weight[:, :, tiles]))
                    dve.wait_ge(rows_in, 16 * K * LT)
                    if K == 2:
                        for k in range(K):
                            for j in range(LT):
                                hh = t.h[:, bass.ds(b * KT + th * LT + j, 1), :].rearrange("p o d -> p (o d)")
                                src = hh if k == 0 else res[:, j, :]
                                dst = res[:, j, :] if k == 0 else hh
                                dve.scalar_tensor_tensor(out=dst, in0=rows[:, k, j, :], scalar=wts[:, k, j:j + 1],
                                                         in1=src, op0=ALU.mult, op1=ALU.add).then_inc(chain.sem, 1)
                                chain.n += 1
                            dve.wait_ge(chain.sem, chain.n)
                    else:
                        chain(dve.tensor_tensor(res[:], rows[:, 0], t.h[:, tiles, :], ALU.add))

                @block.gpsimd
                def _(pool):
                    pool.wait_ge(idx_ready, 1)
                    for k in range(K):
                        for j in range(LT):
                            off = bass.IndirectOffsetOnAxis(ap=idx[:, k, j:j + 1], axis=0)
                            pool.indirect_dma_start(rows[:, k, j, :], None, t.y_rows[layer], off).then_inc(rows_in, 16)
                    pool.wait_ge(rows_in, 16 * K * LT)

                if layer:
                    @block.sync
                    def _(sp):
                        sp.wait_ge(chain_sem, 3 * K + 2)
                        dst = out.rearrange("b (k p) d -> (b k) p d", p=P)[tiles].rearrange("k p d -> p k d")
                        sp.dma_start(dst, res[:]).then_inc(stored, 16)
                        sp.wait_ge(stored, 16)


def build(nc, a, out, upto=99):
    with ExitStack() as ctx:
        t = Tensors()
        dram = lambda n, s, d=F32: nc.dram_tensor(n, s, d).ap()
        t.qk_dram = dram("qk_parts", [B, 2, 3, HEADS, HD, S], BF16)
        t.v_dram = dram("v_rows", [B * KT, P, HEADS * 32])
        t.attn_dram = dram("attn_rows", [B * HEADS, S * HD // D, D])
        t.x_rows = [dram(f"x_rows{l}", [m.rows, D]) for l, m in enumerate((MOE0, MOE1))]
        t.y_rows = [dram(f"y_rows{l}", [m.NT * P, D]) for l, m in enumerate((MOE0, MOE1))]
        sb = lambda n, s, d=F32: ctx.enter_context(nc.sbuf_tensor(n, s, d))
        t.table = sb("tile_table", [1, 3, max(MOE0.NT, MOE1.NT)], I32)
        t.row_of = sb("row_of", [P, 2, TILES])
        t.weight = sb("weight", [P, 2, TILES])
        t.expert_of = sb("expert_of", [P, 2, TILES])
        t.shift = sb("region_shift", [P, MOE1.E])
        t.iota_e = sb("iota_e", [P, MOE1.E])
        setup(nc, ctx, t, a)
        steps = [lambda: embed(nc, t, a),
                 lambda: project(nc, t, a, 0), lambda: attention(nc, t, a, 0),
                 lambda: route(nc, t, a, 0, MOE0), lambda: experts(nc, t, a, 0, MOE0),
                 lambda: combine(nc, t, a, 0, MOE0, out),
                 lambda: project(nc, t, a, 1), lambda: (attention(nc, t, a, 1), add_attention(nc, t)),
                 lambda: route(nc, t, a, 1, MOE1), lambda: experts(nc, t, a, 1, MOE1),
                 lambda: combine(nc, t, a, 1, MOE1, out)]
        for s in steps[:upto]:
            s()
        if upto < len(steps):
            with phase(nc, "stored") as (block, stored):
                @block.sync
                def _(sp):
                    sp.dma_start(out.rearrange("b (k p) d -> p (b k) d", p=P), t.h[:]).then_inc(stored, 16)
                    sp.wait_ge(stored, 16)


def constants():
    f = np.float32
    p, k, q = np.arange(P), np.arange(KT), np.arange(S)
    freq = (10000.0 ** (-np.arange(0, HD, 2) / HD)).astype(f)
    angle = q.astype(f)[None, :] * freq[p % FREQ][:, None]
    ident = np.eye(P, dtype=f)
    den_row = (p[:, None] == 32 * (p[None, :] // 32) + HD).astype(f)
    key_rows = np.concatenate([np.ones((ROW_MAX, S), f)] + [(q[None, :] // P == k[:, None]).astype(f)] * 3)
    above = (q[None, :] < P * k[:, None] - 64).astype(f)
    below = (q[None, :] >= P * k[:, None] - 64 + BAND).astype(f)
    return {"c_ident": ident, "c_den_row": den_row, "c_cos": np.cos(angle), "c_sin": np.sin(angle),
            "c_key_rows": key_rows, "c_above": above, "c_below": below}


def kernel(**inputs):
    from concourse import bacc
    from concourse.bass_utils import run_bass_kernel_spmd

    nc = bacc.Bacc("TRN2", target_bir_lowering=False, num_devices=1)
    arrays, a = {}, {}
    for name, value in [*inputs.items(), *constants().items()]:
        value = np.ascontiguousarray(value)
        arrays[name] = value
        a[name] = nc.dram_tensor(name, value.shape, mybir.dt.from_np(value.dtype), kind="ExternalInput").ap()
    out = nc.dram_tensor("out", [B, S, D], F32, kind="ExternalOutput").ap()
    build(nc, a, out)
    r = run_bass_kernel_spmd(nc, [arrays], core_ids=[0])
    return r.results[0]["out"]
```

```python
from contextlib import ExitStack, contextmanager

import numpy as np

import concourse.bass as bass
from concourse import mybir

F32 = mybir.dt.float32
F32R = mybir.dt.float32r
BF16 = mybir.dt.bfloat16
I32 = mybir.dt.int32
ALU = mybir.AluOpType
ACT = mybir.ActivationFunctionType
AX = mybir.AxisListType.X

P = 128
B, S, D = 4, 1024, 256
TILES = B * S // P
DT = D // P
HEADS, HD = 16, 16
FREQ = HD // 2
GH = 4
UH = HEADS // 2
KT = S // P
LT = 4
EPS = 1e-5
NEG = -1e30
PARTS_Q = (0, 0, 1, 0, 1, 2)
PARTS_K = (0, 1, 0, 2, 1, 0)
PROD = len(PARTS_Q) * HD
LATEST = (0.75, 0.9)
PIECE, V_WEIGHT = (0, 300), (0.6, 1.15)
ROW_MAX = 2
TB = 125
REACH = TB // 2
BAND = P + 2 * 64
BIAS_ROWS = 3 * KT
NO_TARGET = float(2 ** 20)
XW = D + 1
STRIP = 2 * S - P


@contextmanager
def phase(nc, *names):
    with ExitStack() as held:
        sems = [held.enter_context(nc.semaphore(n)) for n in names]
        with nc.Block() as block:
            yield (block, *sems)
        numbers = sorted(s.num for s in sems)
        first = 0
        for i in range(len(numbers)):
            if i + 1 == len(numbers) or numbers[i + 1] != numbers[i] + 1:
                used = range(numbers[first], numbers[i] + 1)
                nc.gpsimd.dma_reset(used)
                nc.gpsimd.sem_clear(used)
                first = i + 1
        nc.all_engine_barrier()


def buffers(nc, held, tag):
    return (lambda n, s, d=F32: held.enter_context(nc.sbuf_tensor(f"{tag}_{n}", s, d)),
            lambda n, s: held.enter_context(nc.psum_tensor(f"{tag}_ps_{n}", s, F32)))


class Tensors:
    pass


class Chain:

    def __init__(self, eng, sem):
        self.eng, self.sem, self.n = eng, sem, 0

    def __call__(self, ins):
        ins.then_inc(self.sem, 1)
        self.n += 1
        self.eng.wait_ge(self.sem, self.n)


class Expert:

    def __init__(self, experts, top, hidden, per, slots):
        self.E, self.top, self.F = experts, top, hidden
        self.FT = max(1, hidden // P)
        self.FP = min(P, hidden)
        self.cap = B * S + P
        self.tiles = B * S * top // P + experts - 1
        self.per, self.slots = per, slots
        self.passes = -(-self.tiles // self.per)
        self.NT = self.passes * self.per
        self.zero_row = experts * self.cap
        self.rows = self.zero_row + P


EXPERT_NAMES = (("L0_ffn_W1", "L0_ffn_b1", "L0_ffn_W2", "L0_ffn_b2"),
                ("L1_ffn_weights1", "L1_ffn_bias1", "L1_ffn_weights2", "L1_ffn_bias2"))
MOE0, MOE1 = Expert(8, 2, 1024, 24, 2), Expert(32, 1, 64, 32, 4)


def start(nc, ctx, t, a):
    sb, _ = buffers(nc, ctx, "all")
    t.h = sb("h", [P, TILES, D])
    t.ident = sb("ident", [P, P])
    t.ident_bf = sb("ident_bf", [P, P], BF16)
    t.ident_r = sb("ident_r", [P, P], F32R)
    t.ones_bf = sb("ones_bf", [P, P], BF16)
    t.before = sb("before", [P, P], BF16)
    t.den_row = sb("den_row", [P, P])
    t.wqT = [sb(f"wqT{l}", [P, DT, D]) for l in range(2)]
    t.wkT = [sb(f"wkT{l}", [P, DT, D]) for l in range(2)]
    t.wvT = [sb(f"wvT{l}", [P, DT, D]) for l in range(2)]
    t.woP = [sb(f"woP{l}", [P, HEADS // GH, D]) for l in range(2)]
    t.bqk = sb("bqk", [P, 2, 2])
    t.bv = sb("bv", [P, D])
    t.bo = sb("bo", [P, D])
    t.mv = sb("mean_and_variance", [P, TILES, 2])
    t.mean, t.inv = sb("mean", [P, TILES]), sb("inv", [P, TILES])
    t.bias_strip = sb("bias_strip", [P, STRIP])
    t.band = [sb(f"band{i}", [P, BAND], F32R) for i in range(2)]
    LS = STRIP + P - 1
    strip_dram = nc.dram_tensor("strip_rows", [P, LS], F32).ap()
    row_dram = nc.dram_tensor("strip_row", [1, LS], F32).ap()
    t.far_dram = nc.dram_tensor("bias_far", [BIAS_ROWS, S], BF16).ap()
    t.key_dram = nc.dram_tensor("key_rows", [ROW_MAX + BIAS_ROWS, S], BF16).ap()
    R = 16
    w = {0: "L0_attn_", 1: "L1_attn_"}
    with ExitStack() as own:
        tb_, tp_ = buffers(nc, own, "start")
        nat = tb_("w_nat", [P, 8, 2, D])
        woT = tb_("woT", [P, 2, DT, D])
        ids_nat = tb_("ids_by_tile", [TILES, P], I32)
        ids_f = tb_("ids_by_tile_f", [TILES, P])
        ids = tb_("ids", [P, TILES], I32)
        la = tb_("lora_rows", [P, TILES, R])
        laT = tb_("lora_rowsT", [R, 2, KT, P])
        lb = tb_("lora_b", [R, D])
        g = tb_("gates", [1, 4])
        tbf = tb_("time_bias", [1, TB])
        srow = tb_("strip_row_sb", [1, LS])
        vcol = tb_("bias_vals_col", [KT, 2])
        above, below = tb_("above", [KT, S]), tb_("below", [KT, S])
        far, rest = tb_("far", [KT, S]), tb_("far_rest", [KT, S])
        fp = [tb_(f"far_part{i}", [KT, S], BF16) for i in range(3)]
        n = moment_buffers(tb_)
        psW = tp_("w", [P, 2, 512])
        psB = tp_("band", [P, 512])
        psT = tp_("loraT", [R, KT, P])
        psD = tp_("delta", [P, KT // 2, D])
        x = a["x"].rearrange("b (t p) -> (b t) p", p=P)
        batches = range(B)
        with phase(nc, "ids_in", "ident_in", "consts_in", "w_in", "small_in", "lb_in", "bias_in", "masks_in",
                   *[f"lora{b}_in" for b in batches], *[f"rows{b}_in" for b in batches], "ids_f_ready", "ids_turned",
                   "ids_ready", "made", "zeroed", "key_out", "turned", "moved", "placed", "sig", "chain", "row_ready",
                   "row_out", "sheared", "strip_in", "col_in", "band_ready", "parts_ready", "parts_out",
                   "lora_turned", "lora_moved", "delta_ready", "added", "stats_ready", "var_ready", "root_ready") as (
                block, ids_in, ident_in, consts_in, w_in, small_in, lb_in, bias_in, masks_in, *more):
            lora_in, rows_in = more[0:B], more[B:2 * B]
            (ids_f_ready, ids_turned, ids_ready, made, zeroed, key_out, turned, moved, placed, sig, chain_sem,
             row_ready, row_out, sheared, strip_in, col_in, band_ready, parts_ready, parts_out,
             lora_turned, lora_moved, delta_ready, added, stats_ready, var_ready, root_ready) = more[2 * B:]

            @block.sync
            def _(sp):
                sp.dma_start(ids_nat[:], x).then_inc(ids_in, 16)
                sp.dma_start(t.ident[:], a["c_ident"]).then_inc(ident_in, 16)
                sp.dma_start(g[:, 0:1], a["L1_attn_et_gate"].rearrange("a b n -> (a b) n")).then_inc(bias_in, 16)
                sp.dma_start(g[:, 1:2], a["L1_attn_is_gate"].rearrange("a b n -> (a b) n")).then_inc(bias_in, 16)
                sp.dma_start(tbf[:], a["L1_attn_time_bias"].rearrange("a b n -> (a b) n")).then_inc(bias_in, 16)
                sp.dma_start(t.den_row[:], a["c_den_row"]).then_inc(consts_in, 16)
                for l in range(2):
                    for m, name in enumerate(("Wq", "Wk")):
                        src = a[w[l] + name].rearrange("(hi par) d -> hi par d", par=2)
                        sp.dma_start(nat[:, 4 * l + m, :, :], src).then_inc(w_in, 16)
                    for m, name in enumerate(("Wv", "Wo")):
                        src = a[w[l] + name].rearrange("(et e) d -> e et d", e=P)
                        sp.dma_start(nat[:, 4 * l + 2 + m, :, :], src).then_inc(w_in, 16)
                sp.dma_start(lb[:], a["L0_tok_lora_b"]).then_inc(lb_in, 16)
                sp.dma_start(above[:], a["c_above"]).then_inc(masks_in, 16)
                sp.dma_start(below[:], a["c_below"]).then_inc(masks_in, 16)
                with nc.allow_non_contiguous_dma(reason="biases of one value per partition"):
                    for m, name in enumerate(("bq", "bk")):
                        src = a["L1_attn_" + name].rearrange("(hi par) -> hi par", par=2)
                        sp.dma_start(t.bqk[:, m, :], src).then_inc(small_in, 16)
                for dst, name in ((t.bv, "bv"), (t.bo, "bo")):
                    src = a["L1_attn_" + name].rearrange("(o d) -> o d", o=1).to_broadcast([P, D])
                    sp.dma_start(dst[:], src).then_inc(small_in, 16)
                sp.wait_ge(row_ready, 1)
                sp.dma_start(row_dram, srow[:]).then_inc(row_out, 16)
                sp.wait_ge(row_out, 16)
                sp.dma_start(strip_dram, row_dram.to_broadcast([P, LS])).then_inc(sheared, 16)
                for i, at in enumerate((LS - 1, 0)):
                    sp.dma_start(vcol[:, i:i + 1], row_dram[:, at:at + 1].to_broadcast([KT, 1])).then_inc(col_in, 16)
                sp.wait_ge(sheared, 16)
                sp.dma_start(t.bias_strip[:], bass.AP(tensor=strip_dram.tensor, offset=P - 1,
                                                      ap=[[LS - 1, P], [1, STRIP]])).then_inc(strip_in, 16)
                sp.wait_ge(zeroed, 2)
                sp.wait_ge(moved, 8)
                for l in range(2):
                    for gg in range(HEADS // GH):
                        for j in range(GH):
                            d0 = (GH * gg + j) * HD
                            row, slot = (j, gg) if l == 0 else (gg, j)
                            sp.dma_start(t.woP[l][32 * row:32 * row + HD, slot, :],
                                         woT[d0 % P:d0 % P + HD, l, d0 // P, :]).then_inc(placed, 16)
                sp.wait_ge(parts_ready, 3)
                for s in range(3):
                    sp.dma_start(t.far_dram[s * KT:(s + 1) * KT, :], fp[s][:]).then_inc(parts_out, 16)
                sp.wait_ge(parts_out, 48)
                sp.wait_ge(placed, 16 * 2 * HEADS)
                sp.wait_ge(small_in, 64)

            @block.gpsimd
            def _(pool):
                for l in range(2):
                    pool.memset(t.woP[l][:], 0.0).then_inc(zeroed, 1)
                pool.dma_start(t.key_dram, a["c_key_rows"]).then_inc(key_out, 16)
                pool.wait_ge(ids_ready, 1)
                for b in batches:
                    for table, dst, sem in ((a["L0_tok_lora_a"], la, lora_in[b]), (a["L0_tok_weight"], t.h, rows_in[b])):
                        for i in range(b * KT, (b + 1) * KT):
                            off = bass.IndirectOffsetOnAxis(ap=ids[:, i:i + 1], axis=0)
                            pool.indirect_dma_start(dst[:, i, :], None, table, off).then_inc(sem, 16)
                pool.memset(t.ones_bf[:], 1.0)
                pool.memset(t.before[:], 1.0).then_inc(made, 1)
                pool.wait_ge(made, 1)
                pool.affine_select(out=t.before[:], in_=t.before[:], compare_op=ALU.is_gt, fill=0.0,
                                   base=0, pattern=[[1, P]], channel_multiplier=-1)
                for b in batches:
                    pool.wait_ge(lora_in[b], 16 * KT)
                    pool.wait_ge(rows_in[b], 16 * KT)
                pool.wait_ge(key_out, 16)

            @block.tensor
            def _(pe):
                pe.wait_ge(ident_in, 16)
                pe.wait_ge(ids_f_ready, 1)
                pe.transpose(psB[:, 0:TILES], ids_f[:], t.ident[0:TILES, 0:TILES]).then_inc(ids_turned, 1)
                pe.wait_ge(w_in, 128)
                for m in range(8):
                    if m >= 2:
                        pe.wait_ge(moved, m - 1)
                    for dt in range(DT):
                        for et in range(2):
                            at = dt * D + et * P
                            mm = pe.transpose(psW[:, m % 2, at:at + P], nat[:, m, et, dt * P:(dt + 1) * P], t.ident[:])
                    mm.then_inc(turned, 1)
                for b in batches:
                    if b == 2:
                        pe.wait_ge(strip_in, 16)
                        pe.wait_ge(ids_ready, 1)
                        for c in range(2):
                            at = S - P + 64 - c * P
                            mm = pe.transpose(psB[:, c * P:(c + 1) * P], t.bias_strip[:, at:at + P], t.ident[:])
                        mm.then_inc(band_ready, 1)
                    pe.wait_ge(lora_in[b], 16 * KT)
                    if b:
                        pe.wait_ge(lora_moved, b)
                    for i in range(KT):
                        mm = pe.transpose(psT[:, i, :], la[:, b * KT + i, :], t.ident[:])
                    mm.then_inc(lora_turned, 1)
                    pe.wait_ge(lora_moved, b + 1)
                    pe.wait_ge(lb_in, 16)
                    for half in range(2):
                        if b or half:
                            pe.wait_ge(added, 2 * b + half)
                        for i in range(KT // 2):
                            mm = pe.matmul(psD[:, i, :], laT[:, b % 2, half * (KT // 2) + i, :], lb[:],
                                           start=True, stop=True)
                        mm.then_inc(delta_ready, 1)

            @block.scalar
            def _(act):
                act.wait_ge(bias_in, 48)
                act.activation(g[:, 2:3], g[:, 0:1], ACT.Exp, scale=-1.0).then_inc(sig, 1)
                for b in batches:
                    act.wait_ge(lora_turned, b + 1)
                    act.activation(laT[:, b % 2], psT[:], ACT.Copy).then_inc(lora_moved, 1)
                act_moments(act, n, var_ready, root_ready)

            @block.vector
            def _(dve):
                chain = Chain(dve, chain_sem)
                dve.wait_ge(ids_in, 16)
                dve.tensor_copy(ids_f[:], ids_nat[:]).then_inc(ids_f_ready, 1)
                dve.wait_ge(ids_turned, 1)
                dve.tensor_copy(ids[:], psB[:, 0:TILES]).then_inc(ids_ready, 1)
                dve.wait_ge(ident_in, 16)
                dve.tensor_copy(t.ident_bf[:], t.ident[:])
                dve.tensor_copy(t.ident_r[:], t.ident[:])
                dve.wait_ge(sig, 1)
                chain(dve.tensor_scalar(g[:, 2:3], g[:, 2:3], 1.0, None, ALU.add))
                chain(dve.reciprocal(g[:, 3:4], g[:, 2:3]))
                chain(dve.tensor_scalar(tbf[:], tbf[:], g[:, 3:4], None, ALU.mult))
                first = S - 1 - REACH
                chain(dve.memset(srow[:], 0.0))
                chain(dve.tensor_scalar(srow[:, 0:first], srow[:, 0:first], tbf[:, 0:1], g[:, 1:2], ALU.add, ALU.add))
                chain(dve.tensor_scalar(srow[:, first:first + TB], tbf[:], g[:, 1:2], None, ALU.add))
                dve.tensor_scalar(srow[:, first + TB:], srow[:, first + TB:], tbf[:, TB - 1:TB], g[:, 1:2],
                                  ALU.add, ALU.add).then_inc(row_ready, 1)

                for m in range(8):
                    l = m // 4
                    dst = (t.wqT[l], t.wkT[l], t.wvT[l], None)[m % 4]
                    dst = woT[:, l] if dst is None else dst[:]
                    dve.wait_ge(turned, m + 1)
                    dve.tensor_copy(dst.rearrange("p a b -> p (a b)"), psW[:, m % 2, :]).then_inc(moved, 1)

                for b in batches:
                    if b == 2:
                        dve.wait_ge(band_ready, 1)
                        chain(dve.tensor_copy(t.band[0][:], psB[:, 0:BAND]))
                        chain(dve.tensor_tensor(t.band[1][:], psB[:, 0:BAND], t.band[0][:].bitcast(F32), ALU.subtract))
                        dve.wait_ge(col_in, 32)
                        dve.wait_ge(masks_in, 32)
                        chain(dve.tensor_scalar(far[:], above[:], vcol[:, 0:1], None, ALU.mult))
                        chain(dve.tensor_scalar(rest[:], below[:], vcol[:, 1:2], None, ALU.mult))
                        chain(dve.tensor_tensor(far[:], far[:], rest[:], ALU.add))
                        chain(dve.tensor_copy(fp[0][:], far[:]))
                        chain(dve.tensor_tensor(rest[:], far[:], fp[0][:], ALU.subtract))
                        chain(dve.tensor_copy(fp[1][:], rest[:]))
                        dve.tensor_tensor(fp[2][:], rest[:], fp[1][:], ALU.subtract).then_inc(parts_ready, 3)
                    dve.wait_ge(rows_in[b], 16 * KT)
                    for half in range(2):
                        dve.wait_ge(delta_ready, 2 * b + half + 1)
                        i = b * KT + half * (KT // 2)
                        hh = t.h[:, i:i + KT // 2, :]
                        dve.scalar_tensor_tensor(out=hh, in0=psD[:], scalar=2.0, in1=hh, op0=ALU.mult, op1=ALU.add
                                                 ).then_inc(added, 1)
                        dve.wait_ge(added, 2 * b + half + 1)
                        for j in range(i, i + KT // 2):
                            dve.bn_stats(n.stats[:, j, :], t.h[:, j, :]).then_inc(stats_ready, 1)
                dve_aggregate(dve, t, n, stats_ready)
                dve_moments(dve, chain, t, n, var_ready, root_ready)


def moment_buffers(sb):
    n = Tensors()
    n.stats = sb("stats", [P, TILES, 6])
    n.var, n.root = sb("var", [P, TILES]), sb("root", [P, TILES])
    return n


def act_moments(act, n, var_ready, root_ready):
    act.wait_ge(var_ready, 1)
    act.activation(n.root[:], n.var[:], ACT.Sqrt).then_inc(root_ready, 1)


def dve_aggregate(dve, t, n, stats_ready):
    for j in range(TILES):
        dve.wait_ge(stats_ready, j + 1)
        dve.bn_aggr(t.mv[:, j, :], n.stats[:, j, :]).then_inc(stats_ready, 1)
    dve.wait_ge(stats_ready, 2 * TILES)


def dve_moments(dve, chain, t, n, var_ready, root_ready):
    chain(dve.tensor_copy(t.mean[:], t.mv[:, :, 0]))
    dve.tensor_scalar(n.var[:], t.mv[:, :, 1], EPS, None, ALU.add).then_inc(var_ready, 1)
    dve.wait_ge(var_ready, 1)
    dve.wait_ge(root_ready, 1)
    chain(dve.reciprocal(t.inv[:], n.root[:]))
    chain(dve.tensor_tensor(t.inv[:], n.var[:], t.inv[:], ALU.mult))
    chain(dve.tensor_tensor(t.inv[:], t.inv[:], n.root[:], ALU.add))
    chain(dve.tensor_scalar(t.inv[:], t.inv[:], 0.5, None, ALU.mult))
    chain(dve.reciprocal(t.inv[:], t.inv[:]))


def norm_moments(nc, t, tag, add=False):
    with ExitStack() as own:
        sb, _ = buffers(nc, own, f"moments{tag}")
        n = moment_buffers(sb)
        rows = sb("attn_rows", [P, TILES, D]) if add else None
        with phase(nc, *[f"rows{b}_in" for b in range(B)], "added", "stats_ready", "var_ready", "root_ready",
                   "chain") as (block, *sems):
            rows_in = sems[0:B]
            added, stats_ready, var_ready, root_ready, chain_sem = sems[B:]

            if add:
                @block.sync
                def _(sp):
                    src = t.attn_dram.rearrange("(n k) p d -> n (k p) d", k=2)
                    for b in range(B):
                        sp.dma_start(rows[:, b * KT:(b + 1) * KT, :],
                                     src[b * KT:(b + 1) * KT].rearrange("n p d -> p n d")).then_inc(rows_in[b], 16)

            @block.scalar
            def _(act):
                act_moments(act, n, var_ready, root_ready)

            @block.vector
            def _(dve):
                chain = Chain(dve, chain_sem)
                for b in range(B):
                    tiles = slice(b * KT, (b + 1) * KT)
                    if add:
                        dve.wait_ge(rows_in[b], 16)
                        dve.tensor_tensor(t.h[:, tiles, :], t.h[:, tiles, :], rows[:, tiles, :], ALU.add
                                          ).then_inc(added, 1)
                        dve.wait_ge(added, b + 1)
                    for j in range(b * KT, (b + 1) * KT):
                        dve.bn_stats(n.stats[:, j, :], t.h[:, j, :]).then_inc(stats_ready, 1)
                dve_aggregate(dve, t, n, stats_ready)
                dve_moments(dve, chain, t, n, var_ready, root_ready)


def project(nc, t, a, layer):
    W = LT * P
    NP = B * S // W
    rope = layer == 0
    with ExitStack() as own:
        sb, ps = buffers(nc, own, f"proj{layer}")
        xn = sb("xn", [P, 2, LT, D])
        xT = sb("xT", [P, 2, DT, W])
        raw = sb("qk_raw", [P, 2, 2, 2, W])
        if rope:
            rot = sb("qk_rot", [P, 2, 2, W])
            m = [sb(f"rope_m{i}", [P, 2, W]) for i in range(4)]
            cos, sin = sb("cos", [P, S]), sb("sin", [P, S])
        part = [sb(f"part{i}", [P, 2, 2, W], BF16) for i in range(3)]
        rest = sb("rest", [P, 2, 2, W])
        vst = sb("v_stage", [P, LT, HEADS, 32])
        psT = ps("xT", [P, DT, W])
        psQ = ps("qk", [P, 2, 2, W])
        psV = ps("v", [P, LT, D])
        by_head = lambda ap: ap.rearrange("p (h c) -> p h c", h=HEADS)
        with phase(nc, "normed", "turned", "x_ready", "qk_ready", "v_ready", "raw_ready",
                   "v_staged", "m_ready", "pool_m_ready", "even_ready", "odd_ready", "split1", "split2",
                   "rest_ready", "split3", "v_out", "tables_in", "v_set", "scaled",
                   "part0_out", "part1_out", "part2_out") as (
                block, normed, turned, x_ready, qk_ready, v_ready, raw_ready,
                v_staged, m_ready, pool_m_ready, even_ready, odd_ready, split1, split2,
                rest_ready, split3, v_out, tables_in, v_set, scaled, *part_out):

            @block.tensor
            def _(pe):
                def turn(p):
                    if p:
                        pe.wait_ge(x_ready, p)
                    for j in range(LT):
                        pe.wait_ge(normed, p * LT + j + 1)
                        for dt in range(DT):
                            mm = pe.transpose(psT[:, dt, j * P:(j + 1) * P], xn[:, p % 2, j, dt * P:(dt + 1) * P],
                                              t.ident[:])
                    mm.then_inc(turned, 1)

                turn(0)
                for p in range(NP):
                    pe.wait_ge(x_ready, p + 1)
                    for i in range(4):
                        wT = (t.wqT, t.wkT)[i // 2][layer]
                        if p:
                            pe.wait_ge(raw_ready, 4 * (p - 1) + i + 1)
                        for dt in range(DT):
                            mm = pe.matmul(psQ[:, i // 2, i % 2, :], wT[:, dt, i % 2 * P:(i % 2 + 1) * P],
                                           xT[:, p % 2, dt, :], start=(dt == 0), stop=(dt == DT - 1))
                        mm.then_inc(qk_ready, 1)
                    if p + 1 < NP:
                        turn(p + 1)
                    if p:
                        pe.wait_ge(v_staged, LT * p)
                    for j in range(LT):
                        for dt in range(DT):
                            mm = pe.matmul(psV[:, j, :], xT[:, p % 2, dt, j * P:(j + 1) * P],
                                           t.wvT[layer][:, dt, :], start=(dt == 0), stop=(dt == DT - 1))
                    mm.then_inc(v_ready, 1)

            @block.scalar
            def _(act):
                def move_x(p):
                    act.wait_ge(turned, p + 1)
                    if p >= 2:
                        act.wait_ge(v_ready, p - 1)
                    act.activation(xT[:, p % 2], psT[:], ACT.Copy).then_inc(x_ready, 1)

                def second_part(p):
                    act.wait_ge(rest_ready, p + 1)
                    if p:
                        act.wait_ge(part_out[1], 16 * 4 * p)
                    act.activation(part[1][:], rest[:], ACT.Copy).then_inc(split2, 1)

                move_x(0)
                if rope:
                    act.wait_ge(v_set, 2)
                else:
                    act.wait_ge(scaled, 1)
                for p in range(NP):
                    for i in range(4):
                        act.wait_ge(qk_ready, 4 * p + i + 1)
                        if p >= 2 and i == 0:
                            act.wait_ge(rest_ready, p - 1)
                        bias = 0.0 if rope else t.bqk[:, i // 2, i % 2:i % 2 + 1]
                        act.activation(raw[:, p % 2, i // 2, i % 2, :], psQ[:, i // 2, i % 2, :], ACT.Identity,
                                       bias=bias, scale=(0.25 if i < 2 else 1.0)).then_inc(raw_ready, 1)
                    if p + 1 < NP:
                        move_x(p + 1)
                    if p:
                        second_part(p - 1)
                    if rope:
                        act.wait_ge(v_ready, p + 1)
                        if p:
                            act.wait_ge(v_out, 16 * p)
                        for j in range(LT):
                            act.activation(vst[:, j, :, 0:HD], by_head(psV[:, j, :]), ACT.Copy
                                           ).then_inc(v_staged, 1)
                        act.wait_ge(even_ready, p + 1)
                        act.wait_ge(odd_ready, p + 1)
                    if p:
                        act.wait_ge(part_out[0], 16 * 4 * p)
                    if not rope:
                        act.wait_ge(raw_ready, 4 * (p + 1))
                    act.activation(part[0][:], rot[:] if rope else raw[:, p % 2], ACT.Copy).then_inc(split1, 1)
                second_part(NP - 1)

            @block.vector
            def _(dve):
                def norm(p):
                    if p >= 2:
                        dve.wait_ge(turned, p - 1)
                    for j in range(LT):
                        i = p * LT + j
                        dve.tensor_scalar(xn[:, p % 2, j, :], t.h[:, i, :], t.mean[:, i:i + 1], t.inv[:, i:i + 1],
                                          ALU.subtract, ALU.mult).then_inc(normed, 1)

                def third_part(p):
                    dve.wait_ge(split2, p + 1)
                    if p:
                        dve.wait_ge(part_out[2], 16 * 4 * p)
                    dve.tensor_tensor(part[2][:], rest[:], part[1][:], ALU.subtract).then_inc(split3, 1)

                norm(0)
                if rope:
                    dve.wait_ge(tables_in, 32)
                else:
                    dve.tensor_scalar(t.bqk[:, 0, :], t.bqk[:, 0, :], 0.25, None, ALU.mult).then_inc(scaled, 1)
                    dve.wait_ge(v_set, 2)
                for p in range(NP):
                    if p + 1 < NP:
                        norm(p + 1)
                    if rope:
                        cols = slice(p % 2 * W, (p % 2 + 1) * W)
                        c = cos[:, cols].rearrange("p (o w) -> p o w", o=1).to_broadcast([P, 2, W])
                        s = sin[:, cols].rearrange("p (o w) -> p o w", o=1).to_broadcast([P, 2, W])
                        dve.wait_ge(raw_ready, 4 * (p + 1))
                        if p:
                            dve.wait_ge(even_ready, p)
                        dve.tensor_tensor(m[0][:], raw[:, p % 2, :, 0, :], c, ALU.mult).then_inc(m_ready, 1)
                        dve.tensor_tensor(m[1][:], raw[:, p % 2, :, 1, :], s, ALU.mult).then_inc(m_ready, 1)
                        dve.wait_ge(m_ready, 2 * (p + 1))
                        if p:
                            dve.wait_ge(rest_ready, p)
                        dve.tensor_tensor(rot[:, :, 0, :], m[0][:], m[1][:], ALU.subtract).then_inc(even_ready, 1)
                    if p:
                        third_part(p - 1)
                    if not rope:
                        dve.wait_ge(v_ready, p + 1)
                        if p:
                            dve.wait_ge(v_out, 16 * p)
                        for j in range(LT):
                            dve.tensor_tensor(vst[:, j, :, 0:HD], by_head(psV[:, j, :]), by_head(t.bv[:]),
                                              ALU.add).then_inc(v_staged, 1)
                    dve.wait_ge(split1, p + 1)
                    if p:
                        dve.wait_ge(split3, p)
                    if rope:
                        dve.wait_ge(odd_ready, p + 1)
                    dve.tensor_tensor(rest[:], rot[:] if rope else raw[:, p % 2], part[0][:], ALU.subtract
                                      ).then_inc(rest_ready, 1)
                third_part(NP - 1)

            @block.gpsimd
            def _(pool):
                pool.memset(vst[:, :, :, HD:32], 0.0).then_inc(v_set, 1)
                pool.wait_ge(v_set, 1)
                pool.memset(vst[:, :, :, HD:HD + 1], 1.0).then_inc(v_set, 1)
                if rope:
                    pool.wait_ge(tables_in, 32)
                for p in range(NP if rope else 0):
                    cols = slice(p % 2 * W, (p % 2 + 1) * W)
                    c = cos[:, cols].rearrange("p (o w) -> p o w", o=1).to_broadcast([P, 2, W])
                    s = sin[:, cols].rearrange("p (o w) -> p o w", o=1).to_broadcast([P, 2, W])
                    pool.wait_ge(raw_ready, 4 * (p + 1))
                    if p:
                        pool.wait_ge(odd_ready, p)
                    pool.tensor_tensor(m[2][:], raw[:, p % 2, :, 0, :], s, ALU.mult).then_inc(pool_m_ready, 1)
                    pool.tensor_tensor(m[3][:], raw[:, p % 2, :, 1, :], c, ALU.mult).then_inc(pool_m_ready, 1)
                    pool.wait_ge(pool_m_ready, 2 * (p + 1))
                    if p:
                        pool.wait_ge(rest_ready, p)
                    pool.tensor_tensor(rot[:, :, 1, :], m[2][:], m[3][:], ALU.add).then_inc(odd_ready, 1)

            @block.sync
            def _(sp):
                if rope:
                    sp.dma_start(cos[:], a["c_cos"]).then_inc(tables_in, 16)
                    sp.dma_start(sin[:], a["c_sin"]).then_inc(tables_in, 16)

                def store_part(s, p):
                    sp.wait_ge((split1, split2, split3)[s], p + 1)
                    for i in range(4):
                        par = i % 2
                        dst = t.qk_dram[p // 2, i // 2, s, :, par * FREQ:(par + 1) * FREQ,
                                        p % 2 * W:(p % 2 + 1) * W]
                        sp.dma_start(dst, part[s][:, i // 2, par, :]
                                     ).then_inc(part_out[s], 16)

                sp.wait_ge(v_set, 2)
                for p in range(NP):
                    if p:
                        store_part(1, p - 1)
                        store_part(2, p - 1)
                    sp.wait_ge(v_staged, LT * (p + 1))
                    dst = t.v_dram[p * LT:(p + 1) * LT].rearrange("j p c -> p j c")
                    sp.dma_start(dst, vst[:].rearrange("p j h c -> p j (h c)")).then_inc(v_out, 16)
                    store_part(0, p)
                store_part(1, NP - 1)
                store_part(2, NP - 1)
                sp.wait_ge(v_out, 16 * NP)
                for s in range(3):
                    sp.wait_ge(part_out[s], 16 * 4 * NP)


def attention(nc, t, a, layer):
    causal = layer == 0
    KS = PROD + ROW_MAX + (0 if causal else BIAS_ROWS)
    G = HEADS // GH
    with ExitStack() as own:
        sb, ps = buffers(nc, own, f"attn{layer}")
        if causal:
            t.strip = sb("mask_strip", [P, STRIP])
            maskT = sb("maskT", [P, P], BF16)
        else:
            t.strip = t.bias_strip
        qst = [sb(f"q_rows{g}", [P, GH, S], BF16) for g in range(G)]
        kst = [sb(f"k_rows{g}", [P, GH, S], BF16) for g in range(G)]
        v = sb("v", [P, 2, KT, GH * 32])
        prob = sb("prob", [P, 2 * GH, S])
        junk = sb("junk", [P, 4, 512], BF16)
        mx = sb("mx", [P, 2, 2, GH * KT])
        negm = sb("negm", [P, 2, 2, GH * KT], BF16)
        negmT = sb("negmT", [2 * GH * KT, 2, P], BF16)
        oT = sb("oT", [P, 2, S])
        rsum = sb("one_over_sums", [P, S])
        fold = sb("sums_folded", [P, S // 32])
        on = sb("on", [P, 2, S])
        dens = sb("den_partitions", [P, 1])
        stage = None if causal else sb("out_stage", [P, 4, D])
        psS = ps("scores", [P, 2, S])
        acc = ps("out", [P, S])
        aux = ps("aux", [P, 2, 512])
        jobs = []
        for j in range(GH):
            for qt in range(KT):
                end = (qt + 1) * P if causal else S
                for kh in range(2):
                    n = min(end - 512 * kh, 512)
                    if n > 0:
                        jobs.append((j, qt, kh, n))
        NJ = len(jobs)
        live = lambda kt: (kt * P if causal else 0)
        last_kt = lambda qh: (3 if causal and qh == 0 else KT - 1)
        halves = lambda kt: [qh for qh in range(2) if live(kt) < 512 * (qh + 1)]

        def load_qk(sp, b, g, sem):
            for m, (dst, parts) in enumerate(((qst[g], PARTS_Q), (kst[g], PARTS_K))):
                for c, s in enumerate(parts):
                    src = t.qk_dram[bass.ds(b, 1), m, s, g * GH:(g + 1) * GH]
                    sp.dma_start(dst[c * HD:(c + 1) * HD, :, :],
                                 src.rearrange("o h i w -> i (o h) w")).then_inc(sem, 16)
        QK_IN = 16 * 2 * len(PARTS_Q)

        def load_v(sp, b, g, sem):
            src = t.v_dram[bass.ds(b * KT, KT), :, g * GH * 32:(g + 1) * GH * 32]
            sp.dma_start(v[:, g % 2], src.rearrange("k p c -> p k c")).then_inc(sem, 16)

        def store_max(sp, g, sem):
            n = GH * KT
            for s in range(ROW_MAX):
                sp.dma_start(qst[g][PROD + s:PROD + s + 1, :, :].rearrange("p j (q w) -> p (j q) w", w=P),
                             negmT[s * n:(s + 1) * n, g % 2, :]).then_inc(sem, 16)
        MAX_IN = 16 * ROW_MAX

        def pe_max(pe, g, i, bank):
            j, qt, kh, w = jobs[i]
            return pe.matmul(bank[:, 0:w], qst[g][0:PROD, j, qt * P:(qt + 1) * P],
                             kst[g][0:PROD, j, kh * 512:kh * 512 + w], start=True, stop=True)

        def pe_turn(pe, g, bank):
            return pe.transpose(bank[0:2 * GH * KT, 0:P // 2].bitcast(BF16),
                                negm[:, g % 2, :, :].rearrange("p s n -> p (s n)"), t.ident_bf[:])

        def dve_max(dve, chain, g, i, bank, n, aux_free, negm_ready):
            j, qt, kh, w = jobs[i]
            at = S - P - P * qt + 512 * kh
            c = j * KT + qt
            if n >= 4:
                dve.wait_ge(aux_free, n - 3)
            dve.tensor_tensor_reduce(junk[:, n % 4, 0:w], bank[:, 0:w], t.strip[:, at:at + w], 1.0, NEG,
                                     ALU.add, ALU.max, mx[:, g % 2, kh, c:c + 1]).then_inc(aux_free, 1)
            if i == NJ - 1:
                dve.wait_ge(aux_free, n + 1)
                top = mx[:, g % 2, 0, :]
                chain(dve.tensor_tensor(top, top, mx[:, g % 2, 1, :], ALU.max))
                chain(dve.tensor_scalar(negm[:, g % 2, 0, :], top, -1.0, None, ALU.mult))
                dve.scalar_tensor_tensor(out=negm[:, g % 2, 1, :], in0=top, scalar=-1.0, in1=negm[:, g % 2, 0, :],
                                         op0=ALU.mult, op1=ALU.subtract).then_inc(negm_ready, 1)

        def dve_turn(dve, g, bank, aux_free):
            dve.tensor_copy(negmT[:, g % 2, :], bank[0:2 * GH * KT, 0:P // 2].bitcast(BF16)).then_inc(aux_free, 1)

        def fold_sums(pool, g, sem):
            pool.dma_start(fold[:], oT[HD:P:32, g % 2, :].rearrange("j (k q) -> j k q", k=32)).then_inc(sem, 16)

        def unfold_sums(pool, sem):
            pool.dma_start(rsum[HD:P:32, :].rearrange("j (k q) -> j k q", k=32), fold[:]).then_inc(sem, 16)

        def pe_sums(pe, i, bank):
            return pe.matmul(bank, t.den_row[:], rsum[:, i * 512:(i + 1) * 512], start=True, stop=True)

        def dve_sums(dve, g, i, bank, aux_free):
            cols = slice(i * 512, (i + 1) * 512)
            dve.tensor_tensor(on[:, g % 2, cols], oT[:, g % 2, cols], bank, ALU.mult).then_inc(aux_free, 1)

        def pe_out(pe, hg, i, bank):
            if causal:
                for k in range(2):
                    q = (2 * i + k) * P
                    for g in range(2):
                        mm = pe.matmul(bank[:, k * D:(k + 1) * D], on[:, g, q:q + P], t.woP[layer][:, 2 * hg + g, :],
                                       start=(g == 0), stop=(g == 1))
                return mm
            for r in range(4):
                for k in range(2):
                    j = 2 * (i % 2) + k
                    lhs = on[:, i // 2, j * 256:(j + 1) * 256].rearrange("p (u r) -> p r u", r=4)[:, r]
                    mm = pe.matmul(bank[64 * k:64 * k + 64, 0:D], lhs, t.woP[layer][:, r, :],
                                   start=(r == 0), stop=(r == 3))
            return mm

        def dve_out(dve, b, i, bank, aux_free):
            if causal:
                hh = t.h[:, bass.ds(b * KT + 2 * i, 2), :].rearrange("p k d -> p (k d)")
                dve.tensor_tensor(hh, hh, bank, ALU.add).then_inc(aux_free, 1)
            else:
                dve.tensor_tensor(stage[:, i, :], bank[:, 0:D], t.bo[:], ALU.add).then_inc(aux_free, 1)

        def store_rows(sp, b, hg, i, rows_out):
            for k in range(2):
                head = hg * UH + 2 * i + k
                sp.dma_start(t.attn_dram[bass.ds(head * B + b, 1)].rearrange("o p d -> (o p) d"),
                             stage[64 * k:64 * k + 64, i, :]).then_inc(rows_out, 16)

        early = int(NJ * (1 - LATEST[layer]))
        first_jobs = ([("max", 0, i) for i in range(NJ)] + [("turn", 0, 0)] + [("max", 1, i) for i in range(early)])
        banks = [aux[:, 0, :], aux[:, 1, :]] + [psS[:, i // 2, i % 2 * 512:(i % 2 + 1) * 512] for i in range(4)]
        with phase(nc, "qk0_in", "qk1_in", "v_in", "m_in", "fixed_in", "aux_full", "aux_free", "negm_ready",
                   "strip_ready", "made", "chain") as (
                block, qk0_in, qk1_in, v_in, m_in, fixed_in, aux_full, aux_free, negm_ready,
                strip_ready, made, chain_sem):

            @block.sync
            def _(sp):
                load_qk(sp, 0, 0, qk0_in)
                load_v(sp, 0, 0, v_in)
                load_qk(sp, 0, 1, qk1_in)
                every = lambda src, rows: src.rearrange("r (o s) -> r o s", o=1).to_broadcast([rows, GH, S])
                for g in range(G):
                    sp.dma_start(kst[g][PROD:KS, :, :], every(t.key_dram[0:KS - PROD, :], KS - PROD)
                                 ).then_inc(fixed_in, 16)
                    if not causal:
                        sp.dma_start(qst[g][PROD + ROW_MAX:KS, :, :], every(t.far_dram, BIAS_ROWS)
                                     ).then_inc(fixed_in, 16)
                sp.wait_ge(aux_free, NJ + 1)
                store_max(sp, 0, m_in)
                sp.wait_ge(m_in, MAX_IN)
                sp.wait_ge(v_in, 16)
                sp.wait_ge(qk1_in, QK_IN)
                sp.wait_ge(fixed_in, 16 * G * (1 if causal else 2))

            @block.gpsimd
            def _(pool):
                chain = Chain(pool, made)
                if causal:
                    chain(pool.memset(t.strip[:], 0.0))
                    pool.affine_select(out=t.strip[:], in_=t.strip[:], compare_op=ALU.is_ge, fill=NEG,
                                       base=S - P, pattern=[[-1, STRIP]], channel_multiplier=1).then_inc(strip_ready, 1)
                    chain(pool.memset(maskT[:], 0.0))
                    pool.affine_select(out=maskT[:], in_=maskT[:], compare_op=ALU.is_ge, fill=NEG,
                                       base=0, pattern=[[1, P]], channel_multiplier=-1)

            @block.tensor
            def _(pe):
                pe.wait_ge(qk0_in, QK_IN)
                for n, (kind, g, i) in enumerate(first_jobs):
                    bank = banks[n % len(banks)]
                    if n >= len(banks):
                        pe.wait_ge(aux_free, n - len(banks) + 1)
                    if kind == "turn":
                        pe.wait_ge(negm_ready, 1)
                        pe_turn(pe, 0, bank).then_inc(aux_full, 1)
                        continue
                    if g == 1 and i == 0:
                        pe.wait_ge(qk1_in, QK_IN)
                    pe_max(pe, g, i, bank).then_inc(aux_full, 1)

            @block.vector
            def _(dve):
                chain = Chain(dve, chain_sem)
                chain(dve.memset(mx[:], NEG))
                chain(dve.memset(on[:], 0.0))
                chain(dve.memset(rsum[:], 0.0))
                chain(dve.memset(oT[:], 1.0))
                chain(dve.tensor_reduce(dens[:], t.den_row[:].rearrange("p (j c) -> p c j", j=GH)[:, 0, :], AX, ALU.add))
                chain(dve.tensor_scalar(oT[:, 1, :], oT[:, 1, :], dens[:], None, ALU.mult))
                if causal:
                    dve.wait_ge(strip_ready, 1)
                for n, (kind, g, i) in enumerate(first_jobs):
                    dve.wait_ge(aux_full, n + 1)
                    if kind == "max":
                        dve_max(dve, chain, g, i, banks[n % len(banks)], n, aux_free, negm_ready)
                    else:
                        dve_turn(dve, 0, banks[n % len(banks)], aux_free)

        pieces = []
        for g in range(G):
            for kt in range(KT):
                for j in range(GH):
                    pieces.append(("score", g, kt, j))
                    if j % 2 == 1:
                        pg, pk = (g, kt - 1) if kt else (g - 1, KT - 1)
                        if pg >= 0 and j // 2 in halves(pk):
                            pieces.append(("pv", pg, pk, j // 2))
        pieces += [("pv", G - 1, KT - 1, qh) for qh in halves(KT - 1)]

        def cost(x):
            kind, g, kt, j = x
            if kind == "score":
                return S - live(kt) + PIECE[layer]
            return GH * (512 * (j + 1) - max(live(kt), 512 * j)) * V_WEIGHT[layer]

        after = {}
        add = lambda g, kt, j, x: after.setdefault(("score", g, kt, j), []).append(x)
        for g in range(G):
            add(g, 2, 0, ("invert", (g - 1) % G, 0))
            for i in range(2):
                add(g, 2, 3, ("sums", (g - 1) % G, i))
            if g % 2 == 0:
                for i in range(4):
                    add(g, 3, i, ("out", (g // 2 - 1) % 2, i))
        order = []
        for g in range(G):
            mine = [x for x in pieces if (x[1] if x[0] == "score" else x[1] + (x[2] == KT - 1)) == g]
            total, done = sum(cost(x) for x in mine), 0
            todo = [("max", (g + 1) % G, i) for i in range(early, NJ)] + [("turn", (g + 1) % G, 0)]
            todo += [("max", (g + 2) % G, i) for i in range(early)]
            given = 0
            for x in mine:
                order.append(x)
                order += after.get(x, [])
                done += cost(x)
                while given < min(len(todo), len(todo) * done / total):
                    order.append(todo[given])
                    given += 1
            order += todo[given:]
        order += [x for x in pieces if x[1] == G - 1 and x[0] == "pv" and x[2] == KT - 1]
        aux_jobs = [x for x in order if x[0] not in ("score", "pv", "invert")]
        aux_no = {x: i for i, x in enumerate(aux_jobs)}
        sums_done = lambda g: aux_no[("sums", g % G, 1)] + 1

        with nc.Fori(0, B) as b:
            b_next, b_prev = (b + 1) & (B - 1), (b + B - 1) & (B - 1)
            in_names = [f"qk{g}_in" for g in range(G)] + [f"v{g}_in" for g in range(G)] + [f"m{g}_in" for g in range(G)]
            with phase(nc, *in_names, "aux_full", "aux_free", "negm_ready", "scores_full", "probs_ready",
                       "pv_done", "acc_moved", "folded", "inverted", "unfolded", "rows_out", "chain") as (block, *sems):
                qk_in, v_in, m_in = sems[0:G], sems[G:2 * G], sems[2 * G:3 * G]
                (aux_full, aux_free, negm_ready, scores_full, probs_ready,
                 pv_done, acc_moved, folded, inverted, unfolded, rows_out, chain_sem) = sems[3 * G:]

                @block.sync
                def _(sp):
                    for g in range(G):
                        far, near = (g + 2) % G, (g + 1) % G
                        if g >= 2:
                            sp.wait_ge(scores_full, (g - 1) * KT * GH)
                        load_qk(sp, b if g < 2 else b_next, far, qk_in[far])
                        if g >= 1:
                            sp.wait_ge(pv_done, g * KT)
                        load_v(sp, b if g < 3 else b_next, near, v_in[near])
                        if not causal and g % 2 == 0:
                            hg = (g // 2 - 1) % 2
                            for i in range(4):
                                sp.wait_ge(aux_free, aux_no[("out", hg, i)] + 1)
                                store_rows(sp, b_prev if g == 0 else b, hg, i, rows_out)
                        sp.wait_ge(aux_free, aux_no[("turn", near, 0)] + 1)
                        store_max(sp, near, m_in[near])
                    sp.wait_ge(m_in[0], MAX_IN)
                    sp.wait_ge(v_in[0], 16)
                    for g in range(2):
                        sp.wait_ge(qk_in[g], QK_IN)
                    if not causal:
                        sp.wait_ge(rows_out, 16 * 16)

                def scores(pe, g, kt, j):
                    n = (g * KT + kt) * GH + j
                    if n >= 2:
                        pe.wait_ge(probs_ready, n - 1)
                    if g and kt == 0 and j == 0:
                        pe.wait_ge(m_in[g], MAX_IN)
                    lhs = kst[g][0:KS, j, kt * P:(kt + 1) * P]
                    for qh in halves(kt):
                        c0, c1 = max(live(kt), 512 * qh), 512 * (qh + 1)
                        extra = []
                        if causal and live(kt) // 512 == qh:
                            extra = [(live(kt), P, t.ident_bf, maskT[:])]
                        if not causal:
                            q0, q1 = max(c0, kt * P - 64), min(c1, kt * P - 64 + BAND)
                            if q0 < q1:
                                o = q0 - (kt * P - 64)
                                extra = [(q0, q1 - q0, t.ident_r, t.band[i][:, o:o + q1 - q0]) for i in range(2)]
                        mm = pe.matmul(psS[:, n % 2, c0:c1], lhs, qst[g][0:KS, j, c0:c1],
                                       start=True, stop=True)
                        for q0, w, eye, add in extra:
                            mm = pe.matmul(psS[:, n % 2, q0:q0 + w], eye[:], add, start=False,
                                           stop=True, skip_group_check=True)
                    mm.then_inc(scores_full, 1)

                def times_v(pe, g, kt, qh):
                    n = (g * KT + kt) * GH
                    pe.wait_ge(probs_ready, n + GH)
                    if g and kt == 0:
                        pe.wait_ge(acc_moved, g)
                        pe.wait_ge(v_in[g], 16)
                    c0, c1 = max(live(kt), 512 * qh), 512 * (qh + 1)
                    for j in range(GH):
                        vj = v[:, g % 2, kt, 32 * j:32 * j + 32]
                        if causal:
                            mm = pe.matmul(acc[32 * j:32 * j + 32, c0:c1], vj, prob[:, (n + j) % (2 * GH), c0:c1],
                                           start=(kt == 0), stop=(kt == last_kt(qh)))
                            continue
                        by_w = prob[:, (n + j) % (2 * GH), :].rearrange("p (u w r) -> p w u r", w=4, r=4)
                        for w in range(2 * qh, 2 * qh + 2):
                            mm = pe.matmul(acc[32 * w:32 * w + 32, j * 256:(j + 1) * 256], vj, by_w[:, w],
                                           start=(kt == 0 and j % 2 == 0), stop=(kt == KT - 1),
                                           skip_group_check=True)
                    if qh == 1:
                        mm.then_inc(pv_done, 1)

                @block.tensor
                def _(pe):
                    for x in order:
                        kind, g, i = x[0:3]
                        if kind == "score":
                            scores(pe, g, i, x[3])
                            continue
                        if kind == "pv":
                            times_v(pe, g, i, x[3])
                            continue
                        if kind == "invert":
                            continue
                        n = aux_no[x]
                        if n >= 2:
                            pe.wait_ge(aux_free, n - 1)
                        bank = aux[:, n % 2, :]
                        if kind == "max":
                            if i == 0:
                                pe.wait_ge(qk_in[g], QK_IN)
                            mm = pe_max(pe, g, i, bank)
                        elif kind == "turn":
                            pe.wait_ge(negm_ready, g if g else G)
                            mm = pe_turn(pe, g, bank)
                        elif kind == "sums":
                            pe.wait_ge(unfolded, 16 * ((g + 1) % G + 1))
                            mm = pe_sums(pe, i, bank)
                        else:
                            pe.wait_ge(aux_free, sums_done(2 * g + 1))
                            mm = pe_out(pe, g, i, bank)
                        mm.then_inc(aux_full, 1)

                @block.scalar
                def _(act):
                    def move(g):
                        act.wait_ge(pv_done, (g + 1) * KT)
                        if g:
                            act.wait_ge(aux_free, sums_done(g - 2))
                        act.activation(oT[:, g % 2, :], acc[:], ACT.Copy).then_inc(acc_moved, 1)

                    for g in range(G):
                        for kt in range(KT):
                            for j in range(GH):
                                n = (g * KT + kt) * GH + j
                                act.wait_ge(scores_full, n + 1)
                                if n >= 2 * GH:
                                    act.wait_ge(pv_done, n // GH - 1)
                                q0 = live(kt)
                                act.activation(prob[:, n % (2 * GH), q0:S], psS[:, n % 2, q0:S], ACT.Exp
                                               ).then_inc(probs_ready, 1)
                                if g and kt == 0 and j == 2:
                                    move(g - 1)
                    move(G - 1)

                @block.vector
                def _(dve):
                    chain = Chain(dve, chain_sem)
                    for kind, g, i in [x for x in order if x[0] not in ("score", "pv")]:
                        if kind == "invert":
                            k = (g + 1) % G
                            dve.wait_ge(folded, 16 * (k + 1))
                            dve.reciprocal(fold[:], fold[:]).then_inc(inverted, 1)
                            continue
                        n = aux_no[(kind, g, i)]
                        bank = aux[:, n % 2, :]
                        dve.wait_ge(aux_full, n + 1)
                        if kind == "max":
                            dve_max(dve, chain, g, i, bank, n, aux_free, negm_ready)
                        elif kind == "turn":
                            dve_turn(dve, g, bank, aux_free)
                        elif kind == "sums":
                            dve_sums(dve, g, i, bank, aux_free)
                        else:
                            if g == 0 and not causal:
                                dve.wait_ge(rows_out, 16 * 8)
                            dve_out(dve, b_prev if g else b, i, bank, aux_free)

                @block.gpsimd
                def _(pool):
                    for k in range(G):
                        g = (k - 1) % G
                        if k:
                            pool.wait_ge(acc_moved, k)
                            pool.wait_ge(unfolded, 16 * k)
                        fold_sums(pool, g, folded)
                        pool.wait_ge(inverted, k + 1)
                        if k:
                            pool.wait_ge(aux_full, sums_done(g - 1))
                        unfold_sums(pool, unfolded)
                    pool.wait_ge(unfolded, 16 * G)

        with phase(nc, "aux_full", "aux_free", "folded", "inverted", "unfolded", "rows_out") as (
                block, aux_full, aux_free, folded, inverted, unfolded, rows_out):

            @block.gpsimd
            def _(pool):
                fold_sums(pool, G - 1, folded)
                pool.wait_ge(inverted, 1)
                unfold_sums(pool, unfolded)
                pool.wait_ge(unfolded, 16)

            @block.tensor
            def _(pe):
                pe.wait_ge(unfolded, 16)
                for n in range(6):
                    bank = aux[:, n % 2, :]
                    if n >= 2:
                        pe.wait_ge(aux_free, max(n - 1, 2))
                    (pe_sums(pe, n, bank) if n < 2 else pe_out(pe, 1, n - 2, bank)).then_inc(aux_full, 1)

            @block.vector
            def _(dve):
                dve.wait_ge(folded, 16)
                dve.reciprocal(fold[:], fold[:]).then_inc(inverted, 1)
                for n in range(6):
                    dve.wait_ge(aux_full, n + 1)
                    if n < 2:
                        dve_sums(dve, G - 1, n, aux[:, n % 2, :], aux_free)
                    else:
                        dve_out(dve, B - 1, n - 2, aux[:, n % 2, :], aux_free)

            if not causal:
                @block.sync
                def _(sp):
                    for i in range(4):
                        sp.wait_ge(aux_free, i + 3)
                        store_rows(sp, B - 1, 1, i, rows_out)
                    sp.wait_ge(rows_out, 16 * 8)


def expert_buffers(nc, held, layer, m):
    sb, _ = buffers(nc, held, f"kept{layer}")
    x = Tensors()
    x.b1 = sb("b1", [m.FP, m.E * m.FT])
    if layer:
        x.w2 = sb("w2", [m.FP + 32, m.E, D])
    else:
        x.b2 = sb("b2", [P, m.E, D])
    return x


def route(nc, t, a, layer, m, x):
    W, E, K, NT = LT * P, m.E, m.top, m.NT
    HT = TILES // 2
    NP = HT // LT
    norm_moments(nc, t, f"_route{layer}", add=layer == 1)
    with ExitStack() as own:
        sb, ps = buffers(nc, own, f"route{layer}")
        xk = [sb(f"rows{k}", [P, 2, HT, XW]) for k in range(K)]
        xT = sb("xT", [P, 2, DT, W])
        wg = sb("router_w", [P, DT, E])
        bg = sb("router_b", [P, E])
        iota_e, cap_e = sb("iota_e", [P, E]), sb("cap_e", [P, E])
        carry = sb("carry", [P, E])
        lg, pos = sb("logits", [P, HT, E]), sb("pos", [P, HT, E])
        pr, tmp = sb("gate_probs", [P, HT, E]), sb("tmp", [P, HT, E])
        count, total = sb("count", [P, E, HT]), sb("running_count", [P, E, HT])
        keep = sb("keep", [P, E, HT])
        red, wsum = sb("red", [P, HT]), sb("weight_sum", [P, HT])
        top, topi = sb("top8", [P, HT, 8]), sb("top8_index", [P, HT, 8], mybir.dt.uint32)
        topf = sb("top_index", [P, HT, K])
        hot = [sb(f"one_hot{k}", [P, HT, E]) for k in range(K)]
        hot_bf = sb("one_hot_bf", [P, HT, E], BF16)
        posf, posi = sb("pos_f", [P, K, HT]), sb("pos_i", [P, 2, K, HT], I32)
        zero = sb("zero_rows", [P, XW])
        zposi = sb("zero_pos_i", [1, E], I32)
        cnt, cnti = sb("cnt", [1, E]), sb("cnt_i", [1, E], I32)
        end, one, first = sb("end", [1, E]), sb("one_row", [1, E]), sb("first_row", [1, E])
        tno, x1 = sb("tile_no", [1, NT]), sb("x1", [1, NT])
        past, sel = sb("past", [1, NT, E]), sb("owner", [1, NT, E])
        te, row = sb("tile_expert", [1, NT]), sb("tile_row", [1, NT])
        psT = ps("xT", [P, DT, W])
        psL, psR, psN = ps("logits", [P, 512]), ps("rank", [P, 512]), ps("count", [P, 512])
        tiles_of = lambda ap: ap[:, 0:HT * E].rearrange("p (j e) -> p j e", e=E)
        wide = lambda ap: ap.rearrange("p (o e) -> p o e", o=1).to_broadcast([P, HT, E])
        tall = lambda ap: ap.rearrange("p (k o) -> p k o", o=1).to_broadcast([P, HT, E])
        if layer == 1:
            wnat = sb("router_nat", [E, D])
        with phase(nc, "chain", "normed", "turned", "x_ready", "logits_ready", "shifted", "exped", "hot_ready",
                   "ranked", "pos_ready", "copied", "scattered", "zero_pos_ready", "zeroed", "kept_in", "kept_set",
                   "loaded", "made", "router_turned", "router_ready") as (
                block, chain_sem, normed, turned, x_ready, logits_ready, shifted, exped, hot_ready,
                ranked, pos_ready, copied, scattered, zero_pos_ready, zeroed, kept_in, kept_set,
                loaded, made, router_turned, router_ready):

            @block.tensor
            def _(pe):
                pe.wait_ge(loaded, 32)
                if layer == 1:
                    for dt in range(DT):
                        mm = pe.transpose(psR[:, dt * E:(dt + 1) * E], wnat[:, dt * P:(dt + 1) * P], t.ident[0:E, 0:E])
                    mm.then_inc(router_turned, 1)
                for half in range(2):
                    for s in range(half * NP, (half + 1) * NP):
                        if s:
                            pe.wait_ge(x_ready, s)
                        for j in range(LT):
                            i = s * LT + j
                            pe.wait_ge(normed, i + 1)
                            for dt in range(DT):
                                mm = pe.transpose(psT[:, dt, j * P:(j + 1) * P],
                                                  xk[0][:, half, i % HT, dt * P:(dt + 1) * P], t.ident[:])
                        mm.then_inc(turned, 1)
                        pe.wait_ge(x_ready, s + 1)
                        if layer == 1 and s == 0:
                            pe.wait_ge(router_ready, 1)
                        if half and s == NP:
                            pe.wait_ge(shifted, 1)
                        for j in range(LT):
                            i = (s * LT + j) % HT
                            for dt in range(DT):
                                mm = pe.matmul(psL[:, i * E:(i + 1) * E], xT[:, s % 2, dt, j * P:(j + 1) * P],
                                               wg[:, dt, :], start=(dt == 0), stop=(dt == DT - 1))
                        mm.then_inc(logits_ready, 1)
                    pe.wait_ge(hot_ready, half + 1)
                    flat = hot_bf[:].rearrange("p j e -> p (j e)")
                    pe.matmul(psR[:, 0:HT * E], t.before[:], flat, start=True, stop=True)
                    pe.matmul(psN[:, 0:HT * E], t.ones_bf[:], flat, start=True, stop=True).then_inc(ranked, 1)

            @block.scalar
            def _(act):
                for half in range(2):
                    for s in range(half * NP, (half + 1) * NP):
                        act.wait_ge(turned, s + 1)
                        if s >= 2:
                            act.wait_ge(logits_ready, s - 1)
                        act.activation(xT[:, s % 2], psT[:], ACT.Copy).then_inc(x_ready, 1)
                        if K == 2:
                            i = s % NP * LT
                            act.activation(xk[1][:, half, i:i + LT, 0:D], xk[0][:, half, i:i + LT, 0:D], ACT.Copy
                                           ).then_inc(copied, 1)
                    if K == 2:
                        act.wait_ge(shifted, half + 1)
                        act.activation(pr[:], lg[:], ACT.Exp).then_inc(exped, 1)

            @block.vector
            def _(dve):
                chain = Chain(dve, chain_sem)
                if layer == 1:
                    dve.wait_ge(router_turned, 1)
                    dve.tensor_copy(wg[:].rearrange("p a e -> p (a e)"), psR[:, 0:DT * E]).then_inc(router_ready, 1)
                for half in range(2):
                    for j in range(HT):
                        i = half * HT + j
                        dve.tensor_scalar(xk[0][:, half, j, 0:D], t.h[:, i, :], t.mean[:, i:i + 1], t.inv[:, i:i + 1],
                                          ALU.subtract, ALU.mult).then_inc(normed, 1)
                dve.wait_ge(made, 2)
                dve.wait_ge(loaded, 32)
                for half in range(2):
                    mine = slice(half * HT, (half + 1) * HT)
                    dve.wait_ge(logits_ready, (half + 1) * NP)
                    if K == 2:
                        chain(dve.tensor_tensor(lg[:], tiles_of(psL), wide(bg[:]), ALU.add))
                        chain(dve.tensor_reduce(red[:], lg[:], AX, ALU.max))
                        dve.tensor_tensor(lg[:], lg[:], tall(red[:]), ALU.subtract).then_inc(shifted, 1)
                        dve.wait_ge(exped, half + 1)
                        chain(dve.tensor_reduce(red[:], pr[:], AX, ALU.add))
                        chain(dve.reciprocal(red[:], red[:]))
                        chain(dve.tensor_tensor(pr[:], pr[:], tall(red[:]), ALU.mult))
                        score = pr
                    else:
                        dve.tensor_tensor(lg[:], tiles_of(psL), wide(bg[:]), ALU.add).then_inc(shifted, 1)
                        dve.wait_ge(shifted, half + 1)
                        score = lg
                    for j in range(HT):
                        dve.max(top[:, j, :], score[:, j, :]).then_inc(chain.sem, 1)
                    chain.n += HT
                    dve.wait_ge(chain.sem, chain.n)
                    for j in range(HT):
                        dve.max_index(topi[:, j, :], top[:, j, :], score[:, j, :]).then_inc(chain.sem, 1)
                    chain.n += HT
                    dve.wait_ge(chain.sem, chain.n)
                    chain(dve.tensor_copy(topf[:], topi[:, :, 0:K]))
                    for k in range(K):
                        chain(dve.tensor_tensor(hot[k][:], wide(iota_e[:]), topf[:, :, k:k + 1].to_broadcast([P, HT, E]),
                                                ALU.is_equal))
                    if K == 2:
                        dve.tensor_tensor(hot_bf[:], hot[0][:], hot[1][:], ALU.add).then_inc(hot_ready, 1)
                        chain(dve.tensor_tensor(wsum[:], top[:, :, 0], top[:, :, 1], ALU.add))
                        chain(dve.tensor_scalar(wsum[:], wsum[:], 1e-8, None, ALU.add))
                        chain(dve.reciprocal(wsum[:], wsum[:]))
                        for k in range(K):
                            chain(dve.tensor_tensor(t.weight[:, k, mine], top[:, :, k], wsum[:], ALU.mult))
                    else:
                        dve.tensor_copy(hot_bf[:], hot[0][:]).then_inc(hot_ready, 1)
                    dve.wait_ge(ranked, half + 1)
                    chain(dve.tensor_copy(count[:], tiles_of(psN).rearrange("p j e -> p e j")))
                    chain(dve.tensor_tensor_scan(total[:].rearrange("p e j -> p (e j)"),
                                                 keep[:].rearrange("p e j -> p (e j)"),
                                                 count[:].rearrange("p e j -> p (e j)"), 0.0, ALU.mult, ALU.add))
                    chain(dve.tensor_tensor(pos[:], tiles_of(psR), total[:].rearrange("p e j -> p j e"), ALU.add))
                    chain(dve.tensor_tensor(pos[:], pos[:], count[:].rearrange("p e j -> p j e"), ALU.subtract))
                    chain(dve.tensor_tensor(pos[:], pos[:], wide(carry[:]), ALU.add))
                    chain(dve.tensor_tensor(carry[:], carry[:], total[:, :, HT - 1], ALU.add))
                    for k in range(K):
                        chain(dve.tensor_tensor(tmp[:], pos[:], hot[k][:], ALU.mult))
                        chain(dve.tensor_reduce(posf[:, k, :], tmp[:], AX, ALU.add))
                    dve.tensor_copy(posi[:, half], posf[:]).then_inc(pos_ready, 1)
                    dve.wait_ge(pos_ready, half + 1)

                dve.tensor_copy(zposi[:], carry[0:1, :]).then_inc(zero_pos_ready, 1)
                chain(dve.tensor_tensor(cnt[:], carry[0:1, :], cap_e[0:1, :], ALU.subtract))
                chain(dve.tensor_scalar(cnt[:], cnt[:], float(P - 1), None, ALU.add))
                chain(dve.tensor_copy(cnti[:], cnt[:]))
                chain(dve.tensor_scalar(cnti[:], cnti[:], 7, None, ALU.arith_shift_right))
                chain(dve.tensor_copy(cnt[:], cnti[:]))
                chain(dve.memset(one[:], 1.0))
                chain(dve.tensor_tensor_scan(end[:], one[:], cnt[:], 0.0, ALU.mult, ALU.add))
                chain(dve.tensor_tensor(first[:], end[:], cnt[:], ALU.subtract))
                chain(dve.tensor_scalar(first[:], first[:], -float(P), None, ALU.mult))
                chain(dve.tensor_tensor(first[:], first[:], cap_e[0:1, :], ALU.add))
                by_tile = lambda ap: ap.rearrange("p (n o) -> p n o", o=1).to_broadcast([1, NT, E])
                by_e = lambda ap: ap.rearrange("p (o e) -> p o e", o=1).to_broadcast([1, NT, E])
                chain(dve.tensor_tensor(past[:], by_e(end[:]), by_tile(tno[:]), ALU.is_le))
                chain(dve.tensor_reduce(te[:], past[:], AX, ALU.add))
                chain(dve.tensor_scalar(te[:], te[:], float(E - 1), None, ALU.min))
                chain(dve.tensor_tensor(sel[:], by_e(iota_e[0:1, :]), by_tile(te[:]), ALU.is_equal))
                chain(dve.tensor_tensor(sel[:], sel[:], by_e(first[:]), ALU.mult))
                chain(dve.tensor_reduce(row[:], sel[:], AX, ALU.add))
                chain(dve.tensor_scalar(x1[:], tno[:], float(P), None, ALU.mult))
                chain(dve.tensor_tensor(row[:], row[:], x1[:], ALU.add))
                chain(dve.tensor_copy(t.table[:, 0, 0:NT], te[:]))
                chain(dve.tensor_scalar(x1[:], row[:], -1.0, float(m.zero_row), ALU.mult, ALU.add))
                chain(dve.tensor_tensor(x1[:], x1[:], past[:, :, E - 1], ALU.mult))
                chain(dve.tensor_tensor(x1[:], x1[:], row[:], ALU.add))
                chain(dve.tensor_copy(t.table[:, 1, 0:NT], x1[:]))
                chain(dve.memset(x1[:], 1.0))
                chain(dve.tensor_tensor(x1[:, m.slots:NT], te[:, m.slots:NT], te[:, 0:NT - m.slots], ALU.not_equal))
                chain(dve.tensor_copy(t.table[:, 2, 0:NT], x1[:]))

            @block.gpsimd
            def _(pool):
                iota = lambda ap, pattern, base, cm: pool.iota(ap, pattern=pattern, base=base, channel_multiplier=cm,
                                                               allow_small_or_imprecise_dtypes=True)
                pool.memset(zero[:, 0:D], 0.0)
                pool.memset(zero[:, D:XW], NO_TARGET)
                iota(iota_e[:], [[1, E]], 0, 0)
                iota(cap_e[:], [[m.cap, E]], 0, 0)
                iota(carry[:], [[m.cap, E]], 0, 0)
                iota(tno[:], [[1, NT]], 0, 0)
                for k in range(K):
                    iota(xk[k][:, :, :, D], [[HT * P, 2], [P, HT]], k * B * S, 1)
                pool.memset(keep[:], 1.0).then_inc(made, 1)
                pool.wait_ge(made, 1)
                pool.memset(keep[:, :, 0:1], 0.0).then_inc(made, 1)
                pool.wait_ge(made, 2)
                if layer:
                    pool.memset(x.w2[m.FP:m.FP + 32], 0.0).then_inc(kept_set, 1)
                for half in range(2):
                    pool.wait_ge(pos_ready, half + 1)
                    for k in range(K):
                        if k:
                            pool.wait_ge(copied, (half + 1) * NP)
                        for j in range(HT):
                            off = bass.IndirectOffsetOnAxis(ap=posi[:, half, k, j:j + 1], axis=0)
                            pool.indirect_dma_start(t.x_rows[layer], off, xk[k][:, half, j, :], None
                                                    ).then_inc(scattered, 16)
                pool.wait_ge(scattered, 16 * K * TILES)

            @block.sync
            def _(sp):
                if layer == 0:
                    sp.dma_start(wg[:], a["L0_ffn_Wg"].rearrange("(dt d) e -> d dt e", d=P)).then_inc(loaded, 16)
                    bias = a["L0_ffn_bg"]
                else:
                    sp.dma_start(wnat[:], a["L1_ffn_router_w"]).then_inc(loaded, 16)
                    bias = a["L1_ffn_router_b"]
                sp.dma_start(bg[:], bias.rearrange("(o e) -> o e", o=1).to_broadcast([P, E])).then_inc(loaded, 16)
                _, B1, W2, B2 = (a[n] for n in EXPERT_NAMES[layer])
                with nc.allow_non_contiguous_dma(reason="hidden biases go one to a partition"):
                    sp.dma_start(x.b1[:], B1.rearrange("e (ft f) -> f (e ft)", f=m.FP)).then_inc(kept_in, 16)
                if layer:
                    sp.dma_start(x.w2[0:m.FP], W2.rearrange("e f d -> f e d")).then_inc(kept_in, 16)
                    sp.wait_ge(kept_set, 1)
                    sp.dma_start(x.w2[m.FP:m.FP + 1], B2.rearrange("(o e) d -> o e d", o=1)).then_inc(kept_in, 16)
                else:
                    src = B2.rearrange("(o e) d -> o e d", o=1).to_broadcast([P, E, D])
                    sp.dma_start(x.b2[:], src).then_inc(kept_in, 16)
                sp.wait_ge(made, 2)
                sp.dma_start(t.x_rows[layer][m.zero_row:m.zero_row + P, :], zero[:]).then_inc(zeroed, 16)
                sp.wait_ge(zero_pos_ready, 1)
                for e in range(E):
                    at = sp.value_load(zposi[0:1, e:e + 1], min_val=0, max_val=m.rows - P)
                    sp.dma_start(t.x_rows[layer][bass.ds(at, P), :], zero[:]).then_inc(zeroed, 16)
                sp.wait_ge(zeroed, 16 * (E + 1))
                sp.wait_ge(kept_in, 48 if layer else 32)


def experts(nc, t, a, layer, m, x):
    E, FT, FP, F, NW = m.E, m.FT, m.FP, m.F, m.slots
    with ExitStack() as own:
        sb, ps = buffers(nc, own, f"experts{layer}")
        w1 = sb("w1", [P, NW, DT, F])
        w2 = None if layer else sb("w2", [FP, NW, FT, D])
        b1 = x.b1
        KR = FP + 32 if layer else FP
        NX = 4 if layer == 0 else 8
        HB = 512 // P
        HBANKS = -(-FT // HB)
        xr = sb("x_tile", [P, NX, XW])
        target = sb("target_row", [P, NX], I32)
        spare = sb("spare_row", [P, m.per])
        xT = sb("xT_tile", [P, 2, DT, P])
        hT = sb("hidden", [KR, 2, FT, P])
        y = sb("y_tile", [P, NX, D])
        psX = ps("x", [P, 2, 512])
        psH = ps("hidden", [FP, 2, 1024])
        psY = ps("y", [P, 2, 512])
        W1, _, W2, _ = (a[n] for n in EXPERT_NAMES[layer])
        with phase(nc) as (block,):

            @block.gpsimd
            def _(pool):
                pool.iota(spare[:], pattern=[[P, m.per]], base=m.top * B * S, channel_multiplier=1,
                          allow_small_or_imprecise_dtypes=True)

            if layer:
                @block.vector
                def _(dve):
                    dve.memset(hT[FP:KR], 1.0)

        with nc.Fori(0, m.passes) as it:
            names = ([f"w_in{i}" for i in range(NW)] + [f"x_in{i}" for i in range(NX)] +
                     [f"y_out{i}" for i in range(NX)] +
                     ["turned", "xT_ready", "hidden_full", "hidden_ready", "y_full", "y_ready",
                      "target_ready"])
            with phase(nc, *names) as (block, *sems):
                w_in, x_in, y_out = sems[0:NW], sems[NW:NW + NX], sems[NW + NX:NW + 2 * NX]
                (turned, xT_ready, hidden_full, hidden_ready, y_full, y_ready,
                 target_ready) = sems[NW + 2 * NX:]

                @block.sync
                def _(sp):
                    def load_x(i):
                        row = sp.value_load(t.table[0:1, 1, bass.ds(it * m.per + i, 1)], min_val=0, max_val=m.rows - P)
                        if i >= NX:
                            sp.wait_ge(turned, i - NX + 1)
                            sp.wait_ge(target_ready, i - NX + 1)
                        sp.dma_start(xr[:, i % NX, :], t.x_rows[layer][bass.ds(row, P), :]).then_inc(x_in[i % NX], 16)

                    for i in range(m.per):
                        load_x(i)

                @block.tensor
                def _(pe):
                    def turn(i):
                        pe.wait_ge(x_in[i % NX], 16 * (i // NX + 1))
                        if i >= 2:
                            pe.wait_ge(xT_ready, i - 1)
                        for dt in range(DT):
                            mm = pe.transpose(psX[:, i % 2, dt * P:(dt + 1) * P], xr[:, i % NX, dt * P:(dt + 1) * P],
                                              t.ident[:])
                        mm.then_inc(turned, 1)

                    def up(i):
                        pe.wait_ge(w_in[i % NW], (16 if layer else 32) * (i // NW + 1))
                        pe.wait_ge(xT_ready, i + 1)
                        for ft in range(FT):
                            if i >= 2 and ft % HB == 0:
                                pe.wait_ge(hidden_ready, FT * (i - 2) + min(ft + HB, FT))
                            for dt in range(DT):
                                mm = pe.matmul(psH[:, i % 2, ft * P:ft * P + P], w1[:, i % NW, dt, ft * P:ft * P + FP],
                                               xT[:, i % 2, dt, :], start=(dt == 0), stop=(dt == DT - 1))
                            if ft % HB == HB - 1 or ft == FT - 1:
                                mm.then_inc(hidden_full, 1)

                    def down(i):
                        if layer:
                            e = pe.value_load(t.table[0:1, 0, bass.ds(it * m.per + i, 1)], min_val=0, max_val=E - 1)
                        if i >= 2:
                            pe.wait_ge(y_ready, i - 1)
                        for ft in range(FT):
                            pe.wait_ge(hidden_ready, FT * i + ft + 1)
                            w = x.w2[:, bass.ds(e, 1), :].rearrange("p o d -> p (o d)") if layer else w2[:, i % NW, ft, :]
                            mm = pe.matmul(psY[:, i % 2, 0:D], hT[:, i % 2, ft, :], w,
                                           start=(ft == 0), stop=(ft == FT - 1))
                        mm.then_inc(y_full, 1)

                    ahead = layer
                    for i in range(1 + ahead):
                        turn(i)
                    for i in range(m.per + ahead):
                        if i < m.per:
                            up(i)
                        if i + 1 + ahead < m.per:
                            turn(i + 1 + ahead)
                        if i >= ahead:
                            down(i - ahead)

                @block.scalar
                def _(act):
                    def load_w(i):
                        if i >= m.per:
                            return
                        e = act.value_load(t.table[0:1, 0, bass.ds(it * m.per + i, 1)], min_val=0, max_val=E - 1)
                        need = act.value_load(t.table[0:1, 2, bass.ds(it * m.per + i, 1)], min_val=0, max_val=1)
                        if i >= NW:
                            act.wait_ge(y_full, i - NW + 1)
                        src1 = W1[bass.ds(e, 1)].rearrange("o (dt d) f -> d (o dt) f", d=P)
                        act.dma_start(w1[:, i % NW], src1, cond=need).then_inc(w_in[i % NW], 16)
                        if not layer:
                            src2 = W2[bass.ds(e, 1)].rearrange("o (ft f) d -> f (o ft) d", f=FP)
                            act.dma_start(w2[:, i % NW], src2, cond=need).then_inc(w_in[i % NW], 16)

                    for i in range(NW - 1):
                        load_w(i)
                    for i in range(m.per):
                        if not layer:
                            load_w(i + NW - 1)
                        e = act.value_load(t.table[0:1, 0, bass.ds(it * m.per + i, 1)], min_val=0, max_val=E - 1)
                        for ft in range(FT):
                            if ft % HB == 0:
                                act.wait_ge(hidden_full, HBANKS * i + ft // HB + 1)
                            if i >= 2:
                                act.wait_ge(y_full, i - 1)
                            act.activation(hT[0:FP, i % 2, ft, :], psH[:, i % 2, ft * P:(ft + 1) * P],
                                           ACT.Relu if layer else ACT.Gelu_apprx_tanh,
                                           bias=b1[:, bass.ds(e * FT + ft, 1)]).then_inc(hidden_ready, 1)
                        if layer:
                            load_w(i + NW - 1)

                @block.vector
                def _(dve):
                    def move(i):
                        dve.wait_ge(turned, i + 1)
                        if i >= 2:
                            dve.wait_ge(hidden_full, HBANKS * (i - 1))
                        dve.tensor_copy(xT[:, i % 2], psX[:, i % 2, 0:DT * P].rearrange("p (a b) -> p a b", a=DT)
                                        ).then_inc(xT_ready, 1)
                        if i >= NX:
                            dve.wait_ge(y_out[i % NX], 16 * (i // NX))
                        dve.tensor_tensor(target[:, i % NX:i % NX + 1], xr[:, i % NX, D:XW], spare[:, i:i + 1], ALU.min
                                          ).then_inc(target_ready, 1)

                    ahead = 1 + layer
                    for i in range(ahead):
                        move(i)
                    for i in range(m.per):
                        if not layer:
                            e = dve.value_load(t.table[0:1, 0, bass.ds(it * m.per + i, 1)], min_val=0, max_val=E - 1)
                        if i + ahead < m.per:
                            move(i + ahead)
                        dve.wait_ge(y_full, i + 1)
                        if i >= NX:
                            dve.wait_ge(y_out[i % NX], 16 * (i // NX))
                        if layer:
                            dve.tensor_scalar(y[:, i % NX, :], psY[:, i % 2, 0:D], 0.0, None, ALU.max
                                              ).then_inc(y_ready, 1)
                            continue
                        bias = x.b2[:, bass.ds(e, 1), :].rearrange("p o d -> p (o d)")
                        dve.tensor_tensor(y[:, i % NX, :], psY[:, i % 2, 0:D], bias, ALU.add).then_inc(y_ready, 1)
                    dve.wait_ge(target_ready, m.per)
                    dve.tensor_scalar(spare[:], spare[:], float(m.per * P), None, ALU.add)

                @block.gpsimd
                def _(pool):
                    for i in range(m.per):
                        pool.wait_ge(target_ready, i + 1)
                        pool.wait_ge(y_ready, i + 1)
                        off = bass.IndirectOffsetOnAxis(ap=target[:, i % NX:i % NX + 1], axis=0)
                        pool.indirect_dma_start(t.y_rows[layer], off, y[:, i % NX, :], None).then_inc(y_out[i % NX], 16)
                    for s in range(NX):
                        pool.wait_ge(y_out[s], 16 * (m.per // NX))


def combine(nc, t, a, layer, m, out):
    K, CT = m.top, 4
    NL = TILES // CT
    with ExitStack() as own:
        sb, _ = buffers(nc, own, f"combine{layer}")
        rows = sb("y_rows", [P, NL, K, CT, D])
        part = sb("first_choice", [P, 2, CT, D])
        n = moment_buffers(sb)
        src = t.y_rows[layer][0:K * B * S, :].rearrange("(k n p) d -> k n p d", k=K, p=P)
        with phase(nc, *[f"rows{i}_in" for i in range(NL)], "first_added", "added", "stats_ready", "var_ready",
                   "root_ready", "chain", "stored") as (block, *sems):
            rows_in = sems[0:NL]
            first_added, added, stats_ready, var_ready, root_ready, chain_sem, stored = sems[NL:]

            @block.vector
            def _(dve):
                chain = Chain(dve, chain_sem)
                for l in range(NL):
                    dve.wait_ge(rows_in[l], 16 * K)
                    if K == 1:
                        hh = t.h[:, l * CT:(l + 1) * CT, :]
                        dve.tensor_tensor(hh, rows[:, l, 0], hh, ALU.add).then_inc(added, 1)
                        continue
                    for c in range(CT):
                        j = l * CT + c
                        dve.scalar_tensor_tensor(out=part[:, l % 2, c, :], in0=rows[:, l, 0, c, :],
                                                 scalar=t.weight[:, 0, j:j + 1], in1=t.h[:, j, :],
                                                 op0=ALU.mult, op1=ALU.add).then_inc(first_added, 1)
                    for c in range(CT):
                        j = l * CT + c
                        dve.wait_ge(first_added, j + 1)
                        dve.scalar_tensor_tensor(out=t.h[:, j, :], in0=rows[:, l, 1, c, :],
                                                 scalar=t.weight[:, 1, j:j + 1], in1=part[:, l % 2, c, :],
                                                 op0=ALU.mult, op1=ALU.add).then_inc(added, 1)
                    for j in range(l * CT, (l + 1) * CT):
                        dve.wait_ge(added, j + 1)
                        dve.bn_stats(n.stats[:, j, :], t.h[:, j, :]).then_inc(stats_ready, 1)
                if not layer:
                    dve_aggregate(dve, t, n, stats_ready)
                    dve_moments(dve, chain, t, n, var_ready, root_ready)

            if not layer:
                @block.scalar
                def _(act):
                    act_moments(act, n, var_ready, root_ready)

            @block.sync
            def _(sp):
                for l in range(NL):
                    for k in range(K):
                        sp.dma_start(rows[:, l, k], src[k, l * CT:(l + 1) * CT].rearrange("n p d -> p n d")
                                     ).then_inc(rows_in[l], 16)
                if layer:
                    dst = out.rearrange("b (k p) d -> (b k) p d", p=P)
                    for l in range(NL):
                        sp.wait_ge(added, l + 1)
                        sp.dma_start(dst[l * CT:(l + 1) * CT].rearrange("k p d -> p k d"),
                                     t.h[:, l * CT:(l + 1) * CT, :]).then_inc(stored, 16)
                    sp.wait_ge(stored, 16 * NL)


def build(nc, a, out, upto=99):
    with ExitStack() as ctx:
        t = Tensors()
        dram = lambda n, s, d=F32: nc.dram_tensor(n, s, d).ap()
        t.qk_dram = dram("qk_parts", [B, 2, 3, HEADS, HD, S], BF16)
        t.v_dram = dram("v_rows", [B * KT, P, HEADS * 32])
        t.attn_dram = dram("attn_rows", [B * HEADS, S * HD // D, D])
        t.x_rows = [dram(f"x_rows{l}", [m.rows, XW]) for l, m in enumerate((MOE0, MOE1))]
        t.y_rows = [dram(f"y_rows{l}", [m.top * B * S + m.NT * P, D]) for l, m in enumerate((MOE0, MOE1))]
        sb = lambda n, s, d=F32: ctx.enter_context(nc.sbuf_tensor(n, s, d))
        t.table = sb("tile_table", [1, 3, max(MOE0.NT, MOE1.NT)], I32)
        t.weight = sb("weight", [P, 2, TILES])
        def mixture(layer, m):
            with ExitStack() as held:
                x = expert_buffers(nc, held, layer, m)
                route(nc, t, a, layer, m, x)
                experts(nc, t, a, layer, m, x)
            combine(nc, t, a, layer, m, out)

        steps = [lambda: start(nc, ctx, t, a),
                 lambda: project(nc, t, a, 0), lambda: attention(nc, t, a, 0), lambda: mixture(0, MOE0),
                 lambda: project(nc, t, a, 1), lambda: attention(nc, t, a, 1), lambda: mixture(1, MOE1)]
        for s in steps[:upto]:
            s()
        if upto < len(steps):
            with phase(nc, "stored") as (block, stored):
                @block.sync
                def _(sp):
                    sp.dma_start(out.rearrange("b (k p) d -> p (b k) d", p=P), t.h[:]).then_inc(stored, 16)
                    sp.wait_ge(stored, 16)


def constants():
    f = np.float32
    p, k, q = np.arange(P), np.arange(KT), np.arange(S)
    freq = (10000.0 ** (-np.arange(0, HD, 2) / HD)).astype(f)
    angle = q.astype(f)[None, :] * freq[p % FREQ][:, None]
    ident = np.eye(P, dtype=f)
    den_row = (p[:, None] == 32 * (p[None, :] // 32) + HD).astype(f)
    key_rows = np.concatenate([np.ones((ROW_MAX, S), f)] + [(q[None, :] // P == k[:, None]).astype(f)] * 3)
    above = (q[None, :] < P * k[:, None] - 64).astype(f)
    below = (q[None, :] >= P * k[:, None] - 64 + BAND).astype(f)
    return {"c_ident": ident, "c_den_row": den_row, "c_cos": np.cos(angle), "c_sin": np.sin(angle),
            "c_key_rows": key_rows, "c_above": above, "c_below": below}


def kernel(**inputs):
    from concourse import bacc
    from concourse.bass_utils import run_bass_kernel_spmd

    nc = bacc.Bacc("TRN2", target_bir_lowering=False, num_devices=1)
    arrays, a = {}, {}
    for name, value in [*inputs.items(), *constants().items()]:
        value = np.ascontiguousarray(value)
        arrays[name] = value
        a[name] = nc.dram_tensor(name, value.shape, mybir.dt.from_np(value.dtype), kind="ExternalInput").ap()
    out = nc.dram_tensor("out", [B, S, D], F32, kind="ExternalOutput").ap()
    build(nc, a, out)
    r = run_bass_kernel_spmd(nc, [arrays], core_ids=[0])
    return r.results[0]["out"]
```
